# Optimizing a Trainium2 kernel written in Bass

```python
import numpy as np
import jax
import jax.numpy as jnp

def _softmax(x, axis=-1):
    return jax.nn.softmax(x, axis=axis)

def _gelu(x):
    return jax.nn.gelu(x, approximate=True)

def _silu(x):
    return jax.nn.silu(x)

def _sigmoid(x):
    return jax.nn.sigmoid(x)

def _layernorm(x, axis=-1, eps=1e-05):
    m = jnp.mean(x, axis=axis, keepdims=True)
    v = jnp.var(x, axis=axis, keepdims=True)
    return (x - m) / jnp.sqrt(v + eps)

def _scatter_add(tgt, idx, src, axis=0):
    return tgt.at[idx].add(src)

def _segment_sum(src, seg, n):
    return jax.ops.segment_sum(src, seg, n)
kernel_name = 'mk_gnn_ffn_d4_gnn_r64_41c606'

def setup_inputs(seed: int=0):
    np.random.seed(seed)
    _w = jnp.asarray

    def _rec_inputs():
        import jax
        import jax.numpy as jnp
        _gk = jax.random.key(seed)
        x = -0.0002928 + 1 * jax.random.normal(jax.random.fold_in(_gk, 1), (128, 512), jnp.float32)
        src = jax.random.randint(jax.random.fold_in(_gk, 2), (2048,), 0, 128, jnp.int32)
        dst = jnp.minimum((128 * jax.random.uniform(jax.random.fold_in(_gk, 3), (2048,)) ** 2.0).astype(jnp.int32), 8191)
        _o = jnp.argsort(dst, stable=True)
        src = src[_o]
        dst = dst[_o]
        edge_weight = jax.random.uniform(jax.random.fold_in(_gk, 13), (2048,), jnp.float32, 0.0, 0.999996)
        return (x, src, dst, edge_weight)
    x, src, dst, edge_weight = _rec_inputs()

    def _L0_gnn_setup():
        import jax, jax.numpy as jnp
        import numpy as np
        N = 128
        D_IN = 512
        D_OUT = 128
        E = 4096
        key = jax.random.key(seed)
        k = jax.random.split(key, 6)
        glorot1 = np.sqrt(6.0 / (D_IN + D_OUT))
        return {'inputs': jax.random.normal(k[0], (N, D_IN), dtype=jnp.float32), 'emb_1': jax.random.uniform(k[1], (D_IN, D_OUT), minval=-glorot1, maxval=glorot1, dtype=jnp.float32), 'emb_2': jax.random.uniform(k[2], (D_IN, D_OUT), minval=-glorot1, maxval=glorot1, dtype=jnp.float32), 'alpha_p': jnp.zeros((1,), dtype=jnp.float32), 'beta_p': jnp.zeros((1,), dtype=jnp.float32), 'edge_vals': jax.random.uniform(k[3], (E,), dtype=jnp.float32), 'edge_row': jax.random.randint(k[4], (E,), 0, N, dtype=jnp.int32), 'edge_col': jax.random.randint(k[5], (E,), 0, N, dtype=jnp.int32), 'num_iters': 5}
    _L0_gnn_all = _L0_gnn_setup()
    _L0_gnn_in = {k: v for k, v in _L0_gnn_all.items() if k in ('emb_1', 'emb_2', 'alpha_p', 'beta_p')}
    del _L0_gnn_all

    def _L0_ffn_setup():
        import jax, jax.numpy as jnp
        import numpy as np
        B, S, D, H, O, E, TOPK = (4, 32, 512, 1024, 512, 8, 2)
        key = jax.random.key(seed)
        ks = jax.random.split(key, 6)
        s = lambda d: 1.0 / np.sqrt(d)
        return {'x': jax.random.normal(ks[0], (B, S, D), dtype=jnp.float32), 'Wg': jax.random.normal(ks[1], (D, E), dtype=jnp.float32) * s(D), 'W1': jax.random.normal(ks[2], (E, D, H), dtype=jnp.float32) * s(D), 'b1': jnp.zeros((E, H), dtype=jnp.float32), 'W2': jax.random.normal(ks[3], (E, H, O), dtype=jnp.float32) * s(H), 'b2': jnp.zeros((E, O), dtype=jnp.float32)}
    _L0_ffn_all = _L0_ffn_setup()
    _L0_ffn_in = {k: v for k, v in _L0_ffn_all.items() if k in ('Wg', 'W1', 'b1', 'W2', 'b2')}
    del _L0_ffn_all

    def _L1_gnn_setup():
        import jax, jax.numpy as jnp
        import numpy as np
        N, D, E = (50000, 512, 6250)
        LN_EPS = 1e-05
        key = jax.random.key(seed)
        ks = jax.random.split(key, 8)
        x = jax.random.normal(ks[0], (N, D), dtype=jnp.float32)
        edge_index = jax.random.randint(ks[1], (2, E), 0, N, dtype=jnp.int64)
        s = 1.0 / np.sqrt(D)
        W1 = jax.random.uniform(ks[2], (D, D), jnp.float32, -s, s)
        b1 = jax.random.uniform(ks[3], (D,), jnp.float32, -s, s)
        W2 = jax.random.uniform(ks[4], (D, D), jnp.float32, -s, s)
        b2 = jax.random.uniform(ks[5], (D,), jnp.float32, -s, s)
        eps = jnp.zeros((), dtype=jnp.float32)
        gamma = jnp.ones((D,), dtype=jnp.float32)
        beta = jnp.zeros((D,), dtype=jnp.float32)
        return {'x': x, 'edge_index': edge_index, 'eps': eps, 'W1': W1, 'b1': b1, 'W2': W2, 'b2': b2, 'gamma': gamma, 'beta': beta}
    _L1_gnn_all = _L1_gnn_setup()
    _L1_gnn_in = {k: v for k, v in _L1_gnn_all.items() if k in ('eps', 'W1', 'b1', 'W2', 'b2', 'gamma', 'beta')}
    del _L1_gnn_all

    def _L1_ffn_setup():
        import jax, jax.numpy as jnp
        import numpy as np
        B, S, D = (8, 64, 512)
        H = 32
        O = 512
        E = 8
        TOP_K = 1
        key = jax.random.key(seed)
        ks = jax.random.split(key, 8)
        sc = 0.02
        return {'x': jax.random.normal(ks[0], (B, S, D), dtype=jnp.float32), 'Wr': jax.random.normal(ks[1], (D, E), dtype=jnp.float32) * sc, 'br': jnp.zeros((E,), dtype=jnp.float32), 'W1': jax.random.normal(ks[2], (E, D, H), dtype=jnp.float32) * sc, 'b1': jnp.zeros((E, H), dtype=jnp.float32), 'W2': jax.random.normal(ks[3], (E, H, O), dtype=jnp.float32) * sc, 'b2': jnp.zeros((E, O), dtype=jnp.float32)}
    _L1_ffn_all = _L1_ffn_setup()
    _L1_ffn_in = {k: v for k, v in _L1_ffn_all.items() if k in ('Wr', 'br', 'W1', 'b1', 'W2', 'b2')}
    del _L1_ffn_all

    def _L2_gnn_setup():
        import jax, jax.numpy as jnp
        import numpy as np
        N_NODES = 512
        N_EDGES = 4096
        D = 512
        NUM_EXPERTS = 4
        TOP_K = 2
        LAYERS = 2
        key = jax.random.key(seed)
        ks = jax.random.split(key, 8)
        x = jax.random.normal(ks[0], (N_NODES, D), dtype=jnp.float32)
        edge_index = jax.random.randint(ks[1], (2, N_EDGES), 0, N_NODES, dtype=jnp.int64)
        s = 1.0 / np.sqrt(D)
        gate_W = jax.random.uniform(ks[2], (D, NUM_EXPERTS), jnp.float32, -s, s)
        gate_b = jax.random.uniform(ks[3], (NUM_EXPERTS,), jnp.float32, -s, s)
        Wl = jax.random.uniform(ks[4], (NUM_EXPERTS, LAYERS, D, D), jnp.float32, -s, s)
        bl = jax.random.uniform(ks[5], (NUM_EXPERTS, LAYERS, D), jnp.float32, -s, s)
        Wr = jax.random.uniform(ks[6], (NUM_EXPERTS, LAYERS, D, D), jnp.float32, -s, s)
        return {'x': x, 'gate_W': gate_W, 'gate_b': gate_b, 'Wl': Wl, 'bl': bl, 'Wr': Wr, 'edge_index': edge_index}
    _L2_gnn_all = _L2_gnn_setup()
    _L2_gnn_in = {k: v for k, v in _L2_gnn_all.items() if k in ('gate_W', 'gate_b', 'Wl', 'bl', 'Wr')}
    del _L2_gnn_all

    def _L2_ffn_setup():
        import jax, jax.numpy as jnp
        import numpy as np
        DIM, DEPTH, MULT = (512, 3, 4)
        E = 2 ** DEPTH
        HID = MULT * DIM
        B, S = (4, 1024)

        def _leaf_probs(flat_x, rw, rb):
            n_tok = flat_x.shape[0]
            leaf = jnp.ones((n_tok, 1), dtype=flat_x.dtype)
            for d in range(DEPTH):
                off, n = (2 ** d - 1, 2 ** d)
                logits = flat_x @ rw[off:off + n].T + rb[off:off + n]
                p = jax.nn.sigmoid(logits)
                leaf = (leaf[:, :, None] * jnp.stack([1.0 - p, p], axis=2)).reshape(n_tok, 2 * n)
            return leaf
        key = jax.random.key(seed)
        ks = jax.random.split(key, 7)
        sd = 1.0 / np.sqrt(DIM)
        sh = 1.0 / np.sqrt(HID)
        return {'x': jax.random.normal(ks[0], (B, S, DIM), dtype=jnp.float32), 'rw': jax.random.normal(ks[1], (E - 1, DIM), dtype=jnp.float32) * sd, 'rb': jax.random.normal(ks[2], (E - 1,), dtype=jnp.float32) * sd, 'w1': jax.random.normal(ks[3], (E, DIM, HID), dtype=jnp.float32) * sd, 'b1': jax.random.normal(ks[4], (E, HID), dtype=jnp.float32) * sd, 'w2': jax.random.normal(ks[5], (E, HID, DIM), dtype=jnp.float32) * sh, 'b2': jax.random.normal(ks[6], (E, DIM), dtype=jnp.float32) * sh}
    _L2_ffn_all = _L2_ffn_setup()
    _L2_ffn_in = {k: v for k, v in _L2_ffn_all.items() if k in ('rw', 'rb', 'w1', 'b1', 'w2', 'b2')}
    del _L2_ffn_all

    def _L3_gnn_setup():
        import jax, jax.numpy as jnp
        import numpy as np
        N, E, DM, H, DFF = (20000, 10000, 512, 8, 32)
        DK = DM // H

        def _layernorm(x, g, b, eps=1e-05):
            mu = jnp.mean(x, axis=-1, keepdims=True)
            var = jnp.mean(jnp.square(x - mu), axis=-1, keepdims=True)
            return (x - mu) * jax.lax.rsqrt(var + eps) * g + b
        key = jax.random.key(seed)
        ks = jax.random.split(key, 12)
        s = 0.02
        h = jax.random.normal(ks[0], (N, DM), dtype=jnp.float32)
        src = jax.random.randint(ks[1], (E,), 0, N, dtype=jnp.int32)
        dst = jnp.sort(jax.random.randint(ks[2], (E,), 0, N, dtype=jnp.int32))
        return {'h': h, 'src': src, 'dst': dst, 'Wq': jax.random.normal(ks[3], (DM, DM), dtype=jnp.float32) * s, 'Wk': jax.random.normal(ks[4], (DM, DM), dtype=jnp.float32) * s, 'Wv': jax.random.normal(ks[5], (DM, DM), dtype=jnp.float32) * s, 'Wo': jax.random.normal(ks[6], (DM, DM), dtype=jnp.float32) * s, 'ln1_g': jnp.ones((DM,), jnp.float32), 'ln1_b': jnp.zeros((DM,), jnp.float32), 'ln2_g': jnp.ones((DM,), jnp.float32), 'ln2_b': jnp.zeros((DM,), jnp.float32), 'W1': jax.random.normal(ks[7], (DM, DFF), dtype=jnp.float32) * s, 'b1': jnp.zeros((DFF,), jnp.float32), 'W2': jax.random.normal(ks[8], (DFF, DM), dtype=jnp.float32) * s, 'b2': jnp.zeros((DM,), jnp.float32)}
    _L3_gnn_all = _L3_gnn_setup()
    _L3_gnn_in = {k: v for k, v in _L3_gnn_all.items() if k in ('Wq', 'Wk', 'Wv', 'Wo', 'ln1_g', 'ln1_b', 'ln2_g', 'ln2_b', 'W1', 'b1', 'W2', 'b2')}
    del _L3_gnn_all

    def _L3_ffn_setup():
        import jax, jax.numpy as jnp
        import numpy as np
        B, S, D = (2, 32, 512)
        E, H, TOP_K = (8, 1024, 2)
        SCALE = 1.0
        key = jax.random.key(seed)
        ks = jax.random.split(key, 7)
        s = lambda fan_in: 1.0 / np.sqrt(fan_in)
        return {'x': jax.random.normal(ks[0], (B, S, D), dtype=jnp.float32), 'gate_w': jax.random.normal(ks[1], (E, D), dtype=jnp.float32) * s(D), 'w1': jax.random.normal(ks[2], (E, H, D), dtype=jnp.float32) * s(D), 'w2': jax.random.normal(ks[3], (E, D, H), dtype=jnp.float32) * s(H), 'sg_gate': jax.random.normal(ks[4], (H, D), dtype=jnp.float32) * s(D), 'sg_up': jax.random.normal(ks[5], (H, D), dtype=jnp.float32) * s(D), 'sg_down': jax.random.normal(ks[6], (D, H), dtype=jnp.float32) * s(H)}
    _L3_ffn_all = _L3_ffn_setup()
    _L3_ffn_in = {k: v for k, v in _L3_ffn_all.items() if k in ('gate_w', 'w1', 'w2', 'sg_gate', 'sg_up', 'sg_down')}
    del _L3_ffn_all
    return {'x': x, 'src': src, 'dst': dst, 'edge_weight': edge_weight, 'L0_gnn_emb_1': _L0_gnn_in['emb_1'], 'L0_gnn_emb_2': _L0_gnn_in['emb_2'], 'L0_gnn_alpha_p': _L0_gnn_in['alpha_p'], 'L0_gnn_beta_p': _L0_gnn_in['beta_p'], 'L0_ffn_Wg': _L0_ffn_in['Wg'], 'L0_ffn_W1': _L0_ffn_in['W1'], 'L0_ffn_b1': _L0_ffn_in['b1'], 'L0_ffn_W2': _L0_ffn_in['W2'], 'L0_ffn_b2': _L0_ffn_in['b2'], 'L1_gnn_eps': _L1_gnn_in['eps'], 'L1_gnn_W1': _L1_gnn_in['W1'], 'L1_gnn_b1': _L1_gnn_in['b1'], 'L1_gnn_W2': _L1_gnn_in['W2'], 'L1_gnn_b2': _L1_gnn_in['b2'], 'L1_gnn_gamma': _L1_gnn_in['gamma'], 'L1_gnn_beta': _L1_gnn_in['beta'], 'L1_ffn_Wr': _L1_ffn_in['Wr'], 'L1_ffn_br': _L1_ffn_in['br'], 'L1_ffn_W1': _L1_ffn_in['W1'], 'L1_ffn_b1': _L1_ffn_in['b1'], 'L1_ffn_W2': _L1_ffn_in['W2'], 'L1_ffn_b2': _L1_ffn_in['b2'], 'L2_gnn_gate_W': _L2_gnn_in['gate_W'], 'L2_gnn_gate_b': _L2_gnn_in['gate_b'], 'L2_gnn_Wl': _L2_gnn_in['Wl'], 'L2_gnn_bl': _L2_gnn_in['bl'], 'L2_gnn_Wr': _L2_gnn_in['Wr'], 'L2_ffn_rw': _L2_ffn_in['rw'], 'L2_ffn_rb': _L2_ffn_in['rb'], 'L2_ffn_w1': _L2_ffn_in['w1'], 'L2_ffn_b1': _L2_ffn_in['b1'], 'L2_ffn_w2': _L2_ffn_in['w2'], 'L2_ffn_b2': _L2_ffn_in['b2'], 'L3_gnn_Wq': _L3_gnn_in['Wq'], 'L3_gnn_Wk': _L3_gnn_in['Wk'], 'L3_gnn_Wv': _L3_gnn_in['Wv'], 'L3_gnn_Wo': _L3_gnn_in['Wo'], 'L3_gnn_ln1_g': _L3_gnn_in['ln1_g'], 'L3_gnn_ln1_b': _L3_gnn_in['ln1_b'], 'L3_gnn_ln2_g': _L3_gnn_in['ln2_g'], 'L3_gnn_ln2_b': _L3_gnn_in['ln2_b'], 'L3_gnn_W1': _L3_gnn_in['W1'], 'L3_gnn_b1': _L3_gnn_in['b1'], 'L3_gnn_W2': _L3_gnn_in['W2'], 'L3_gnn_b2': _L3_gnn_in['b2'], 'L3_ffn_gate_w': _L3_ffn_in['gate_w'], 'L3_ffn_w1': _L3_ffn_in['w1'], 'L3_ffn_w2': _L3_ffn_in['w2'], 'L3_ffn_sg_gate': _L3_ffn_in['sg_gate'], 'L3_ffn_sg_up': _L3_ffn_in['sg_up'], 'L3_ffn_sg_down': _L3_ffn_in['sg_down']}

def reference(x, src, dst, edge_weight, L0_gnn_emb_1, L0_gnn_emb_2, L0_gnn_alpha_p, L0_gnn_beta_p, L0_ffn_Wg, L0_ffn_W1, L0_ffn_b1, L0_ffn_W2, L0_ffn_b2, L1_gnn_eps, L1_gnn_W1, L1_gnn_b1, L1_gnn_W2, L1_gnn_b2, L1_gnn_gamma, L1_gnn_beta, L1_ffn_Wr, L1_ffn_br, L1_ffn_W1, L1_ffn_b1, L1_ffn_W2, L1_ffn_b2, L2_gnn_gate_W, L2_gnn_gate_b, L2_gnn_Wl, L2_gnn_bl, L2_gnn_Wr, L2_ffn_rw, L2_ffn_rb, L2_ffn_w1, L2_ffn_b1, L2_ffn_w2, L2_ffn_b2, L3_gnn_Wq, L3_gnn_Wk, L3_gnn_Wv, L3_gnn_Wo, L3_gnn_ln1_g, L3_gnn_ln1_b, L3_gnn_ln2_g, L3_gnn_ln2_b, L3_gnn_W1, L3_gnn_b1, L3_gnn_W2, L3_gnn_b2, L3_ffn_gate_w, L3_ffn_w1, L3_ffn_w2, L3_ffn_sg_gate, L3_ffn_sg_up, L3_ffn_sg_down):
    import jax
    import jax.numpy as jnp

    def _L0_gnn_ref(inputs, emb_1, emb_2, alpha_p, beta_p, edge_vals, edge_row, edge_col, num_iters):
        import jax, jax.numpy as jnp
        import numpy as np
        N = 128
        D_IN = 512
        D_OUT = 128
        E = 4096
        n = inputs.shape[0]
        x1 = inputs @ emb_1
        x2 = inputs @ emb_2
        logits = x1 @ x2.T
        sim = jax.nn.softmax(jax.nn.leaky_relu(logits, 0.2), axis=-1)
        vals = edge_vals * sim[edge_row, edge_col]
        normalize = jax.ops.segment_sum(vals, edge_row, num_segments=n)[:, None]
        alpha = jnp.exp(alpha_p)
        beta = jnp.exp(beta_p)
        denom = beta + normalize * alpha + alpha

        def body(out, _):
            sp = jax.ops.segment_sum(vals[:, None] * out[edge_col], edge_row, num_segments=n)
            out = (inputs * beta + (sp + out) * alpha) / denom
            return (out, None)
        out, _ = jax.lax.scan(body, inputs, None, length=num_iters)
        return out

    def _L0_ffn_ref(x, Wg, W1, b1, W2, b2):
        import jax, jax.numpy as jnp
        import numpy as np
        B, S, D, H, O, E, TOPK = (4, 32, 512, 1024, 512, 8, 2)
        Bsz, Seq, Din = x.shape
        T = Bsz * Seq
        xm = x.reshape(T, Din)
        probs = jax.nn.softmax(xm @ Wg, axis=-1)
        top_p, top_i = jax.lax.top_k(probs, TOPK)
        gates = jnp.zeros((T, E), dtype=probs.dtype).at[jnp.arange(T)[:, None], top_i].set(top_p)
        h = jax.nn.gelu(jnp.einsum('td,edh->teh', xm, W1) + b1[None])
        y = jnp.einsum('teh,eho->teo', h, W2) + b2[None]
        out = jnp.einsum('te,teo->to', gates, y)
        return out.reshape(Bsz, Seq, O)

    def _L1_gnn_ref(x, edge_index, eps, W1, b1, W2, b2, gamma, beta):
        import jax, jax.numpy as jnp
        import numpy as np
        N, D, E = (50000, 512, 6250)
        LN_EPS = 1e-05
        i, j = (edge_index[0], edge_index[1])
        agg = jax.ops.segment_sum(x[j], i, num_segments=x.shape[0])
        h = (1.0 + eps) * x + agg
        h = jax.nn.relu(h @ W1.T + b1)
        h = h @ W2.T + b2
        mu = jnp.mean(h, axis=-1, keepdims=True)
        var = jnp.var(h, axis=-1, keepdims=True)
        out = (h - mu) * jax.lax.rsqrt(var + LN_EPS) * gamma + beta
        return out

    def _L1_ffn_ref(x, Wr, br, W1, b1, W2, b2):
        import jax, jax.numpy as jnp
        import numpy as np
        B, S, D = (8, 64, 512)
        H = 32
        O = 512
        E = 8
        TOP_K = 1
        b, s, d = x.shape
        xf = x.reshape(-1, d)
        router_logits = xf @ Wr + br
        topk_logits, topk_idx = jax.lax.top_k(router_logits, TOP_K)
        topk_gates = jax.nn.softmax(topk_logits, axis=1)
        out = jnp.zeros((xf.shape[0], O), dtype=x.dtype)
        for k in range(TOP_K):
            idx_k = topk_idx[:, k]
            gate_k = topk_gates[:, k:k + 1]
            for e in range(E):
                h = jax.nn.relu(xf @ W1[e] + b1[e])
                oe = h @ W2[e] + b2[e]
                mask = (idx_k == e)[:, None]
                out = out + jnp.where(mask, gate_k * oe, 0.0)
        return out.reshape(b, s, O)

    def _L2_gnn_ref(x, gate_W, gate_b, Wl, bl, Wr, edge_index):
        import jax, jax.numpy as jnp
        import numpy as np
        N_NODES = 512
        N_EDGES = 4096
        D = 512
        NUM_EXPERTS = 4
        TOP_K = 2
        LAYERS = 2
        n = x.shape[0]
        src, dst = (edge_index[0], edge_index[1])
        gates = jax.nn.softmax(x @ gate_W + gate_b, axis=-1)
        top_v, top_i = jax.lax.top_k(gates, TOP_K)
        deg = jax.ops.segment_sum(jnp.ones((src.shape[0],), x.dtype), dst, num_segments=n)
        inv_deg = jnp.where(deg > 0, 1.0 / jnp.maximum(deg, 1.0), 0.0)[:, None]

        def sage_conv(h, W_l, b_l, W_r):
            aggr = jax.ops.segment_sum(h[src], dst, num_segments=n) * inv_deg
            return aggr @ W_l + b_l + h @ W_r
        expert_outs = []
        for e in range(NUM_EXPERTS):
            h = x
            for l in range(LAYERS):
                h = sage_conv(h, Wl[e, l], bl[e, l], Wr[e, l])
                h = jax.nn.relu(h)
            expert_outs.append(h)
        expert_outputs = jnp.stack(expert_outs, axis=1)
        sel = jnp.take_along_axis(expert_outputs, top_i[:, :, None], axis=1)
        out = jnp.sum(sel * top_v[:, :, None], axis=1)
        return out

    def _L2_ffn_ref(x, rw, rb, w1, b1, w2, b2):
        import jax, jax.numpy as jnp
        import numpy as np
        DIM, DEPTH, MULT = (512, 3, 4)
        E = 2 ** DEPTH
        HID = MULT * DIM
        B, S = (4, 1024)

        def _leaf_probs(flat_x, rw, rb):
            n_tok = flat_x.shape[0]
            leaf = jnp.ones((n_tok, 1), dtype=flat_x.dtype)
            for d in range(DEPTH):
                off, n = (2 ** d - 1, 2 ** d)
                logits = flat_x @ rw[off:off + n].T + rb[off:off + n]
                p = jax.nn.sigmoid(logits)
                leaf = (leaf[:, :, None] * jnp.stack([1.0 - p, p], axis=2)).reshape(n_tok, 2 * n)
            return leaf
        b, s, dim = x.shape
        flat_x = x.reshape(b * s, dim)
        leaf_probs = _leaf_probs(flat_x, rw, rb)
        h = jnp.einsum('nd,edh->neh', flat_x, w1) + b1[None]
        h = jax.nn.gelu(h, approximate=False)
        y = jnp.einsum('neh,ehd->ned', h, w2) + b2[None]
        out = jnp.einsum('ned,ne->nd', y, leaf_probs)
        return out.reshape(b, s, dim)

    def _L3_gnn_ref(h, src, dst, Wq, Wk, Wv, Wo, ln1_g, ln1_b, ln2_g, ln2_b, W1, b1, W2, b2):
        import jax, jax.numpy as jnp
        import numpy as np
        N, E, DM, H, DFF = (20000, 10000, 512, 8, 32)
        DK = DM // H

        def _layernorm(x, g, b, eps=1e-05):
            mu = jnp.mean(x, axis=-1, keepdims=True)
            var = jnp.mean(jnp.square(x - mu), axis=-1, keepdims=True)
            return (x - mu) * jax.lax.rsqrt(var + eps) * g + b
        n = h.shape[0]
        q = (h @ Wq).reshape(n, H, DK)
        k = (h @ Wk).reshape(n, H, DK)
        v = (h @ Wv).reshape(n, H, DK)
        e = jnp.einsum('ehd,ehd->eh', k[src], q[dst]) / np.sqrt(DK).astype(np.float32)
        m = jax.ops.segment_max(e, dst, num_segments=n)
        ex = jnp.exp(e - m[dst])
        z = jax.ops.segment_sum(ex, dst, num_segments=n)
        attn = ex / z[dst]
        a = jax.ops.segment_sum(attn[:, :, None] * v[src], dst, num_segments=n)
        a = a.reshape(n, DM)
        o = a @ Wo
        x = _layernorm(h + o, ln1_g, ln1_b)
        f = jax.nn.relu(x @ W1 + b1) @ W2 + b2
        return _layernorm(x + f, ln2_g, ln2_b)

    def _L3_ffn_ref(x, gate_w, w1, w2, sg_gate, sg_up, sg_down):
        import jax, jax.numpy as jnp
        import numpy as np
        B, S, D = (2, 32, 512)
        E, H, TOP_K = (8, 1024, 2)
        SCALE = 1.0
        b, s_len, d = x.shape
        xf = x.reshape(-1, d)
        n = xf.shape[0]
        logits = xf @ gate_w.T * SCALE
        topk_w, idx = jax.lax.top_k(logits, TOP_K)
        topk_w = jax.nn.softmax(topk_w, axis=-1)
        comb = jnp.zeros((n, E), dtype=xf.dtype).at[jnp.arange(n)[:, None], idx].add(topk_w)
        h = jax.nn.silu(jnp.einsum('td,ehd->teh', xf, w1))
        eo = jnp.einsum('teh,edh->ted', h, w2)
        routed = jnp.einsum('te,ted->td', comb, eo)
        shared = jax.nn.silu(xf @ sg_gate.T) * (xf @ sg_up.T) @ sg_down.T
        return (routed + shared).reshape(b, s_len, d)
    edge_index = jnp.stack([src, dst])
    x = x + _L0_gnn_ref(_layernorm(x, axis=-1), L0_gnn_emb_1, L0_gnn_emb_2, L0_gnn_alpha_p, L0_gnn_beta_p, edge_weight, src, dst, 5)
    x = x + _L0_ffn_ref(_layernorm(x, axis=-1)[None], L0_ffn_Wg, L0_ffn_W1, L0_ffn_b1, L0_ffn_W2, L0_ffn_b2)[0]
    x = x + _L1_gnn_ref(_layernorm(x, axis=-1), edge_index, L1_gnn_eps, L1_gnn_W1, L1_gnn_b1, L1_gnn_W2, L1_gnn_b2, L1_gnn_gamma, L1_gnn_beta)
    x = x + _L1_ffn_ref(_layernorm(x, axis=-1)[None], L1_ffn_Wr, L1_ffn_br, L1_ffn_W1, L1_ffn_b1, L1_ffn_W2, L1_ffn_b2)[0]
    x = x + _L2_gnn_ref(_layernorm(x, axis=-1), L2_gnn_gate_W, L2_gnn_gate_b, L2_gnn_Wl, L2_gnn_bl, L2_gnn_Wr, edge_index)
    x = x + _L2_ffn_ref(_layernorm(x, axis=-1)[None], L2_ffn_rw, L2_ffn_rb, L2_ffn_w1, L2_ffn_b1, L2_ffn_w2, L2_ffn_b2)[0]
    x = x + _L3_gnn_ref(_layernorm(x, axis=-1), src, dst, L3_gnn_Wq, L3_gnn_Wk, L3_gnn_Wv, L3_gnn_Wo, L3_gnn_ln1_g, L3_gnn_ln1_b, L3_gnn_ln2_g, L3_gnn_ln2_b, L3_gnn_W1, L3_gnn_b1, L3_gnn_W2, L3_gnn_b2)
    x = x + _L3_ffn_ref(_layernorm(x, axis=-1)[None], L3_ffn_gate_w, L3_ffn_w1, L3_ffn_w2, L3_ffn_sg_gate, L3_ffn_sg_up, L3_ffn_sg_down)[0]
    return x

_drawn_inputs = setup_inputs


def setup_inputs(seed=0):
    import zlib

    import numpy as np

    out = dict(_drawn_inputs(seed))
    spreads = {'L0_ffn_b1': (0.0, 0.37),
     'L0_ffn_b2': (0.0, 0.1),
     'L1_gnn_gamma': (1.0, 0.2),
     'L1_gnn_beta': (0.0, 0.1),
     'L1_ffn_br': (0.0, 0.325),
     'L1_ffn_b1': (0.0, 0.671),
     'L1_ffn_b2': (0.0, 0.1),
     'L3_gnn_ln1_g': (1.0, 0.2),
     'L3_gnn_ln1_b': (0.0, 0.1),
     'L3_gnn_ln2_g': (1.0, 0.2),
     'L3_gnn_ln2_b': (0.0, 0.1),
     'L3_gnn_b1': (0.0, 0.727),
     'L3_gnn_b2': (0.0, 0.281)}
    factors = {'L1_gnn_b1': 8.0,
     'L1_gnn_b2': 4.033,
     'L1_ffn_W1': 3.459,
     'L1_ffn_W2': 3.165,
     'L2_gnn_gate_b': 8.0,
     'L2_gnn_bl': 7.524,
     'L2_ffn_rb': 5.846,
     'L2_ffn_b1': 7.047,
     'L2_ffn_b2': 8.0,
     'L3_gnn_Wq': 6.359,
     'L3_gnn_Wk': 8.0,
     'L3_gnn_W1': 6.19,
     'L3_gnn_W2': 4.894}
    for name, (base, spread) in spreads.items():
        noise = np.random.default_rng([zlib.crc32(name.encode()), seed]).standard_normal(out[name].shape)
        drawn = base * np.exp(spread * noise) if base else spread * noise
        out[name] = jnp.asarray(drawn.astype(out[name].dtype))
    for name, factor in factors.items():
        out[name] = (out[name] * factor).astype(out[name].dtype)
    return out
```

```python
from contextlib import ExitStack

import concourse.bass as bass
from concourse import mybir

P = 128
D = 512
KC = D // P
NE = 2048
EC = NE // P
RAW_SLOTS = 8
SPLIT_SLOTS = 4
AHEAD = 2
E8 = 8
E4 = 4
HEADS = 8
DK = D // HEADS
H1 = 32
LN_EPS = 1e-5
MASKED = -1e30

F32 = mybir.dt.float32
F32R = mybir.dt.float32r
I32 = mybir.dt.int32
ALU = mybir.AluOpType
ACT = mybir.ActivationFunctionType
AX_X = mybir.AxisListType.X

G_L0F = 0
G_L1G = G_L0F + 32
G_L2G = G_L1G + 2
G_L2F = G_L2G + 16
G_L3G = G_L2F + 64
G_L3F = G_L3G + 4
CHUNKS = G_L3F + 38


class Pipe:

    def __init__(self, tag, g0, n, per_expert, turned, summed, act, lead=0, selected=None):
        self.tag, self.g0, self.n, self.U = tag, g0, n, per_expert
        self.turned = turned
        self.summed = summed
        self.act, self.lead = act, lead
        self.selected = selected

    def chunk(self, s):
        if self.lead:
            return self.g0 + 2 * s if s <= self.n else self.g0 + 2 * self.n + (s - self.n)
        if s < 2:
            return self.g0 + s
        return self.g0 + 2 * (s - 1) if s <= self.n else self.g0 + 2 * self.n - 1

    def loops(self):
        return (self.n - 4) // 4


L0F = Pipe("l0f", G_L0F, 16, 2, 0, 1, ACT.Gelu_apprx_tanh, selected=0)
L2F = Pipe("l2f", G_L2F, 32, 4, 16, 1 + 8 + 1, ACT.Gelu, selected=8)
L3F = Pipe("l3f", G_L3F, 18, 2, 16 + 32, 1 + 8 + 1 + 16, ACT.Silu, lead=2)
BL_COL = 2048


def transposed(g):
    return G_L1G <= g < G_L2G or g >= G_L3F


def turned_quarters(g):
    return 4 * (g - G_L1G) if g < G_L2G else 4 * (G_L2G - G_L1G + g - G_L3F)


NORMED = ["l0g", "l0f", "l1g", "l1g_out", "l1f", "l2g", "l2f", "l3g", "l3g_mid", "l3g_out", "l3f"]
LAYERS = [t for t in NORMED if "_" not in t]
STAGES = {
    "var": NORMED, "rstd": NORMED,
    "xn": LAYERS, "xt": LAYERS,
    "xhi": LAYERS[1:], "xlo": LAYERS[1:],
    "xt32": [t for t in LAYERS if t not in ("l1g", "l3g")],
    "logits": ["l0f", "l1f", "l2g", "l2f", "l3f"],
    "max": ["l0g", "l0f", "l2g", "l3f"], "exp": ["l0g", "l0f", "l2g", "l3g", "l3f"],
    "gates": ["l0f", "l1f", "l2g", "l2f"],
    "gT": ["l0f", "l1f", "l2f"], "gTs": ["l0f", "l1f", "l2f"],
    "seed": ["l0f", "l2f"],
}


def nth(stage, tag):
    return STAGES[stage].index(tag) + 1


def at(count, per, it):
    return count if it is None else count + per * it


def gnn_ffn_kernel(nc, A, out):
    with ExitStack() as ctx:
        def sb(name, shape, dt=F32):
            return ctx.enter_context(nc.sbuf_tensor(name, shape, dt))

        def bank(name):
            return ctx.enter_context(nc.psum_tensor(name, [P, D], F32))

        named = {}

        def sm(name):
            if name not in named:
                named[name] = ctx.enter_context(nc.semaphore("s_" + name))
            return named[name]

        raw = sb("raw", [P, RAW_SLOTS, KC, D])
        w_hi = sb("w_hi", [P, SPLIT_SLOTS, KC, D], F32R)
        w_lo = sb("w_lo", [P, SPLIT_SLOTS, KC, D], F32R)
        X = sb("X", [P, D])
        XN = sb("XN", [P, D])
        XT = sb("XT", [P, KC, P])
        x_hi = sb("x_hi", [P, KC, P], F32R)
        x_lo = sb("x_lo", [P, KC, P], F32R)
        h = sb("h", [P, 2, D])
        hT_hi = sb("hT_hi", [P, 2, KC, P], F32R)
        hT_lo = sb("hT_lo", [P, 2, KC, P], F32R)
        aggT_hi = sb("aggT_hi", [P, 2, KC, P], F32R)
        aggT_lo = sb("aggT_lo", [P, 2, KC, P], F32R)
        bias_hl = sb("bias_hl", [16, BL_COL + D], F32R)
        scratch = sb("scratch", [P, 4 * D])
        affine = sb("affine", [P, 4, D])
        side = sb("side", [P, KC, 256])
        b2 = sb("b2", [33, D])
        brow = sb("brow", [65, D])
        ones = sb("ones", [65, P])
        sel_all = sb("sel_all", [16, E8, P], F32R)
        sel = sb("sel", [16, 2, P], F32R)
        iota_t = sb("iota_t", [P, P])
        ident = sb("ident", [P, P])
        c_sd = sb("c_sd", [P, P])
        c_ds = sb("c_ds", [P, P])
        agg1 = sb("agg1", [P, P])
        agg2 = sb("agg2", [P, P])
        pen = sb("pen", [P, P])
        mat_a = sb("mat_a", [P, P])
        mat_b = sb("mat_b", [P, P])
        tri = sb("tri", [P, E8, E8])
        ends_i = sb("ends_i", [P, 2, EC], I32)
        ends = sb("ends", [P, 3, EC])
        wg0 = sb("wg0", [P, KC, E8])
        wr1 = sb("wr1", [P, KC, E8])
        wg2 = sb("wg2", [P, KC, E4])
        rw_n = sb("rw_n", [15, D])
        rwT = sb("rwT", [P, 2, KC, E8])
        rbias = sb("rbias", [P, 3, E8])
        l3w1 = sb("l3w1", [P, KC, 32])
        l3b1 = sb("l3b1", [32, 1])
        fT = sb("fT", [33, P])
        scal = sb("scal", [P, 3])
        ab = sb("ab", [P, 2])
        gates = sb("gates", [P, 16])
        gT = sb("gT", [E8, P])
        row = sb("row", [P, 8, E8])
        st = sb("st", [P, 6])
        mv = sb("mv", [P, 2])
        rstd = sb("rstd", [P, 2])
        mhalf = sb("mhalf", [P, 1])
        half = sb("half", [16, 2])
        hot = affine[:, 2:4, :].rearrange("p b n -> p (b n)")
        sel_raw = h[0:16, :, :].rearrange("p b n -> p (b n)")

        w_sd = agg1
        cmp = mat_b[:].rearrange("p (a n) -> p a n", a=2)

        pre = [bank("pre0"), bank("pre1")]
        tp = bank("tp")
        y = [bank("y0"), bank("y1")]
        wt = [bank("wt0"), bank("wt1")]
        ms = bank("ms")

        landed = [sm(f"landed{i}") for i in range(RAW_SLOTS)]
        w_hi_ready = sm("w_hi_ready")
        w_lo_ready = sm("w_lo_ready")
        w_turned = sm("w_turned")
        chunk_done = sm("chunk_done")
        h_ready = sm("h_ready")
        h_turned = sm("h_turned")
        hT_hi_ready = sm("hT_hi_ready")
        hT_lo_ready = sm("hT_lo_ready")
        y_summed = sm("y_summed")
        sel_ready = sm("sel_ready")
        dve_link = sm("dve_link")

        block = ctx.enter_context(nc.Block())

        def w1_unit(w, U, u, it):
            wv = w.rearrange("e (c p) n -> e p c n", p=P)
            return wv[at(u // U, 4 // U, it)][:, :, (u % U) * D:(u % U + 1) * D]

        def w2_unit(w, U, u, it):
            wv = w.rearrange("e (k c p) n -> e p k c n", c=KC, p=P)
            return wv[at(u // U, 4 // U, it)][:, u % U]

        @block.sync
        def _(sp):
            sp.dma_start(X[:], A["x"]).then_inc(sm("x_in"), 16)
            for n, name in ((0, "src"), (1, "dst")):
                sp.dma_start(ends_i[:, n], A[name].rearrange("(p k) -> p k", p=P)).then_inc(sm("edges_in"), 16)
            sp.dma_start(ends[:, 2], A["edge_weight"].rearrange("(p k) -> p k", p=P)).then_inc(sm("edges_in"), 16)

            def load(g, source, it=None):
                if g >= RAW_SLOTS or it is not None:
                    sp.wait_ge(w_lo_ready, at(4 * (g - RAW_SLOTS + 1), 32, it))
                sp.dma_start(raw[:, g % RAW_SLOTS], source).then_inc(landed[g % RAW_SLOTS], 16)

            def square(w):
                return w.rearrange("(c p) n -> p c n", p=P)

            def steps(pipe, w1, w2):
                def step(s, it=None):
                    g = pipe.chunk(s)
                    if s < pipe.n:
                        if s < pipe.lead:
                            for i, w in enumerate(("L3_ffn_sg_gate", "L3_ffn_sg_up")):
                                load(g + i, square(A[w][s * D:(s + 1) * D, :]))
                            return
                        load(g, w1(s - pipe.lead, it), it)
                        g += 1
                    if s >= 2:
                        if s - 2 < pipe.lead:
                            load(g, square(A["L3_ffn_sg_down"][:, (s - 2) * D:(s - 1) * D]))
                        else:
                            load(g, w2(s - 2 - pipe.lead, it), it)
                peeled = 8 if pipe.g0 == 0 else 4
                for s in range(peeled):
                    step(s)
                with sp.Fori(0, pipe.loops() - (peeled - 4) // 4) as it:
                    for s in range(peeled, peeled + 4):
                        step(s, it)
                for s in range(4 + 4 * pipe.loops(), pipe.n + 2):
                    step(s)

            steps(L0F, lambda u, it: w1_unit(A["L0_ffn_W1"], 2, u, it),
                  lambda u, it: w2_unit(A["L0_ffn_W2"], 2, u, it))
            load(G_L1G, square(A["L1_gnn_W1"]))
            load(G_L1G + 1, square(A["L1_gnn_W2"]))
            g = G_L2G
            for s in range(E4 + 2):
                for e, layer in ((s, 0), (s - 2, 1)):
                    if 0 <= e < E4:
                        load(g, square(A["L2_gnn_Wl"][e, layer]))
                        load(g + 1, square(A["L2_gnn_Wr"][e, layer]))
                        g += 2
            steps(L2F, lambda u, it: w1_unit(A["L2_ffn_w1"], 4, u, it),
                  lambda u, it: w2_unit(A["L2_ffn_w2"], 4, u, it))
            for i, name in enumerate(("L3_gnn_Wq", "L3_gnn_Wk", "L3_gnn_Wv", "L3_gnn_Wo")):
                load(G_L3G + i, square(A[name]))
            steps(L3F, lambda u, it: w2_unit(A["L3_ffn_w1"], 2, u, it),
                  lambda u, it: w1_unit(A["L3_ffn_w2"], 2, u, it))
            sp.wait_ge(y_summed, L3F.summed + L3F.n // 2)
            sp.dma_start(out, X[:]).then_inc(sm("out_written"), 16)
            sp.wait_ge(sm("out_written"), 16)

        @block.gpsimd
        def _(pool):
            n = [0]

            def link(ins):
                n[0] += 1
                ins.then_inc(sm("pool_link"), 1)
                pool.wait_ge(sm("pool_link"), n[0])

            link(pool.memset(ident[:], 0.0))
            link(pool.affine_select(out=ident[:], in_=ident[:], compare_op=ALU.not_equal, fill=1.0, base=0,
                                    pattern=[[-1, P]], channel_multiplier=1))
            link(pool.memset(mhalf[:], -0.5))
            pool.iota(iota_t[:], pattern=[[1, P]], base=0, channel_multiplier=0,
                      allow_small_or_imprecise_dtypes=True).then_inc(sm("consts"), 1)

            def inv_std(tag):
                pool.wait_ge(sm("var"), nth("var", tag))
                link(pool.tensor_scalar(rstd[:, 0:1], mv[:, 1:2], LN_EPS, None, ALU.add))
                pool.tensor_tensor(rstd[:, 1:2], rstd[:, 0:1], mhalf[:], ALU.pow).then_inc(sm("rstd"), 1)

            inv_std("l0g")
            link(pool.memset(tri[:], 1.0))
            link(pool.affine_select(out=tri[:], in_=tri[:], compare_op=ALU.is_gt, fill=0.0, base=0,
                                    pattern=[[1, E8], [-1, E8]], channel_multiplier=0))
            link(pool.memset(ones[:], 1.0))
            link(pool.memset(fT[:], 1.0))
            link(pool.memset(half[:], 1.0))
            link(pool.affine_select(out=half[:, 0:1], in_=half[:, 0:1], compare_op=ALU.is_gt, fill=0.0, base=-7,
                                    pattern=[[0, 1]], channel_multiplier=1))
            link(pool.affine_select(out=half[:, 1:2], in_=half[:, 1:2], compare_op=ALU.is_gt, fill=-1.0, base=8,
                                    pattern=[[0, 1]], channel_multiplier=-1))
            link(pool.memset(sel_raw, 0.0))
            for base in (0, -E8):
                link(pool.affine_select(out=sel_raw, in_=sel_raw, compare_op=ALU.not_equal, fill=1.0, base=base,
                                        pattern=[[-1, E8], [0, P]], channel_multiplier=1))
            pool.tensor_copy(sel_all[:].rearrange("p e n -> p (e n)"), sel_raw).then_inc(sm("sel_all"), 1)

            for tag in NORMED[1:]:
                inv_std(tag)

        @block.scalar
        def _(act):
            def small(dst, src, sem):
                act.dma_start(dst, src).then_inc(sm(sem), 16)

            emb = [A[n].rearrange("(c p) n -> p c n", p=P) for n in ("L0_gnn_emb_1", "L0_gnn_emb_2")]
            small(side[:, :, 0:P], emb[0], "emb_in")
            small(side[:, :, P:2 * P], emb[1], "emb_in")
            for i, name in enumerate(("L0_gnn_alpha_p", "L0_gnn_beta_p", "L1_gnn_eps")):
                small(scal[:, i:i + 1], A[name].partition_broadcast(P), "scal_in")
            small(wg0[:], A["L0_ffn_Wg"].rearrange("(c p) n -> p c n", p=P), "routers_in")
            small(wr1[:], A["L1_ffn_Wr"].rearrange("(c p) n -> p c n", p=P), "routers_in")
            small(wg2[:], A["L2_gnn_gate_W"].rearrange("(c p) n -> p c n", p=P), "routers_in")
            for top in (0, E8):
                small(scratch[top:top + E8, 0:2 * D], A["L0_ffn_b1"], "bias_in")
                small(scratch[top:top + E8, 2 * D:3 * D], A["L2_gnn_bl"].rearrange("e l n -> (e l) n"), "bias_in")
            small(b2[0:E8, :], A["L0_ffn_b2"], "b2_l0")
            small(rw_n[0:7, :], A["L2_ffn_rw"], "rw_in")
            small(rw_n[7:15, :], A["L3_ffn_gate_w"], "rw_in")
            small(rbias[:, 0, :], A["L1_ffn_br"].partition_broadcast(P), "rbias_in")
            small(rbias[:, 1, 0:E4], A["L2_gnn_gate_b"].partition_broadcast(P), "rbias_in")
            small(rbias[:, 2, 0:7], A["L2_ffn_rb"].partition_broadcast(P), "rbias_in")
            for i, name in enumerate(("L1_gnn_b1", "L1_gnn_b2")):
                small(brow[32 * i:32 * i + 1, :], A[name].rearrange("(a n) -> a n", a=1), "brow_in")
            small(brow[64:65, 0:E8 * H1], A["L1_ffn_b1"].rearrange("(a e) n -> a (e n)", a=1), "brow_in")
            small(affine[:, 0], A["L1_gnn_gamma"].partition_broadcast(P), "affine_l1")
            small(affine[:, 1], A["L1_gnn_beta"].partition_broadcast(P), "affine_l1")
            small(l3w1[:], A["L3_gnn_W1"].rearrange("(c p) n -> p c n", p=P), "l3_small_in")
            small(l3b1[:], A["L3_gnn_b1"].rearrange("(n a) -> n a", a=1), "l3_small_in")

            def round_chunk(g, it=None):
                if g >= CHUNKS:
                    return
                if g >= SPLIT_SLOTS or it is not None:
                    act.wait_ge(chunk_done, at(g - SPLIT_SLOTS + 1, 8, it))
                if transposed(g):
                    for q in range(4):
                        act.wait_ge(w_turned, at(turned_quarters(g) + q + 1, 32, it))
                        act.activation(w_hi[:, g % SPLIT_SLOTS, q], wt[q % 2][:], ACT.Copy).then_inc(w_hi_ready, 1)
                else:
                    act.wait_ge(landed[g % RAW_SLOTS], at(16 * (g // RAW_SLOTS + 1), 16, it))
                    act.activation(w_hi[:, g % SPLIT_SLOTS], raw[:, g % RAW_SLOTS], ACT.Copy).then_inc(w_hi_ready, 4)

            def round_x(tag, plain):
                act.wait_ge(sm("xt"), nth("xt", tag))
                act.activation(x_hi[:], tp[:].rearrange("p (c n) -> p c n", n=P), ACT.Copy).then_inc(sm("xhi"), 1)
                if plain:
                    act.wait_ge(sm("xlo"), nth("xlo", tag))
                    act.activation(XT[:], tp[:].rearrange("p (c n) -> p c n", n=P), ACT.Copy).then_inc(
                        sm("xt32"), 1)

            def round_turned(ready, bank_ap, dst, done):
                act.wait_ge(sm(ready), 1)
                act.activation(dst, bank_ap[:].rearrange("p (c n) -> p c n", n=P), ACT.Copy).then_inc(sm(done), 1)

            def pipeline(pipe, after0):
                def step(s, it=None):
                    g = pipe.chunk(s)
                    if s < pipe.n:
                        round_chunk(g + AHEAD, it)
                        if s < pipe.lead:
                            round_chunk(g + 1 + AHEAD, it)
                        g += 1
                    if 1 <= s <= pipe.n:
                        act.wait_ge(h_turned, at(pipe.turned + s, 4, it))
                        act.activation(hT_hi[:, (s - 1) % 2], tp[:].rearrange("p (c n) -> p c n", n=P),
                                       ACT.Copy).then_inc(hT_hi_ready, 1)
                    if s < pipe.lead:
                        act.wait_ge(chunk_done, pipe.chunk(s) + 2)
                        act.activation(h[:, s % 2], pre[s % 2][:], pipe.act).then_inc(sm("gate_ready"), 1)
                    elif s < pipe.n:
                        act.wait_ge(chunk_done, at(pipe.chunk(s) + 1, 8, it))
                        act.activation(h[:, s % 2], pre[s % 2][:], pipe.act).then_inc(h_ready, 1)
                    if s == 0:
                        after0()
                    if s >= 2:
                        round_chunk(g + AHEAD, it)
                for s in range(4):
                    step(s)
                with act.Fori(0, pipe.loops()) as it:
                    for s in range(4, 8):
                        step(s, it)
                for s in range(4 + 4 * pipe.loops(), pipe.n + 2):
                    step(s)

            def exp_logits(tag, E):
                act.wait_ge(sm("max"), nth("max", tag))
                act.activation(row[:, 1, 0:E], row[:, 0, 0:E], ACT.Exp, bias=row[:, 7, 0:1],
                               accum_out=row[:, 7, 1:2]).then_inc(sm("exp"), 1)

            act.wait_ge(sm("scal_in"), 48)
            act.activation(ab[:], scal[:, 0:2], ACT.Exp).then_inc(sm("ab"), 1)
            act.wait_ge(sm("bias_in"), 64)
            act.activation(bias_hl[:, 0:2 * D], scratch[0:16, 0:2 * D], ACT.Copy).then_inc(sm("bias_hi"), 1)
            act.activation(bias_hl[:, BL_COL:BL_COL + D], scratch[0:16, 2 * D:3 * D], ACT.Copy).then_inc(sm("bias_hi"), 1)
            act.wait_ge(sm("xt"), nth("xt", "l0g"))
            act.activation(XT[:], tp[:].rearrange("p (c n) -> p c n", n=P), ACT.Copy).then_inc(sm("xt32"), 1)
            act.wait_ge(sm("l0g_x12"), 1)
            act.wait_ge(sm("sel_all"), 1)
            act.activation(h[:, 0, 0:2 * P], pre[0][:, 0:2 * P], ACT.Copy).then_inc(sm("l0g_x12s"), 1)
            act.wait_ge(sm("max"), nth("max", "l0g"))
            act.activation(mat_b[:], mat_a[:], ACT.Exp, bias=row[:, 0, 0:1],
                           accum_out=row[:, 0, 1:2]).then_inc(sm("exp"), 1)
            for c in range(KC):
                small(side[:, c].rearrange("p (e n) -> p e n", n=H1),
                      A["L1_ffn_W1"][:, c * P:(c + 1) * P, :].rearrange("e p n -> p e n"), "l1f_w1")
            round_chunk(0)
            round_chunk(1)
            round_x("l0f", True)
            pipeline(L0F, lambda: exp_logits("l0f", E8))
            act.wait_ge(sm("bias_free"), 1)
            for top in (0, E8):
                small(scratch[top:top + E8, :], A["L2_ffn_b1"], "bias_in")
            small(b2[0:E8, :], A["L1_ffn_b2"], "b2_l1")
            round_x("l1g", False)
            act.wait_ge(chunk_done, G_L1G + 1)
            act.activation(h[:, 0], pre[0][:], ACT.Relu).then_inc(sm("l1g_h"), 1)
            round_chunk(G_L1G + 2)
            round_turned("l1g_hT", tp, hT_hi[:, 0], "l1g_hThi")
            act.wait_ge(sm("bias_in"), 96)
            act.activation(bias_hl[:, 0:BL_COL], scratch[0:16, :], ACT.Copy).then_inc(sm("bias_hi"), 1)
            round_chunk(G_L1G + 3)
            act.wait_ge(sm("l2_bias"), 1)
            small(scratch[:, 0:2 * D].rearrange("p (c n) -> p c n", n=D),
                  A["L1_ffn_W2"].rearrange("(c a) b n -> (a b) c n", a=4), "l1f_w2")
            round_x("l1f", True)
            act.wait_ge(sm("l1f_hT"), 1)
            act.activation(h[:, 1, 0:2 * P], tp[:, 0:2 * P], ACT.Copy).then_inc(sm("l1f_hTs"), 1)
            small_done = sm("l1f_done")
            act.wait_ge(small_done, 1)
            small(b2[0:E8, :], A["L2_ffn_b2"], "b2_l2")
            for i, name in enumerate(("L3_gnn_ln1_g", "L3_gnn_ln1_b", "L3_gnn_ln2_g", "L3_gnn_ln2_b")):
                small(affine[:, i], A[name].partition_broadcast(P), "affine_l3")
            round_x("l2g", True)
            round_turned("l2g_xagg", y[0], aggT_hi[:, 0], "l2g_xagghi")
            exp_logits("l2g", E4)
            g = G_L2G
            for s in range(E4 + 2):
                if s < E4:
                    round_chunk(g + AHEAD)
                    round_chunk(g + 1 + AHEAD)
                    act.wait_ge(chunk_done, g + 2)
                    act.activation(h[:, s % 2], pre[s % 2][:], ACT.Relu).then_inc(sm("l2g_h"), 1)
                    g += 2
                if s >= 2:
                    round_chunk(g + AHEAD)
                    round_chunk(g + 1 + AHEAD)
                    act.wait_ge(sm("gates"), nth("gates", "l2g"))
                    act.wait_ge(chunk_done, g + 2)
                    if s >= 4:
                        act.wait_ge(sm("l2g_summed"), s - 3)
                    act.activation(scratch[:, (s % 2) * D:(s % 2 + 1) * D], y[s % 2][:], ACT.Relu,
                                   scale=gates[:, s - 2:s - 1]).then_inc(sm("l2g_out"), 1)
                    g += 2
                if 1 <= s <= E4:
                    act.wait_ge(sm("l2g_turned"), s)
                    act.activation(hT_hi[:, 0], tp[:].rearrange("p (c n) -> p c n", n=P), ACT.Copy).then_inc(
                        sm("l2g_hi"), 1)
                    act.activation(aggT_hi[:, 1], wt[0][:].rearrange("p (c n) -> p c n", n=P), ACT.Copy).then_inc(
                        sm("l2g_hi"), 1)
            def leaf_sigmoid():
                act.wait_ge(sm("l2f_tree"), 1)
                act.activation(row[:, 1, 0:7], row[:, 0, 0:7], ACT.Sigmoid).then_inc(sm("l2f_p"), 1)
            round_x("l2f", True)
            pipeline(L2F, leaf_sigmoid)
            small(b2[0:32, :], A["L3_gnn_W2"], "l3_small_in")
            small(b2[32:33, :], A["L3_gnn_b2"].rearrange("(a n) -> a n", a=1), "l3_small_in")
            round_x("l3g", False)
            round_chunk(G_L3G + 2)
            act.wait_ge(chunk_done, G_L3G + 1)
            act.activation(h[:, 0], pre[0][:], ACT.Copy).then_inc(sm("l3g_q"), 1)
            round_chunk(G_L3G + 3)
            act.wait_ge(sm("l3g_qT"), 1)
            act.activation(scratch[:, 2 * D:3 * D], tp[:], ACT.Copy).then_inc(sm("l3g_qTs"), 1)
            round_chunk(G_L3G + 4)
            act.wait_ge(chunk_done, G_L3G + 3)
            act.activation(XT[:].rearrange("p c n -> p (c n)"), y[0][:], ACT.Copy).then_inc(sm("l3g_v"), 1)
            act.wait_ge(sm("l3g_centred"), 1)
            act.activation(scratch[:, 0:2 * D], scratch[:, 0:2 * D], ACT.Exp).then_inc(sm("exp"), 1)
            act.wait_ge(sm("l3g_pT"), 1)
            act.activation(side[:, 0:2].rearrange("p c n -> p (c n)"), tp[:], ACT.Copy).then_inc(sm("l3g_pTs0"), 1)
            round_turned("l3g_aT", tp, hT_hi[:, 0], "l3g_aThi")
            round_chunk(G_L3G + 5)
            act.wait_ge(sm("l3g_midT"), 1)
            act.activation(XT[:], tp[:].rearrange("p (c n) -> p c n", n=P), ACT.Copy).then_inc(sm("l3g_midTs"), 1)
            act.wait_ge(sm("l3g_f1"), 1)
            act.activation(fT[0:32, :], ms[0:32, 0:P], ACT.Relu, bias=l3b1[:, 0:1]).then_inc(sm("l3g_f1s"), 1)
            round_x("l3f", True)
            pipeline(L3F, lambda: exp_logits("l3f", E8))

        @block.tensor
        def _(pe):
            def turn_weights(g, q, it=None):
                if q == 0:
                    pe.wait_ge(landed[g % RAW_SLOTS], at(16 * (g // RAW_SLOTS + 1), 16, it))
                pe.wait_ge(w_lo_ready, at(4 * g + q - 1, 32, it))
                for c in range(KC):
                    last = pe.transpose(wt[q % 2][:, c * P:(c + 1) * P], raw[:, g % RAW_SLOTS, c, q * P:(q + 1) * P],
                                        ident[:])
                last.then_inc(w_turned, 1)

            def product(g, dst, xs_hi, xs_lo, start, stop, it=None, bias=None):
                pe.wait_ge(w_lo_ready, at(4 * (g + 1), 32, it))
                for k in range(KC):
                    if g + AHEAD < CHUNKS and transposed(g + AHEAD):
                        turn_weights(g + AHEAD, k, it)
                    hi, lo = w_hi[:, g % SPLIT_SLOTS, k], w_lo[:, g % SPLIT_SLOTS, k]
                    pe.matmul(dst, xs_hi[:, k], hi, start=start and k == 0, stop=False)
                    pe.matmul(dst, xs_hi[:, k], lo, start=False, stop=False)
                    last = pe.matmul(dst, xs_lo[:, k], hi, start=False, stop=stop and k == KC - 1 and bias is None)
                if bias is not None:
                    pair, rows, halves = bias
                    pe.wait_ge(sel_ready, pair)
                    last = pe.matmul(dst, rows, halves, start=False, stop=True)
                last.then_inc(chunk_done, 1)

            def turn(dst, src, done, n=KC):
                for c in range(n):
                    last = pe.transpose(dst[:, c * P:(c + 1) * P], src[:, c * P:(c + 1) * P], ident[:])
                last.then_inc(done, 1)

            def turn_x(tag):
                pe.wait_ge(sm("xn"), nth("xn", tag))
                turn(tp, XN, sm("xt"))

            def logits(tag, w, E):
                pe.wait_ge(sm("xt32"), nth("xt32", tag))
                for c in range(KC):
                    last = pe.matmul(ms[:, 0:E], XT[:, c], w[:, c, 0:E], start=c == 0, stop=c == KC - 1)
                last.then_inc(sm("logits"), 1)

            def turn_gates(tag, n):
                pe.wait_ge(sm("gates"), nth("gates", tag))
                pe.transpose(ms[0:n, 0:P], gates[:, 0:n], ident[:]).then_inc(sm("gT"), 1)

            def seed(tag, dst):
                pe.wait_ge(sm("gTs"), nth("gTs", tag))
                return pe.matmul(dst, gT[:], b2[0:E8, :], start=True, stop=tag != "l1f")

            def pipeline(pipe, router, seeded):
                def step(s, it=None):
                    g = pipe.chunk(s)
                    if s < pipe.lead:
                        product(g, pre[s % 2][:], x_hi, x_lo, True, True)
                        product(g + 1, y[s % 2][:], x_hi, x_lo, True, True)
                    elif s < pipe.n:
                        bias = None
                        if pipe.selected is not None:
                            col = (s % pipe.U) * D
                            bias = (at(pipe.selected + s // 2 + 1, 2, it), sel[:, (s // 2) % 2], bias_hl[:, col:col + D])
                        product(g, pre[s % 2][:], x_hi, x_lo, True, True, it, bias)
                        g += 1
                    if s == 0:
                        router()
                    if s == 1 and seeded:
                        turn_gates(pipe.tag, E8)
                    if 1 <= s <= pipe.n:
                        if s - 1 < pipe.lead:
                            pe.wait_ge(sm("shared_ready"), s)
                        else:
                            routed_before = pipe.turned
                            pe.wait_ge(h_ready, at(routed_before + s - pipe.lead, 4, it))
                        if pipe.turned + s - 1 > 0:
                            pe.wait_ge(hT_lo_ready, at(pipe.turned + s - 1, 4, it))
                        turn(tp, h[:, (s - 1) % 2], h_turned)
                    if s == 1 and seeded:
                        seed(pipe.tag, wt[0][:]).then_inc(sm("seed"), 1)
                    if s >= 2:
                        pe.wait_ge(hT_lo_ready, at(pipe.turned + s - 1, 4, it))
                        if s % 2 == 0 and s >= 4:
                            pe.wait_ge(y_summed, at(pipe.summed + (s - 4) // 2, 2, it))
                        product(g, y[((s - 2) // 2) % 2][:], hT_hi[:, s % 2], hT_lo[:, s % 2],
                                s % 2 == 0, s % 2 == 1, it)
                for s in range(4):
                    step(s)
                with pe.Fori(0, pipe.loops()) as it:
                    for s in range(4, 8):
                        step(s, it)
                for s in range(4 + 4 * pipe.loops(), pipe.n + 2):
                    step(s)

            pe.wait_ge(sm("consts"), 1)
            turn_x("l0g")
            pe.wait_ge(sm("xt32"), nth("xt32", "l0g"))
            pe.wait_ge(sm("emb_in"), 32)
            for i in range(2):
                for c in range(KC):
                    last = pe.matmul(pre[0][:, i * P:(i + 1) * P], side[:, c, i * P:(i + 1) * P], XT[:, c],
                                     start=c == 0, stop=c == KC - 1)
            last.then_inc(sm("l0g_x12"), 1)
            for k in range(EC):
                o = (k % 2) * 3 * P
                pe.wait_ge(sm("hot_ready"), k + 1)
                pe.matmul(y[0][:, 0:2 * P], hot[:, o:o + P], hot[:, o + P:o + 3 * P], start=k == 0,
                          stop=k == EC - 1).then_inc(sm("hot_used"), 1)
            pe.wait_ge(sm("l0g_x12s"), 1)
            pe.matmul(ms[:, 0:P], h[:, 0, 0:P], h[:, 0, P:2 * P], start=True, stop=True).then_inc(sm("l0g_sim"), 1)
            pe.wait_ge(sm("c_sd"), 1)
            pe.transpose(wt[0][:, 0:P], c_sd[:], ident[:]).then_inc(sm("c_dsT"), 1)
            pe.wait_ge(sm("l0g_a"), 1)
            pe.transpose(ms[:, 0:P], mat_a[:], ident[:]).then_inc(sm("l0g_aT"), 1)
            pe.wait_ge(sm("l0g_aTs"), 1)
            for i in range(5):
                for half_ in range(2):
                    cols = slice(half_ * 256, half_ * 256 + 256)
                    if i:
                        pe.wait_ge(sm("l0g_swept"), 2 * (i - 1) + half_ + 1)
                    pe.matmul(pre[half_][:, 0:256], mat_b[:], XT[:].rearrange("p c n -> p (c n)")[:, cols] if i
                              else XN[:, cols], start=True, stop=True).then_inc(sm("l0g_sweep"), 1)
            pe.wait_ge(sm("rw_in"), 32)
            pe.wait_ge(sm("c_ds"), 1)
            for c in range(KC):
                last = pe.transpose(wt[1][:, c * 15:(c + 1) * 15], rw_n[:, c * P:(c + 1) * P], ident[0:15, 0:15])
            last.then_inc(sm("rwT"), 1)
            pe.wait_ge(sm("agg2_rows"), 1)
            pe.transpose(wt[0][:, 0:P], mat_a[:], ident[:]).then_inc(sm("agg2T"), 1)
            pe.wait_ge(sm("routers_in"), 48)
            pe.wait_ge(sm("l0_bias"), 1)
            turn_x("l0f")
            pe.wait_ge(sm("xlo"), nth("xlo", "l0f"))
            pe.wait_ge(sm("b2_l0"), 16)
            pipeline(L0F, lambda: logits("l0f", wg0, E8), True)
            pe.wait_ge(sm("xn"), nth("xn", "l1g"))
            for c in range(KC):
                last = pe.matmul(tp[:, c * P:(c + 1) * P], XN[:, c * P:(c + 1) * P], agg1[:], start=True, stop=True)
            last.then_inc(sm("xt"), 1)
            pe.wait_ge(sm("brow_in"), 48)
            pe.matmul(pre[0][:], ones[0:1, :], brow[0:1, :], start=True, stop=False)
            pe.matmul(pre[1][:], ones[32:33, :], brow[32:33, :], start=True, stop=False)
            pe.wait_ge(sm("xlo"), nth("xlo", "l1g"))
            product(G_L1G, pre[0][:], x_hi, x_lo, False, True)
            pe.wait_ge(sm("l1g_h"), 1)
            turn(tp, h[:, 0], sm("l1g_hT"))
            pe.wait_ge(sm("l1g_hTlo"), 1)
            product(G_L1G + 1, pre[1][:], hT_hi[:, 0], hT_lo[:, 0], False, True)
            turn_x("l1f")
            pe.matmul(pre[0][:, 0:256], ones[64:65, :], brow[64:65, 0:256], start=True, stop=False)
            logits("l1f", wr1, E8)
            pe.wait_ge(sm("l1f_w1"), 16 * KC)
            for c in range(KC):
                last = pe.matmul(pre[0][:, 0:256], XT[:, c], side[:, c], start=False, stop=c == KC - 1)
            last.then_inc(sm("l1f_pre"), 1)
            turn_gates("l1f", E8)
            pe.wait_ge(sm("b2_l1"), 16)
            seed("l1f", y[0][:])
            pe.wait_ge(sm("l1f_h"), 1)
            turn(tp, h[:, 0], sm("l1f_hT"), 2)
            pe.wait_ge(sm("l1f_hTs"), 1)
            pe.wait_ge(sm("l1f_w2"), 16)
            for c in range(2):
                last = pe.matmul(y[0][:], h[:, 1, c * P:(c + 1) * P], scratch[:, c * D:(c + 1) * D], start=False,
                                 stop=c == 1)
            last.then_inc(sm("l1f_y"), 1)
            turn_x("l2g")
            for c in range(KC):
                last = pe.matmul(y[0][:, c * P:(c + 1) * P], XN[:, c * P:(c + 1) * P], agg2[:], start=True, stop=True)
            last.then_inc(sm("l2g_xagg"), 1)
            logits("l2g", wg2, E4)
            g = G_L2G
            pe.wait_ge(sm("l2g_xagglo"), 1)
            for s in range(E4 + 2):
                if s < E4:
                    pe.matmul(pre[s % 2][:], sel_all[:, 2 * s], bias_hl[:, BL_COL:BL_COL + D], start=True, stop=False)
                    product(g, pre[s % 2][:], aggT_hi[:, 0], aggT_lo[:, 0], False, False)
                    product(g + 1, pre[s % 2][:], x_hi, x_lo, False, True)
                    g += 2
                if s >= 2:
                    pe.wait_ge(sm("l2g_lo"), 2 * (s - 1))
                    if s >= 4:
                        pe.wait_ge(sm("l2g_out"), s - 3)
                    pe.matmul(y[s % 2][:], sel_all[:, 2 * (s - 2) + 1], bias_hl[:, BL_COL:BL_COL + D], start=True,
                              stop=False)
                    product(g, y[s % 2][:], aggT_hi[:, 1], aggT_lo[:, 1], False, False)
                    product(g + 1, y[s % 2][:], hT_hi[:, 0], hT_lo[:, 0], False, True)
                    g += 2
                if 1 <= s <= E4:
                    pe.wait_ge(sm("l2g_h"), s)
                    hs = h[:, (s - 1) % 2]
                    for c in range(KC):
                        pe.transpose(tp[:, c * P:(c + 1) * P], hs[:, c * P:(c + 1) * P], ident[:])
                    for c in range(KC):
                        last = pe.matmul(wt[0][:, c * P:(c + 1) * P], hs[:, c * P:(c + 1) * P], agg2[:], start=True,
                                         stop=True)
                    last.then_inc(sm("l2g_turned"), 1)
            pe.wait_ge(sm("l2_bias"), 1)
            turn_x("l2f")
            pe.wait_ge(sm("xlo"), nth("xlo", "l2f"))
            pe.wait_ge(sm("b2_l2"), 16)
            pipeline(L2F, lambda: logits("l2f", rwT[:, 0], 7), True)
            turn_x("l3g")
            pe.wait_ge(sm("xlo"), nth("xlo", "l3g"))
            product(G_L3G, pre[0][:], x_hi, x_lo, True, True)
            product(G_L3G + 1, pre[1][:], x_hi, x_lo, True, True)
            pe.wait_ge(sm("l3g_q"), 1)
            turn(tp, h[:, 0], sm("l3g_qT"))
            pe.wait_ge(sm("l3g_k"), 1)
            turn(y[1], h[:, 1], sm("l3g_kT"))
            product(G_L3G + 2, y[0][:], x_hi, x_lo, True, True)
            pe.wait_ge(sm("l3g_qTs"), 1)
            pe.wait_ge(sm("l3g_kTs"), 1)
            for j in range(HEADS // 2):
                for p in range(2):
                    rows = slice(p * DK, (p + 1) * DK)
                    last = pe.matmul(pre[p][:, j * P:(j + 1) * P], scratch[rows, 2 * D + j * P:2 * D + (j + 1) * P],
                                     scratch[rows, 3 * D + j * P:3 * D + (j + 1) * P], start=True, stop=True)
            last.then_inc(sm("l3g_scores"), 1)
            pe.wait_ge(sm("l3g_p"), 1)
            for p in range(2):
                for j in range(HEADS // 2):
                    i = 4 * p + j
                    last = pe.transpose((tp, y[1])[p][:, j * P:(j + 1) * P], scratch[:, i * P:(i + 1) * P], ident[:])
            last.then_inc(sm("l3g_pT"), 1)
            pe.wait_ge(sm("l3g_v"), 1)
            pe.wait_ge(sm("l3g_pTs0"), 1)
            pe.wait_ge(sm("l3g_pTs1"), 1)
            probs_T = side[:].rearrange("p c n -> p (c n)")
            for p in range(2):
                for j in range(HEADS // 2):
                    i, hd = 4 * p + j, 2 * j + p
                    last = pe.matmul(pre[0][:, hd * DK:(hd + 1) * DK], probs_T[:, i * P:(i + 1) * P],
                                     XT[:].rearrange("p c n -> p (c n)")[:, hd * DK:(hd + 1) * DK], start=True, stop=True)
            last.then_inc(sm("l3g_av"), 1)
            pe.wait_ge(sm("l3g_a"), 1)
            turn(tp, h[:, 0], sm("l3g_aT"))
            pe.wait_ge(sm("l3g_aTlo"), 1)
            product(G_L3G + 3, pre[1][:], hT_hi[:, 0], hT_lo[:, 0], True, True)
            pe.wait_ge(sm("l3g_mid"), 1)
            turn(tp, h[:, 1], sm("l3g_midT"))
            pe.wait_ge(sm("l3g_midTs"), 1)
            pe.wait_ge(sm("l3_small_in"), 64)
            for c in range(KC):
                last = pe.matmul(ms[0:32, 0:P], l3w1[:, c], XT[:, c], start=c == 0, stop=c == KC - 1)
            last.then_inc(sm("l3g_f1"), 1)
            pe.wait_ge(sm("l3g_f1s"), 1)
            pe.matmul(y[0][:], fT[:], b2[:], start=True, stop=True).then_inc(sm("l3g_f2"), 1)
            turn_x("l3f")
            pe.wait_ge(sm("xlo"), nth("xlo", "l3f"))
            pipeline(L3F, lambda: logits("l3f", rwT[:, 1], E8), False)

        @block.vector
        def _(dve):
            n = [0]

            def link(ins):
                n[0] += 1
                ins.then_inc(dve_link, 1)
                dve.wait_ge(dve_link, n[0])

            def chunks4(ap):
                return ap[:].rearrange("p (c n) -> p c n", n=P)

            def statistics(tag, src):
                link(dve.bn_stats(st[:], src))
                dve.bn_aggr(mv[:], st[:]).then_inc(sm("var"), 1)

            def normalise(tag, dst, src):
                dve.wait_ge(sm("rstd"), nth("rstd", tag))
                return dve.tensor_scalar(dst, src, mv[:, 0:1], rstd[:, 1:2], ALU.subtract, ALU.mult)

            def layer_norm(tag):
                statistics(tag, X[:])
                normalise(tag, XN[:], X[:]).then_inc(sm("xn"), 1)

            def low_x(tag):
                dve.wait_ge(sm("xhi"), nth("xhi", tag))
                dve.tensor_tensor(x_lo[:], chunks4(tp), x_hi[:].bitcast(F32), ALU.subtract).then_inc(
                    sm("xlo"), 1)

            def low_turned(ready, bank_ap, hi, dst, done):
                dve.wait_ge(sm(ready), 1)
                dve.tensor_tensor(dst, chunks4(bank_ap), hi.bitcast(F32), ALU.subtract).then_inc(sm(done), 1)

            def split_chunk(g, it=None):
                if g >= CHUNKS:
                    return
                i = g % SPLIT_SLOTS
                if transposed(g):
                    for q in range(4):
                        dve.wait_ge(w_hi_ready, at(4 * g + q + 1, 32, it))
                        dve.tensor_tensor(w_lo[:, i, q], wt[q % 2][:], w_hi[:, i, q].bitcast(F32),
                                          ALU.subtract).then_inc(w_lo_ready, 1)
                else:
                    dve.wait_ge(w_hi_ready, at(4 * (g + 1), 32, it))
                    dve.tensor_tensor(w_lo[:, i], raw[:, g % RAW_SLOTS], w_hi[:, i].bitcast(F32),
                                      ALU.subtract).then_inc(w_lo_ready, 4)

            def top(values, E, k, src, dst):
                one, other = values.unsqueeze(1).broadcast_to([P, E, E]), values.unsqueeze(2).broadcast_to([P, E, E])
                above = cmp[:, 0, 0:E * E].rearrange("p (a b) -> p a b", b=E)
                equal = cmp[:, 1, 0:E * E].rearrange("p (a b) -> p a b", b=E)
                link(dve.tensor_tensor(above, one, other, ALU.is_gt))
                link(dve.tensor_tensor(equal, one, other, ALU.is_equal))
                link(dve.tensor_tensor(equal, equal, tri[:, 0:E, 0:E], ALU.mult))
                link(dve.tensor_tensor(above, above, equal, ALU.add))
                link(dve.reduce_sum(row[:, 6, 0:E], above, AX_X))
                return dve.scalar_tensor_tensor(out=dst, in0=row[:, 6, 0:E], scalar=float(k), in1=src,
                                                op0=ALU.is_lt, op1=ALU.mult)

            def logits_in(tag, E, bias=None):
                dve.wait_ge(sm("logits"), nth("logits", tag))
                if bias is None:
                    link(dve.tensor_copy(row[:, 0, 0:E], ms[:, 0:E]))
                else:
                    return dve.tensor_tensor(row[:, 0, 0:E], ms[:, 0:E], rbias[:, bias, 0:E], ALU.add)

            def negative_max(tag, E):
                link(dve.reduce_max(row[:, 7, 2:3], row[:, 0, 0:E], AX_X))
                dve.tensor_scalar(row[:, 7, 0:1], row[:, 7, 2:3], -1.0, None, ALU.mult).then_inc(sm("max"), 1)

            def softmax_top(tag, E, k):
                dve.wait_ge(sm("exp"), nth("exp", tag))
                link(dve.reciprocal(row[:, 7, 3:4], row[:, 7, 1:2]))
                link(dve.tensor_scalar(row[:, 2, 0:E], row[:, 1, 0:E], row[:, 7, 3:4], None, ALU.mult))
                top(row[:, 2, 0:E], E, k, row[:, 2, 0:E], gates[:, 0:E]).then_inc(sm("gates"), 1)

            def copy_gates(tag):
                dve.wait_ge(sm("gT"), nth("gT", tag))
                dve.tensor_copy(gT[:], ms[0:E8, 0:P]).then_inc(sm("gTs"), 1)

            def pipeline(pipe, router, per_gate, seeded):
                def select(q, it=None):
                    e = q // (pipe.U // 2)
                    src = sel_all[:, e] if it is None else sel_all[:].rearrange("p e n -> p (e n)")[
                        :, bass.ds((e + (4 // pipe.U) * it) * P, P)]
                    dve.tensor_scalar(sel[:, q % 2], src.bitcast(F32), 1.0, None, ALU.mult).then_inc(sel_ready, 1)

                def step(s, it=None):
                    g = pipe.chunk(s)
                    if pipe.selected is not None and s % 2 == 0 and 4 <= s < pipe.n:
                        select(s // 2, it)
                    if s < pipe.n:
                        split_chunk(g + AHEAD, it)
                        if s < pipe.lead:
                            split_chunk(g + 1 + AHEAD, it)
                        g += 1
                    if s == 0:
                        router()
                    if s == 1 and seeded:
                        copy_gates(pipe.tag)
                    if 1 <= s <= pipe.n:
                        dve.wait_ge(hT_hi_ready, at(pipe.turned + s, 4, it))
                        dve.tensor_tensor(hT_lo[:, (s - 1) % 2], chunks4(tp), hT_hi[:, (s - 1) % 2].bitcast(F32),
                                          ALU.subtract).then_inc(hT_lo_ready, 1)
                    if s < pipe.lead:
                        dve.wait_ge(sm("gate_ready"), s + 1)
                        dve.tensor_tensor(h[:, s % 2], h[:, s % 2], y[s % 2][:], ALU.mult).then_inc(sm("shared_ready"), 1)
                    if s == 1 and seeded:
                        dve.wait_ge(sm("seed"), nth("seed", pipe.tag))
                        dve.tensor_tensor(X[:], X[:], wt[0][:], ALU.add).then_inc(y_summed, 1)
                    if s % 2 == 0 and s >= 4:
                        add_pair((s - 4) // 2, it)
                    if s >= 2:
                        split_chunk(g + AHEAD, it)

                def add_pair(q, it=None):
                    last = pipe.chunk(2 * q + 3) + (1 if 2 * q + 3 < pipe.n else 0)
                    dve.wait_ge(chunk_done, at(last + 1, 8, it))
                    dve.wait_ge(y_summed, at(pipe.summed + q, 2, it)) if pipe.summed + q > 0 else None
                    col = q // per_gate
                    gate = gates[:, col:col + 1] if it is None else gates[:, bass.ds(col + (2 // per_gate) * it, 1)]
                    dve.scalar_tensor_tensor(out=X[:], in0=y[q % 2][:], scalar=gate, in1=X[:], op0=ALU.mult,
                                             op1=ALU.add).then_inc(y_summed, 1)

                if pipe.selected is not None:
                    select(0)
                    select(1)
                for s in range(4):
                    step(s)
                with dve.Fori(0, pipe.loops()) as it:
                    for s in range(4, 8):
                        step(s, it)
                for s in range(4 + 4 * pipe.loops(), pipe.n + 2):
                    step(s)
                add_pair((pipe.n - 2) // 2)
                dve.wait_ge(y_summed, pipe.summed + pipe.n // 2)

            dve.wait_ge(sm("x_in"), 16)
            layer_norm("l0g")
            dve.wait_ge(sm("edges_in"), 48)
            link(dve.tensor_copy(ends[:, 0:2], ends_i[:]))
            dve.wait_ge(sm("consts"), 1)
            for k in range(EC):
                o = (k % 2) * 3 * P
                if k >= 2:
                    dve.wait_ge(sm("hot_used"), k - 1)
                dve.tensor_scalar(hot[:, o:o + P], iota_t[:], ends[:, 0, k:k + 1], None, ALU.is_equal)
                dve.tensor_scalar(hot[:, o + P:o + 2 * P], iota_t[:], ends[:, 1, k:k + 1], ends[:, 2, k:k + 1],
                                  ALU.is_equal, ALU.mult)
                dve.tensor_scalar(hot[:, o + 2 * P:o + 3 * P], iota_t[:], ends[:, 1, k:k + 1], None,
                                  ALU.is_equal).then_inc(sm("hot_ready"), 1)
            dve.wait_ge(sm("hot_used"), EC)
            link(dve.tensor_copy(w_sd[:], y[0][:, 0:P]))
            dve.tensor_copy(c_sd[:], y[0][:, P:2 * P]).then_inc(sm("c_sd"), 1)
            dve.wait_ge(sm("l0g_sim"), 1)
            link(dve.tensor_scalar(mat_b[:], ms[:, 0:P], 0.2, None, ALU.mult))
            link(dve.tensor_tensor(mat_a[:], ms[:, 0:P], mat_b[:], ALU.max))
            link(dve.reduce_max(row[:, 0, 2:3], mat_a[:], AX_X))
            dve.tensor_scalar(row[:, 0, 0:1], row[:, 0, 2:3], -1.0, None, ALU.mult).then_inc(sm("max"), 1)
            dve.wait_ge(sm("exp"), nth("exp", "l0g"))
            link(dve.reciprocal(row[:, 0, 3:4], row[:, 0, 1:2]))
            link(dve.scalar_tensor_tensor(out=mat_a[:], in0=mat_b[:], scalar=row[:, 0, 3:4], in1=w_sd[:],
                                          op0=ALU.mult, op1=ALU.mult, accum_out=row[:, 0, 4:5]))
            dve.wait_ge(sm("ab"), 1)
            link(dve.tensor_scalar(row[:, 0, 5:6], row[:, 0, 4:5], 1.0, None, ALU.add))
            link(dve.scalar_tensor_tensor(out=row[:, 0, 6:7], in0=row[:, 0, 5:6], scalar=ab[:, 0:1], in1=ab[:, 1:2],
                                          op0=ALU.mult, op1=ALU.add))
            link(dve.reciprocal(row[:, 0, 7:8], row[:, 0, 6:7]))
            link(dve.tensor_tensor(row[:, 1, 0:2], ab[:], row[:, 0, 7:8].broadcast_to([P, 2]), ALU.mult))
            link(dve.tensor_scalar(mat_b[:], ident[:], row[:, 1, 0:1], None, ALU.mult))
            dve.scalar_tensor_tensor(out=mat_a[:], in0=mat_a[:], scalar=row[:, 1, 0:1], in1=mat_b[:],
                                     op0=ALU.mult, op1=ALU.add).then_inc(sm("l0g_a"), 1)
            dve.wait_ge(sm("l0g_aT"), 1)
            dve.tensor_copy(mat_b[:], ms[:, 0:P]).then_inc(sm("l0g_aTs"), 1)
            dve.wait_ge(sm("sel_all"), 1)
            link(dve.tensor_scalar(h[:, 1], XN[:], row[:, 1, 1:2], None, ALU.mult))
            link(dve.tensor_tensor(h[:, 0], X[:], h[:, 1], ALU.add))
            for i in range(5):
                for half_ in range(2):
                    cols = slice(half_ * 256, half_ * 256 + 256)
                    dve.wait_ge(sm("l0g_sweep"), 2 * i + half_ + 1)
                    dst = X[:, cols] if i == 4 else XT[:].rearrange("p c n -> p (c n)")[:, cols]
                    dve.tensor_tensor(dst, pre[half_][:, 0:256], h[:, int(i < 4), cols], ALU.add).then_inc(
                        sm("l0g_swept"), 1)
            dve.wait_ge(sm("l0g_swept"), 10)
            layer_norm("l0f")
            dve.wait_ge(sm("c_dsT"), 1)
            link(dve.tensor_copy(c_ds[:], wt[0][:, 0:P]))
            link(dve.reduce_sum(row[:, 2, 0:1], c_ds[:], AX_X))
            link(dve.tensor_scalar(row[:, 2, 1:2], row[:, 2, 0:1], 1.0, None, ALU.max))
            link(dve.reciprocal(row[:, 2, 2:3], row[:, 2, 1:2]))
            link(dve.tensor_scalar(mat_a[:], c_ds[:], row[:, 2, 2:3], None, ALU.mult))
            dve.memset(row[:, 5, :], 1.0).then_inc(sm("agg2_rows"), 1)
            link(dve.tensor_scalar(pen[:], c_ds[:], 1.0, None, ALU.min))
            link(dve.tensor_scalar(pen[:], pen[:], -MASKED, MASKED, ALU.mult, ALU.add))
            link(dve.tensor_scalar(row[:, 2, 3:4], scal[:, 2:3], 1.0, None, ALU.add))
            dve.scalar_tensor_tensor(out=agg1[:], in0=ident[:], scalar=row[:, 2, 3:4], in1=c_ds[:], op0=ALU.mult,
                                     op1=ALU.add).then_inc(sm("c_ds"), 1)
            dve.wait_ge(sm("rwT"), 1)
            both = wt[1][:, 0:KC * 15].rearrange("p (c e) -> p c e", e=15)
            link(dve.tensor_copy(rwT[:, 0, :, 0:7], both[:, :, 0:7]))
            link(dve.tensor_copy(rwT[:, 1], both[:, :, 7:15]))
            dve.wait_ge(sm("agg2T"), 1)
            link(dve.tensor_copy(agg2[:], wt[0][:, 0:P]))

            def halve_bias(cols, raw_cols):
                hl = bias_hl[:, cols]
                link(dve.tensor_scalar(scratch[0:16, raw_cols], scratch[0:16, raw_cols], half[:, 0:1], None, ALU.mult))
                return dve.scalar_tensor_tensor(out=hl, in0=hl.bitcast(F32), scalar=half[:, 1:2],
                                                in1=scratch[0:16, raw_cols], op0=ALU.mult, op1=ALU.add)

            dve.wait_ge(sm("bias_hi"), 2)
            link(halve_bias(slice(0, 2 * D), slice(0, 2 * D)))
            halve_bias(slice(BL_COL, BL_COL + D), slice(2 * D, 3 * D)).then_inc(sm("l0_bias"), 1)
            dve.wait_ge(sm("l0_bias"), 1)
            dve.memset(row[:, 4, :], 0.0).then_inc(sm("bias_free"), 1)
            split_chunk(0)
            split_chunk(1)
            low_x("l0f")

            def route_l0():
                logits_in("l0f", E8)
                negative_max("l0f", E8)
                softmax_top("l0f", E8, 2)
            pipeline(L0F, route_l0, 1, True)
            layer_norm("l1g")
            low_x("l1g")
            split_chunk(G_L1G + 2)
            low_turned("l1g_hThi", tp, hT_hi[:, 0], hT_lo[:, 0], "l1g_hTlo")
            dve.wait_ge(sm("affine_l1"), 32)
            link(dve.tensor_tensor(X[:], X[:], affine[:, 1], ALU.add))
            dve.wait_ge(sm("bias_hi"), 3)
            halve_bias(slice(0, BL_COL), slice(0, BL_COL)).then_inc(sm("l2_bias"), 1)
            split_chunk(G_L1G + 3)
            dve.wait_ge(chunk_done, G_L1G + 2)
            statistics("l1g_out", pre[1][:])
            link(normalise("l1g_out", XN[:], pre[1][:]))
            link(dve.tensor_tensor(XN[:], XN[:], affine[:, 0], ALU.mult))
            link(dve.tensor_tensor(X[:], X[:], XN[:], ALU.add))
            layer_norm("l1f")
            low_x("l1f")
            dve.wait_ge(sm("rbias_in"), 48)
            link(logits_in("l1f", E8, 0))
            top(row[:, 0, 0:E8], E8, 1, row[:, 5, 0:E8], gates[:, 0:E8]).then_inc(sm("gates"), 1)
            dve.wait_ge(sm("gates"), nth("gates", "l1f"))
            dve.wait_ge(sm("l1f_pre"), 1)
            dve.scalar_tensor_tensor(out=h[:, 0, 0:256].rearrange("p (e n) -> p e n", n=H1),
                                     in0=pre[0][:, 0:256].rearrange("p (e n) -> p e n", n=H1), scalar=0.0,
                                     in1=gates[:, 0:E8].unsqueeze(2).broadcast_to([P, E8, H1]), op0=ALU.max,
                                     op1=ALU.mult).then_inc(sm("l1f_h"), 1)
            copy_gates("l1f")
            dve.wait_ge(sm("l1f_y"), 1)
            dve.tensor_tensor(X[:], X[:], y[0][:], ALU.add).then_inc(sm("l1f_done"), 1)
            dve.wait_ge(sm("l1f_done"), 1)
            layer_norm("l2g")
            low_x("l2g")
            low_turned("l2g_xagghi", y[0], aggT_hi[:, 0], aggT_lo[:, 0], "l2g_xagglo")
            link(logits_in("l2g", E4, 1))
            negative_max("l2g", E4)
            softmax_top("l2g", E4, 2)
            g = G_L2G
            for s in range(E4 + 2):
                if s < E4:
                    split_chunk(g + AHEAD)
                    split_chunk(g + 1 + AHEAD)
                    g += 2
                if s >= 2:
                    split_chunk(g + AHEAD)
                    split_chunk(g + 1 + AHEAD)
                    dve.wait_ge(sm("l2g_out"), s - 1)
                    if s >= 3:
                        dve.wait_ge(sm("l2g_summed"), s - 2)
                    dve.tensor_tensor(X[:], X[:], scratch[:, (s % 2) * D:(s % 2 + 1) * D], ALU.add).then_inc(
                        sm("l2g_summed"), 1)
                    g += 2
                if 1 <= s <= E4:
                    dve.wait_ge(sm("l2g_hi"), 2 * s)
                    dve.tensor_tensor(hT_lo[:, 0], chunks4(tp), hT_hi[:, 0].bitcast(F32), ALU.subtract).then_inc(
                        sm("l2g_lo"), 1)
                    dve.tensor_tensor(aggT_lo[:, 1], chunks4(wt[0]), aggT_hi[:, 1].bitcast(F32),
                                      ALU.subtract).then_inc(sm("l2g_lo"), 1)
            dve.wait_ge(sm("l2g_summed"), E4)
            layer_norm("l2f")
            low_x("l2f")

            def route_tree():
                logits_in("l2f", 7, 2).then_inc(sm("l2f_tree"), 1)
                dve.wait_ge(sm("l2f_p"), 1)
                p, q = row[:, 1, 0:7], row[:, 2, 0:7]
                link(dve.tensor_scalar(q, p, -1.0, 1.0, ALU.mult, ALU.add))
                link(dve.tensor_copy(row[:, 3, 0:1], q[:, 0:1]))
                link(dve.tensor_copy(row[:, 3, 1:2], p[:, 0:1]))
                for n_, (a, b) in ((2, (3, 4)), (4, (4, None))):
                    leaf = row[:, a, 0:n_]
                    nxt = (gates[:, 0:2 * n_] if b is None else row[:, b, 0:2 * n_]).rearrange("p (n b) -> p n b", b=2)
                    link(dve.tensor_tensor(nxt[:, :, 0], leaf, q[:, n_ - 1:2 * n_ - 1], ALU.mult))
                    last = dve.tensor_tensor(nxt[:, :, 1], leaf, p[:, n_ - 1:2 * n_ - 1], ALU.mult)
                    if b is None:
                        last.then_inc(sm("gates"), 1)
                    else:
                        link(last)
            pipeline(L2F, route_tree, 2, True)
            layer_norm("l3g")
            low_x("l3g")
            split_chunk(G_L3G + 2)
            dve.wait_ge(chunk_done, G_L3G + 2)
            dve.tensor_copy(h[:, 1], pre[1][:]).then_inc(sm("l3g_k"), 1)
            split_chunk(G_L3G + 3)
            dve.wait_ge(sm("l3g_kT"), 1)
            dve.tensor_copy(scratch[:, 3 * D:4 * D], y[1][:]).then_inc(sm("l3g_kTs"), 1)
            split_chunk(G_L3G + 4)
            dve.wait_ge(sm("l3g_scores"), 1)
            S = scratch[:, 0:2 * D].rearrange("p (i n) -> p i n", n=P)
            for p in range(2):
                link(dve.scalar_tensor_tensor(out=S[:, 4 * p:4 * p + 4], in0=chunks4(pre[p]), scalar=DK ** -0.5,
                                              in1=pen[:].unsqueeze(1).broadcast_to([P, 4, P]), op0=ALU.mult,
                                              op1=ALU.add))
            link(dve.reduce_max(row[:, 0, :], S, AX_X))
            dve.tensor_tensor(S, S, row[:, 0, :].unsqueeze(2).broadcast_to([P, HEADS, P]), ALU.subtract).then_inc(
                sm("l3g_centred"), 1)
            dve.wait_ge(sm("exp"), nth("exp", "l3g"))
            dve.tensor_tensor(S, S, c_ds[:].unsqueeze(1).broadcast_to([P, HEADS, P]), ALU.mult).then_inc(sm("l3g_p"), 1)
            dve.wait_ge(sm("l3g_p"), 1)
            link(dve.reduce_sum(row[:, 1, :], S, AX_X))
            dve.wait_ge(sm("l3g_pT"), 1)
            dve.tensor_copy(side[:, 2:4].rearrange("p c n -> p (c n)"), y[1][:]).then_inc(sm("l3g_pTs1"), 1)
            link(dve.tensor_scalar(row[:, 2, :], row[:, 1, :], 1e-30, None, ALU.max))
            link(dve.reciprocal(row[:, 3, :], row[:, 2, :]))
            dve.wait_ge(sm("l3g_av"), 1)
            dve.tensor_tensor(h[:, 0].rearrange("t (j p d) -> t p j d", p=2, d=DK),
                              pre[0][:].rearrange("t (j p d) -> t p j d", p=2, d=DK),
                              row[:, 3, :].rearrange("t (p j) -> t p j", p=2).unsqueeze(3).broadcast_to(
                                  [P, 2, 4, DK]), ALU.mult).then_inc(sm("l3g_a"), 1)
            low_turned("l3g_aThi", tp, hT_hi[:, 0], hT_lo[:, 0], "l3g_aTlo")
            split_chunk(G_L3G + 5)
            dve.wait_ge(chunk_done, G_L3G + 4)
            link(dve.tensor_tensor(h[:, 1], XN[:], pre[1][:], ALU.add))
            statistics("l3g_mid", h[:, 1])
            link(normalise("l3g_mid", h[:, 1], h[:, 1]))
            dve.wait_ge(sm("affine_l3"), 64)
            link(dve.tensor_tensor(h[:, 1], h[:, 1], affine[:, 0], ALU.mult))
            dve.tensor_tensor(h[:, 1], h[:, 1], affine[:, 1], ALU.add).then_inc(sm("l3g_mid"), 1)
            link(dve.tensor_tensor(X[:], X[:], affine[:, 3], ALU.add))
            dve.wait_ge(sm("l3g_mid"), 1)
            dve.wait_ge(sm("l3g_f2"), 1)
            link(dve.tensor_tensor(h[:, 1], h[:, 1], y[0][:], ALU.add))
            statistics("l3g_out", h[:, 1])
            link(normalise("l3g_out", h[:, 1], h[:, 1]))
            link(dve.tensor_tensor(h[:, 1], h[:, 1], affine[:, 2], ALU.mult))
            link(dve.tensor_tensor(X[:], X[:], h[:, 1], ALU.add))
            layer_norm("l3f")
            low_x("l3f")

            def route_l3():
                logits_in("l3f", E8)
                negative_max("l3f", E8)
                dve.wait_ge(sm("exp"), nth("exp", "l3f"))
                link(top(row[:, 0, 0:E8], E8, 2, row[:, 1, 0:E8], row[:, 2, 0:E8]))
                link(dve.reduce_sum(row[:, 7, 3:4], row[:, 2, 0:E8], AX_X))
                link(dve.reciprocal(row[:, 7, 4:5], row[:, 7, 3:4]))
                link(dve.memset(gates[:, 0:1], 1.0))
                link(dve.tensor_scalar(gates[:, 1:1 + E8], row[:, 2, 0:E8], row[:, 7, 4:5], None, ALU.mult))
            pipeline(L3F, route_l3, 1, False)


_INS = ["x", "src", "dst", "edge_weight", "L0_gnn_emb_1", "L0_gnn_emb_2", "L0_gnn_alpha_p", "L0_gnn_beta_p",
        "L0_ffn_Wg", "L0_ffn_W1", "L0_ffn_b1", "L0_ffn_W2", "L0_ffn_b2", "L1_gnn_eps", "L1_gnn_W1", "L1_gnn_b1",
        "L1_gnn_W2", "L1_gnn_b2", "L1_gnn_gamma", "L1_gnn_beta", "L1_ffn_Wr", "L1_ffn_br", "L1_ffn_W1", "L1_ffn_b1",
        "L1_ffn_W2", "L1_ffn_b2", "L2_gnn_gate_W", "L2_gnn_gate_b", "L2_gnn_Wl", "L2_gnn_bl", "L2_gnn_Wr",
        "L2_ffn_rw", "L2_ffn_rb", "L2_ffn_w1", "L2_ffn_b1", "L2_ffn_w2", "L2_ffn_b2", "L3_gnn_Wq", "L3_gnn_Wk",
        "L3_gnn_Wv", "L3_gnn_Wo", "L3_gnn_ln1_g", "L3_gnn_ln1_b", "L3_gnn_ln2_g", "L3_gnn_ln2_b", "L3_gnn_W1",
        "L3_gnn_b1", "L3_gnn_W2", "L3_gnn_b2", "L3_ffn_gate_w", "L3_ffn_w1", "L3_ffn_w2", "L3_ffn_sg_gate",
        "L3_ffn_sg_up", "L3_ffn_sg_down"]


def kernel(**inputs):
    import numpy as np
    import concourse.bacc as bacc
    from concourse.bass_utils import run_bass_kernel_spmd

    nc = bacc.Bacc("TRN2", target_bir_lowering=False, num_devices=1)
    arrays, handles = {}, {}
    for name in _INS:
        a = np.ascontiguousarray(inputs[name])
        arrays["in_" + name] = a
        handles[name] = nc.dram_tensor("in_" + name, a.shape, mybir.dt.from_np(a.dtype), kind="ExternalInput").ap()
    out = nc.dram_tensor("out_x", (P, D), F32, kind="ExternalOutput").ap()
    gnn_ffn_kernel(nc, handles, out)
    result = run_bass_kernel_spmd(nc, [arrays], core_ids=[0])
    return result.results[0]["out_x"]
```

```python
from contextlib import ExitStack

import concourse.bass as bass
from concourse import mybir

P = 128
D = 512
KC = D // P
NE = 2048
EC = NE // P
RAW_SLOTS = 8
SPLIT_SLOTS = 4
HOTS = 5
SIM_AT = 10
AHEAD = 2
E8 = 8
E4 = 4
HEADS = 8
DK = D // HEADS
H1 = 32
LN_EPS = 1e-5
MASKED = -1e30

F32 = mybir.dt.float32
F32R = mybir.dt.float32r
I32 = mybir.dt.int32
ALU = mybir.AluOpType
ACT = mybir.ActivationFunctionType
AX_X = mybir.AxisListType.X

G_L0F = 0
G_L1G = G_L0F + 32
G_L2G = G_L1G + 2
G_L2F = G_L2G + 16
G_L3G = G_L2F + 64
G_L3F = G_L3G + 4
CHUNKS = G_L3F + 38


class Pipe:

    def __init__(self, tag, g0, n, per_expert, turned, summed, act, lead=0, selected=None):
        self.tag, self.g0, self.n, self.U = tag, g0, n, per_expert
        self.turned = turned
        self.summed = summed
        self.act, self.lead = act, lead
        self.selected = selected

    def chunk(self, s):
        if self.lead:
            return self.g0 + 2 * s if s <= self.n else self.g0 + 2 * self.n + (s - self.n)
        if s < 2:
            return self.g0 + s
        return self.g0 + 2 * (s - 1) if s <= self.n else self.g0 + 2 * self.n - 1

    def loops(self):
        return (self.n - 4) // 4


L0F = Pipe("l0f", G_L0F, 16, 2, 0, 1, ACT.Gelu_apprx_tanh, selected=0)
L2F = Pipe("l2f", G_L2F, 32, 4, 16, 1 + 8 + 1, ACT.Gelu, selected=8)
L3F = Pipe("l3f", G_L3F, 18, 2, 16 + 32, 1 + 8 + 1 + 16, ACT.Silu, lead=2)
BL_COL = 2048


def transposed(g):
    return G_L1G <= g < G_L2G or g >= G_L3F


def turned_quarters(g):
    return 4 * (g - G_L1G) if g < G_L2G else 4 * (G_L2G - G_L1G + g - G_L3F)


NORMED = ["l0g", "l0f", "l1g", "l1g_out", "l1f", "l2g", "l2f", "l3g", "l3g_mid", "l3g_out", "l3f"]
LAYERS = [t for t in NORMED if "_" not in t]
STAGES = {
    "var": NORMED, "rstd": NORMED,
    "xn": LAYERS, "xt": LAYERS,
    "xhi": LAYERS[1:], "xlo": LAYERS[1:],
    "xt32": [t for t in LAYERS if t not in ("l1g", "l3g")],
    "logits": ["l0f", "l1f", "l2g", "l2f", "l3f"],
    "max": ["l0g", "l0f", "l2g", "l3f"], "exp": ["l0g", "l0f", "l2g", "l3g", "l3f"],
    "gates": ["l0f", "l1f", "l2g", "l2f"],
    "gT": ["l0f", "l1f", "l2f"], "gTs": ["l0f", "l1f", "l2f"],
    "seed": ["l0f", "l2f"],
}


def nth(stage, tag):
    return STAGES[stage].index(tag) + 1


def at(count, per, it):
    return count if it is None else count + per * it


def gnn_ffn_kernel(nc, A, out):
    with ExitStack() as ctx:
        def sb(name, shape, dt=F32):
            return ctx.enter_context(nc.sbuf_tensor(name, shape, dt))

        def bank(name):
            return ctx.enter_context(nc.psum_tensor(name, [P, D], F32))

        named = {}

        def sm(name):
            if name not in named:
                named[name] = ctx.enter_context(nc.semaphore("s_" + name))
            return named[name]

        raw = sb("raw", [P, RAW_SLOTS, KC, D])
        w_hi = sb("w_hi", [P, SPLIT_SLOTS, KC, D], F32R)
        w_lo = sb("w_lo", [P, SPLIT_SLOTS, KC, D], F32R)
        X = sb("X", [P, D])
        XN = sb("XN", [P, D])
        XT = sb("XT", [P, KC, P])
        x_hi = sb("x_hi", [P, KC, P], F32R)
        x_lo = sb("x_lo", [P, KC, P], F32R)
        h = sb("h", [P, 2, D])
        hT_hi = sb("hT_hi", [P, 2, KC, P], F32R)
        hT_lo = sb("hT_lo", [P, 2, KC, P], F32R)
        aggT_hi = sb("aggT_hi", [P, 2, KC, P], F32R)
        aggT_lo = sb("aggT_lo", [P, 2, KC, P], F32R)
        bias_hl = sb("bias_hl", [16, BL_COL + D], F32R)
        scratch = sb("scratch", [P, 4 * D])
        affine = sb("affine", [P, 4, D])
        side = sb("side", [P, KC, 256])
        b2 = sb("b2", [33, D])
        brow = sb("brow", [65, D])
        ones = sb("ones", [65, P])
        sel_all = sb("sel_all", [16, E8, P], F32R)
        sel = sb("sel", [16, 2, P], F32R)
        iota_t = sb("iota_t", [P, P])
        ident = sb("ident", [P, P])
        c_sd = sb("c_sd", [P, P])
        c_ds = sb("c_ds", [P, P])
        agg1 = sb("agg1", [P, P])
        agg2 = sb("agg2", [P, P])
        pen = sb("pen", [P, P])
        mat_a = sb("mat_a", [P, P])
        mat_b = sb("mat_b", [P, P])
        tri = sb("tri", [P, E8, E8])
        ends_i = sb("ends_i", [P, 2, EC], I32)
        ends = sb("ends", [P, 3, EC])
        wg0 = sb("wg0", [P, KC, E8])
        wr1 = sb("wr1", [P, KC, E8])
        wg2 = sb("wg2", [P, KC, E4])
        rw_n = sb("rw_n", [15, D])
        rwT = sb("rwT", [P, 2, KC, E8])
        rbias = sb("rbias", [P, 3, E8])
        l3w1 = sb("l3w1", [P, KC, 32])
        l3b1 = sb("l3b1", [32, 1])
        fT = sb("fT", [33, P])
        scal = sb("scal", [P, 3])
        ab = sb("ab", [P, 2])
        gates = sb("gates", [P, 16])
        gT = sb("gT", [E8, P])
        row = sb("row", [P, 8, E8])
        st = sb("st", [P, 6])
        mv = sb("mv", [P, 2])
        rstd = sb("rstd", [P, 2])
        mhalf = sb("mhalf", [P, 1])
        half = sb("half", [16, 2])
        hot = raw[:, RAW_SLOTS - 1].rearrange("p c n -> p (c n)")
        sel_raw = h[0:16, :, :].rearrange("p b n -> p (b n)")

        cmp = mat_b[:].rearrange("p (a n) -> p a n", a=2)

        pre = [bank("pre0"), bank("pre1")]
        tp = bank("tp")
        y = [bank("y0"), bank("y1")]
        wt = [bank("wt0"), bank("wt1")]
        ms = bank("ms")

        landed = [sm(f"landed{i}") for i in range(RAW_SLOTS)]
        w_hi_ready = sm("w_hi_ready")
        w_lo_ready = sm("w_lo_ready")
        w_turned = sm("w_turned")
        chunk_done = sm("chunk_done")
        h_ready = sm("h_ready")
        h_turned = sm("h_turned")
        hT_hi_ready = sm("hT_hi_ready")
        hT_lo_ready = sm("hT_lo_ready")
        y_summed = sm("y_summed")
        sel_ready = sm("sel_ready")
        dve_link = sm("dve_link")

        block = ctx.enter_context(nc.Block())

        def w1_unit(w, U, u, it):
            wv = w.rearrange("e (c p) n -> e p c n", p=P)
            return wv[at(u // U, 4 // U, it)][:, :, (u % U) * D:(u % U + 1) * D]

        def w2_unit(w, U, u, it):
            wv = w.rearrange("e (k c p) n -> e p k c n", c=KC, p=P)
            return wv[at(u // U, 4 // U, it)][:, u % U]

        @block.sync
        def _(sp):
            sp.dma_start(X[:], A["x"]).then_inc(sm("x_in"), 16)
            for n, name in ((0, "src"), (1, "dst")):
                sp.dma_start(ends_i[:, n], A[name].rearrange("(p k) -> p k", p=P)).then_inc(sm("edges_in"), 16)
            sp.dma_start(ends[:, 2], A["edge_weight"].rearrange("(p k) -> p k", p=P)).then_inc(sm("edges_in"), 16)

            def small(dst, src, sem):
                sp.dma_start(dst, src).then_inc(sm(sem), 16)

            def early_loads(g):
                if g == 3:
                    for top in (0, E8):
                        small(scratch[top:top + E8, 0:2 * D], A["L0_ffn_b1"], "bias_in")
                        small(scratch[top:top + E8, 2 * D:3 * D], A["L2_gnn_bl"].rearrange("e l n -> (e l) n"), "bias_in")
                    small(wg0[:], A["L0_ffn_Wg"].rearrange("(c p) n -> p c n", p=P), "wg0_in")
                if g == 5:
                    small(b2[0:E8, :], A["L0_ffn_b2"], "b2_l0")
                    small(rw_n[0:7, :], A["L2_ffn_rw"], "rw_in")
                    small(rw_n[7:15, :], A["L3_ffn_gate_w"], "rw_in")
                if g == RAW_SLOTS - 1:
                    sp.wait_ge(sm("hot_used"), EC)
                if g == RAW_SLOTS:
                    small(wr1[:], A["L1_ffn_Wr"].rearrange("(c p) n -> p c n", p=P), "routers_in")
                    small(wg2[:], A["L2_gnn_gate_W"].rearrange("(c p) n -> p c n", p=P), "routers_in")
                    small(rbias[:, 0, :], A["L1_ffn_br"].partition_broadcast(P), "rbias_in")
                    small(rbias[:, 1, 0:E4], A["L2_gnn_gate_b"].partition_broadcast(P), "rbias_in")
                    small(rbias[:, 2, 0:7], A["L2_ffn_rb"].partition_broadcast(P), "rbias_in")
                    for i, name in enumerate(("L1_gnn_b1", "L1_gnn_b2")):
                        small(brow[32 * i:32 * i + 1, :], A[name].rearrange("(a n) -> a n", a=1), "brow_in")
                    small(brow[64:65, 0:E8 * H1], A["L1_ffn_b1"].rearrange("(a e) n -> a (e n)", a=1), "brow_in")
                    small(affine[:, 0], A["L1_gnn_gamma"].partition_broadcast(P), "affine_l1")
                    small(affine[:, 1], A["L1_gnn_beta"].partition_broadcast(P), "affine_l1")
                    small(l3w1[:], A["L3_gnn_W1"].rearrange("(c p) n -> p c n", p=P), "l3_small_in")
                    small(l3b1[:], A["L3_gnn_b1"].rearrange("(n a) -> n a", a=1), "l3_small_in")

            def load(g, source, it=None):
                if it is None and g <= RAW_SLOTS:
                    early_loads(g)
                if g >= RAW_SLOTS or it is not None:
                    sp.wait_ge(w_lo_ready, at(4 * (g - RAW_SLOTS + 1), 32, it))
                sp.dma_start(raw[:, g % RAW_SLOTS], source).then_inc(landed[g % RAW_SLOTS], 16)

            def square(w):
                return w.rearrange("(c p) n -> p c n", p=P)

            def steps(pipe, w1, w2):
                def step(s, it=None):
                    g = pipe.chunk(s)
                    if s < pipe.n:
                        if s < pipe.lead:
                            for i, w in enumerate(("L3_ffn_sg_gate", "L3_ffn_sg_up")):
                                load(g + i, square(A[w][s * D:(s + 1) * D, :]))
                            return
                        load(g, w1(s - pipe.lead, it), it)
                        g += 1
                    if s >= 2:
                        if s - 2 < pipe.lead:
                            load(g, square(A["L3_ffn_sg_down"][:, (s - 2) * D:(s - 1) * D]))
                        else:
                            load(g, w2(s - 2 - pipe.lead, it), it)
                peeled = 8 if pipe.g0 == 0 else 4
                for s in range(peeled):
                    step(s)
                with sp.Fori(0, pipe.loops() - (peeled - 4) // 4) as it:
                    for s in range(peeled, peeled + 4):
                        step(s, it)
                for s in range(4 + 4 * pipe.loops(), pipe.n + 2):
                    step(s)

            steps(L0F, lambda u, it: w1_unit(A["L0_ffn_W1"], 2, u, it),
                  lambda u, it: w2_unit(A["L0_ffn_W2"], 2, u, it))
            load(G_L1G, square(A["L1_gnn_W1"]))
            load(G_L1G + 1, square(A["L1_gnn_W2"]))
            g = G_L2G
            for s in range(E4 + 2):
                for e, layer in ((s, 0), (s - 2, 1)):
                    if 0 <= e < E4:
                        load(g, square(A["L2_gnn_Wr"][e, layer]))
                        load(g + 1, square(A["L2_gnn_Wl"][e, layer]))
                        g += 2
            steps(L2F, lambda u, it: w1_unit(A["L2_ffn_w1"], 4, u, it),
                  lambda u, it: w2_unit(A["L2_ffn_w2"], 4, u, it))
            for i, name in enumerate(("L3_gnn_Wq", "L3_gnn_Wk", "L3_gnn_Wv", "L3_gnn_Wo")):
                load(G_L3G + i, square(A[name]))
            steps(L3F, lambda u, it: w2_unit(A["L3_ffn_w1"], 2, u, it),
                  lambda u, it: w1_unit(A["L3_ffn_w2"], 2, u, it))
            sp.wait_ge(y_summed, L3F.summed + L3F.n // 2)
            sp.dma_start(out, X[:]).then_inc(sm("out_written"), 16)
            sp.wait_ge(sm("out_written"), 16)

        @block.gpsimd
        def _(pool):
            n = [0]

            def link(ins):
                n[0] += 1
                ins.then_inc(sm("pool_link"), 1)
                pool.wait_ge(sm("pool_link"), n[0])

            link(pool.memset(ident[:], 0.0))
            link(pool.affine_select(out=ident[:], in_=ident[:], compare_op=ALU.not_equal, fill=1.0, base=0,
                                    pattern=[[-1, P]], channel_multiplier=1))
            link(pool.memset(mhalf[:], -0.5))
            pool.iota(iota_t[:], pattern=[[1, P]], base=0, channel_multiplier=0,
                      allow_small_or_imprecise_dtypes=True).then_inc(sm("consts"), 1)

            def inv_std(tag):
                pool.wait_ge(sm("var"), nth("var", tag))
                link(pool.tensor_scalar(rstd[:, 0:1], mv[:, 1:2], LN_EPS, None, ALU.add))
                pool.tensor_tensor(rstd[:, 1:2], rstd[:, 0:1], mhalf[:], ALU.pow).then_inc(sm("rstd"), 1)

            inv_std("l0g")
            link(pool.memset(tri[:], 1.0))
            link(pool.affine_select(out=tri[:], in_=tri[:], compare_op=ALU.is_gt, fill=0.0, base=0,
                                    pattern=[[1, E8], [-1, E8]], channel_multiplier=0))
            link(pool.memset(ones[:], 1.0))
            link(pool.memset(fT[:], 1.0))
            link(pool.memset(half[:], 1.0))
            link(pool.affine_select(out=half[:, 0:1], in_=half[:, 0:1], compare_op=ALU.is_gt, fill=0.0, base=-7,
                                    pattern=[[0, 1]], channel_multiplier=1))
            link(pool.affine_select(out=half[:, 1:2], in_=half[:, 1:2], compare_op=ALU.is_gt, fill=-1.0, base=8,
                                    pattern=[[0, 1]], channel_multiplier=-1))
            link(pool.memset(sel_raw, 0.0))
            link(pool.affine_select(out=sel_raw, in_=sel_raw, compare_op=ALU.not_equal, fill=1.0, base=0,
                                    pattern=[[-1, E8], [0, P]], channel_multiplier=1))
            pool.affine_select(out=sel_raw, in_=sel_raw, compare_op=ALU.not_equal, fill=1.0, base=-E8,
                               pattern=[[-1, E8], [0, P]], channel_multiplier=1).then_inc(sm("sel_raw"), 1)

            for tag in NORMED[1:]:
                inv_std(tag)

        @block.scalar
        def _(act):
            def small(dst, src, sem):
                act.dma_start(dst, src).then_inc(sm(sem), 16)

            emb = [A[n].rearrange("(c p) n -> p c n", p=P) for n in ("L0_gnn_emb_1", "L0_gnn_emb_2")]
            small(side[:, :, 0:P], emb[0], "emb_in")
            small(side[:, :, P:2 * P], emb[1], "emb_in")
            for i, name in enumerate(("L0_gnn_alpha_p", "L0_gnn_beta_p", "L1_gnn_eps")):
                small(scal[:, i:i + 1], A[name].partition_broadcast(P), "scal_in")

            def round_chunk(g, it=None):
                if g >= CHUNKS:
                    return
                if g >= SPLIT_SLOTS or it is not None:
                    act.wait_ge(chunk_done, at(g - SPLIT_SLOTS + 1, 8, it))
                if transposed(g):
                    for q in range(4):
                        act.wait_ge(w_turned, at(turned_quarters(g) + q + 1, 32, it))
                        act.activation(w_hi[:, g % SPLIT_SLOTS, q], wt[q % 2][:], ACT.Copy).then_inc(w_hi_ready, 1)
                else:
                    act.wait_ge(landed[g % RAW_SLOTS], at(16 * (g // RAW_SLOTS + 1), 16, it))
                    act.activation(w_hi[:, g % SPLIT_SLOTS], raw[:, g % RAW_SLOTS], ACT.Copy).then_inc(w_hi_ready, 4)

            def round_x(tag, plain):
                act.wait_ge(sm("xt"), nth("xt", tag))
                act.activation(x_hi[:], tp[:].rearrange("p (c n) -> p c n", n=P), ACT.Copy).then_inc(sm("xhi"), 1)
                if plain:
                    act.wait_ge(sm("xlo"), nth("xlo", tag))
                    act.activation(XT[:], tp[:].rearrange("p (c n) -> p c n", n=P), ACT.Copy).then_inc(
                        sm("xt32"), 1)

            def round_turned(ready, bank_ap, dst, done):
                act.wait_ge(sm(ready), 1)
                act.activation(dst, bank_ap[:].rearrange("p (c n) -> p c n", n=P), ACT.Copy).then_inc(sm(done), 1)

            def pipeline(pipe, after0):
                def step(s, it=None):
                    g = pipe.chunk(s)
                    if s < pipe.n:
                        round_chunk(g + AHEAD, it)
                        if s < pipe.lead:
                            round_chunk(g + 1 + AHEAD, it)
                        g += 1
                    if 1 <= s <= pipe.n:
                        act.wait_ge(h_turned, at(pipe.turned + s, 4, it))
                        act.activation(hT_hi[:, (s - 1) % 2], tp[:].rearrange("p (c n) -> p c n", n=P),
                                       ACT.Copy).then_inc(hT_hi_ready, 1)
                    if s < pipe.lead:
                        act.wait_ge(chunk_done, pipe.chunk(s) + 2)
                        act.activation(h[:, s % 2], pre[s % 2][:], pipe.act).then_inc(sm("gate_ready"), 1)
                    elif s < pipe.n:
                        act.wait_ge(chunk_done, at(pipe.chunk(s) + 1, 8, it))
                        act.activation(h[:, s % 2], pre[s % 2][:], pipe.act).then_inc(h_ready, 1)
                    if s == 0:
                        after0()
                    if s >= 2:
                        round_chunk(g + AHEAD, it)
                for s in range(4):
                    step(s)
                with act.Fori(0, pipe.loops()) as it:
                    for s in range(4, 8):
                        step(s, it)
                for s in range(4 + 4 * pipe.loops(), pipe.n + 2):
                    step(s)

            def exp_logits(tag, E):
                act.wait_ge(sm("max"), nth("max", tag))
                act.activation(row[:, 1, 0:E], row[:, 0, 0:E], ACT.Exp, bias=row[:, 7, 0:1],
                               accum_out=row[:, 7, 1:2]).then_inc(sm("exp"), 1)

            def halve_bias(cols, raw_cols):
                act.activation(bias_hl[:, cols], scratch[0:16, raw_cols], ACT.Copy).then_inc(sm("bias_hi"), 1)
                act.activation(scratch[0:16, raw_cols], scratch[0:16, raw_cols], ACT.Copy,
                               scale=half[:, 0:1]).then_inc(sm("bias_hi"), 1)

            act.wait_ge(sm("xt"), nth("xt", "l0g"))
            act.activation(XT[:], tp[:].rearrange("p (c n) -> p c n", n=P), ACT.Copy).then_inc(sm("xt32"), 1)
            act.wait_ge(sm("scal_in"), 48)
            act.activation(ab[:], scal[:, 0:2], ACT.Exp).then_inc(sm("ab"), 1)
            act.wait_ge(sm("sel_raw"), 1)
            act.activation(sel_all[:].rearrange("p e n -> p (e n)"), sel_raw, ACT.Copy).then_inc(sm("sel_all"), 1)
            act.wait_ge(sm("sel_all"), 1)
            act.wait_ge(sm("l0g_x12"), 1)
            act.activation(h[:, 0, 0:2 * P], pre[0][:, 0:2 * P], ACT.Copy).then_inc(sm("l0g_x12s"), 1)
            act.wait_ge(sm("max"), nth("max", "l0g"))
            act.activation(mat_b[:], mat_a[:], ACT.Exp, bias=row[:, 0, 0:1],
                           accum_out=row[:, 0, 1:2]).then_inc(sm("exp"), 1)
            for c in range(KC):
                small(side[:, c].rearrange("p (e n) -> p e n", n=H1),
                      A["L1_ffn_W1"][:, c * P:(c + 1) * P, :].rearrange("e p n -> p e n"), "l1f_w1")
            round_chunk(0)
            round_chunk(1)
            act.wait_ge(sm("bias_in"), 64)
            halve_bias(slice(0, 2 * D), slice(0, 2 * D))
            halve_bias(slice(BL_COL, BL_COL + D), slice(2 * D, 3 * D))
            round_x("l0f", True)
            pipeline(L0F, lambda: exp_logits("l0f", E8))
            act.wait_ge(sm("l0_bias"), 1)
            for top in (0, E8):
                small(scratch[top:top + E8, :], A["L2_ffn_b1"], "bias_in")
            small(b2[0:E8, :], A["L1_ffn_b2"], "b2_l1")
            round_x("l1g", False)
            act.wait_ge(chunk_done, G_L1G + 1)
            act.activation(h[:, 0], pre[0][:], ACT.Relu).then_inc(sm("l1g_h"), 1)
            round_chunk(G_L1G + 2)
            round_turned("l1g_hT", tp, hT_hi[:, 0], "l1g_hThi")
            act.wait_ge(sm("bias_in"), 96)
            halve_bias(slice(0, BL_COL), slice(0, BL_COL))
            round_chunk(G_L1G + 3)
            act.wait_ge(sm("l2_bias"), 1)
            small(scratch[:, 0:2 * D].rearrange("p (c n) -> p c n", n=D),
                  A["L1_ffn_W2"].rearrange("(c a) b n -> (a b) c n", a=4), "l1f_w2")
            round_x("l1f", True)
            act.wait_ge(sm("l1f_hT"), 1)
            act.activation(h[:, 1, 0:2 * P], tp[:, 0:2 * P], ACT.Copy).then_inc(sm("l1f_hTs"), 1)
            small_done = sm("l1f_done")
            act.wait_ge(small_done, 1)
            small(b2[0:E8, :], A["L2_ffn_b2"], "b2_l2")
            for i, name in enumerate(("L3_gnn_ln1_g", "L3_gnn_ln1_b", "L3_gnn_ln2_g", "L3_gnn_ln2_b")):
                small(affine[:, i], A[name].partition_broadcast(P), "affine_l3")
            round_x("l2g", True)
            round_turned("l2g_xagg", y[0], aggT_hi[:, 0], "l2g_xagghi")
            exp_logits("l2g", E4)
            g = G_L2G
            for s in range(E4 + 2):
                if s < E4:
                    round_chunk(g + AHEAD)
                    round_chunk(g + 1 + AHEAD)
                    act.wait_ge(chunk_done, g + 2)
                    act.activation(h[:, s % 2], pre[s % 2][:], ACT.Relu).then_inc(sm("l2g_h"), 1)
                    g += 2
                if s >= 2:
                    round_chunk(g + AHEAD)
                    round_chunk(g + 1 + AHEAD)
                    act.wait_ge(sm("gates"), nth("gates", "l2g"))
                    act.wait_ge(chunk_done, g + 2)
                    if s >= 4:
                        act.wait_ge(sm("l2g_summed"), s - 3)
                    act.activation(scratch[:, (s % 2) * D:(s % 2 + 1) * D], y[s % 2][:], ACT.Relu,
                                   scale=gates[:, s - 2:s - 1]).then_inc(sm("l2g_out"), 1)
                    g += 2
                if 1 <= s <= E4:
                    act.wait_ge(sm("l2g_turned"), s)
                    act.activation(hT_hi[:, 0], tp[:].rearrange("p (c n) -> p c n", n=P), ACT.Copy).then_inc(
                        sm("l2g_hi"), 1)
                    act.activation(aggT_hi[:, 1], wt[0][:].rearrange("p (c n) -> p c n", n=P), ACT.Copy).then_inc(
                        sm("l2g_hi"), 1)
            def leaf_sigmoid():
                act.wait_ge(sm("l2f_tree"), 1)
                act.activation(row[:, 1, 0:7], row[:, 0, 0:7], ACT.Sigmoid).then_inc(sm("l2f_p"), 1)
            round_x("l2f", True)
            pipeline(L2F, leaf_sigmoid)
            small(b2[0:32, :], A["L3_gnn_W2"], "l3_small_in")
            small(b2[32:33, :], A["L3_gnn_b2"].rearrange("(a n) -> a n", a=1), "l3_small_in")
            round_x("l3g", False)
            round_chunk(G_L3G + 2)
            act.wait_ge(chunk_done, G_L3G + 1)
            act.activation(h[:, 0], pre[0][:], ACT.Copy).then_inc(sm("l3g_q"), 1)
            round_chunk(G_L3G + 3)
            act.wait_ge(sm("l3g_qT"), 1)
            act.activation(scratch[:, 2 * D:3 * D], tp[:], ACT.Copy).then_inc(sm("l3g_qTs"), 1)
            round_chunk(G_L3G + 4)
            act.wait_ge(chunk_done, G_L3G + 3)
            act.activation(XT[:].rearrange("p c n -> p (c n)"), y[0][:], ACT.Copy).then_inc(sm("l3g_v"), 1)
            act.wait_ge(sm("l3g_centred"), 1)
            act.activation(scratch[:, 0:2 * D], scratch[:, 0:2 * D], ACT.Exp).then_inc(sm("exp"), 1)
            act.wait_ge(sm("l3g_pT"), 1)
            act.activation(side[:, 0:2].rearrange("p c n -> p (c n)"), tp[:], ACT.Copy).then_inc(sm("l3g_pTs0"), 1)
            round_turned("l3g_aT", tp, hT_hi[:, 0], "l3g_aThi")
            round_chunk(G_L3G + 5)
            act.wait_ge(sm("l3g_midT"), 1)
            act.activation(XT[:], tp[:].rearrange("p (c n) -> p c n", n=P), ACT.Copy).then_inc(sm("l3g_midTs"), 1)
            act.wait_ge(sm("l3g_f1"), 1)
            act.activation(fT[0:32, :], ms[0:32, 0:P], ACT.Relu, bias=l3b1[:, 0:1]).then_inc(sm("l3g_f1s"), 1)
            round_x("l3f", True)
            pipeline(L3F, lambda: exp_logits("l3f", E8))

        @block.tensor
        def _(pe):
            def turn_weights(g, q, it=None):
                if q == 0:
                    pe.wait_ge(landed[g % RAW_SLOTS], at(16 * (g // RAW_SLOTS + 1), 16, it))
                pe.wait_ge(w_lo_ready, at(4 * g + q - 1, 32, it))
                for c in range(KC):
                    last = pe.transpose(wt[q % 2][:, c * P:(c + 1) * P], raw[:, g % RAW_SLOTS, c, q * P:(q + 1) * P],
                                        ident[:])
                last.then_inc(w_turned, 1)

            def product(g, dst, xs_hi, xs_lo, start, stop, it=None, bias=None, low=None):
                hi, lo = w_hi[:, g % SPLIT_SLOTS], w_lo[:, g % SPLIT_SLOTS]
                passes = [(xs_hi, hi, k) for k in range(KC)] + [(xs_hi, lo, k) for k in range(KC)] + [
                    (xs_lo, hi, k) for k in range(KC)]
                pe.wait_ge(w_hi_ready, at(4 * (g + 1), 32, it))
                for i, (xs, ws, k) in enumerate(passes):
                    if i % 3 == 0 and g + AHEAD < CHUNKS and transposed(g + AHEAD):
                        turn_weights(g + AHEAD, i // 3, it)
                    if i == KC:
                        pe.wait_ge(w_lo_ready, at(4 * (g + 1), 32, it))
                    if i == 2 * KC and low is not None:
                        pe.wait_ge(low[0], low[1])
                    last = pe.matmul(dst, xs[:, k], ws[:, k], start=start and i == 0,
                                     stop=stop and i == len(passes) - 1 and bias is None)
                if bias is not None:
                    pair, rows, halves = bias
                    pe.wait_ge(sel_ready, pair)
                    last = pe.matmul(dst, rows, halves, start=False, stop=True)
                last.then_inc(chunk_done, 1)

            def turn(dst, src, done, n=KC):
                for c in range(n):
                    last = pe.transpose(dst[:, c * P:(c + 1) * P], src[:, c * P:(c + 1) * P], ident[:])
                last.then_inc(done, 1)

            def turn_x(tag):
                pe.wait_ge(sm("xn"), nth("xn", tag))
                turn(tp, XN, sm("xt"))

            def logits(tag, w, E):
                pe.wait_ge(sm("xt32"), nth("xt32", tag))
                for c in range(KC):
                    last = pe.matmul(ms[:, 0:E], XT[:, c], w[:, c, 0:E], start=c == 0, stop=c == KC - 1)
                last.then_inc(sm("logits"), 1)

            def turn_gates(tag, n):
                pe.wait_ge(sm("gates"), nth("gates", tag))
                pe.transpose(ms[0:n, 0:P], gates[:, 0:n], ident[:]).then_inc(sm("gT"), 1)

            def seed(tag, dst):
                pe.wait_ge(sm("gTs"), nth("gTs", tag))
                return pe.matmul(dst, gT[:], b2[0:E8, :], start=True, stop=tag != "l1f")

            def pipeline(pipe, router, seeded, between=None):
                def step(s, it=None):
                    g = pipe.chunk(s)
                    low = None
                    if s == 0:
                        pe.wait_ge(sm("xhi"), nth("xhi", pipe.tag))
                        low = (sm("xlo"), nth("xlo", pipe.tag))
                    if s < pipe.lead:
                        product(g, pre[s % 2][:], x_hi, x_lo, True, True, low=low)
                        product(g + 1, y[s % 2][:], x_hi, x_lo, True, True)
                    elif s < pipe.n:
                        bias = None
                        if pipe.selected is not None:
                            col = (s % pipe.U) * D
                            if s == 0:
                                pe.wait_ge(sm("l0_bias" if pipe is L0F else "l2_bias"), 1)
                            bias = (at(pipe.selected + s // 2 + 1, 2, it), sel[:, (s // 2) % 2], bias_hl[:, col:col + D])
                        product(g, pre[s % 2][:], x_hi, x_lo, True, True, it, bias, low)
                        g += 1
                    if s == 0:
                        router()
                    if s == 1 and seeded:
                        turn_gates(pipe.tag, E8)
                    if 1 <= s <= pipe.n:
                        if s - 1 < pipe.lead:
                            pe.wait_ge(sm("shared_ready"), s)
                        else:
                            pe.wait_ge(h_ready, at(pipe.turned + s - pipe.lead, 4, it))
                        if pipe.turned + s - 1 > 0:
                            pe.wait_ge(hT_lo_ready, at(pipe.turned + s - 1, 4, it))
                        turn(tp, h[:, (s - 1) % 2], h_turned)
                    if s == 1 and seeded:
                        seed(pipe.tag, wt[0][:]).then_inc(sm("seed"), 1)
                    if s >= 2:
                        pe.wait_ge(hT_hi_ready, at(pipe.turned + s - 1, 4, it))
                        if s % 2 == 0 and s >= 4:
                            pe.wait_ge(y_summed, at(pipe.summed + (s - 4) // 2, 2, it))
                        product(g, y[((s - 2) // 2) % 2][:], hT_hi[:, s % 2], hT_lo[:, s % 2],
                                s % 2 == 0, s % 2 == 1, it, low=(hT_lo_ready, at(pipe.turned + s - 1, 4, it)))
                    if between is not None and it is None:
                        between(s)
                for s in range(4):
                    step(s)
                with pe.Fori(0, pipe.loops()) as it:
                    for s in range(4, 8):
                        step(s, it)
                for s in range(4 + 4 * pipe.loops(), pipe.n + 2):
                    step(s)

            pe.wait_ge(sm("consts"), 1)
            turn_x("l0g")
            pe.wait_ge(sm("xt32"), nth("xt32", "l0g"))
            pe.wait_ge(sm("emb_in"), 32)
            for i in range(2):
                for c in range(KC):
                    last = pe.matmul(pre[0][:, i * P:(i + 1) * P], side[:, c, i * P:(i + 1) * P], XT[:, c],
                                     start=c == 0, stop=c == KC - 1)
            last.then_inc(sm("l0g_x12"), 1)
            for k in range(EC):
                o = (k % HOTS) * 3 * P
                pe.wait_ge(sm("hot_ready"), k + 1)
                pe.matmul(y[0][:, 0:2 * P], hot[:, o:o + P], hot[:, o + P:o + 3 * P], start=k == 0,
                          stop=k == EC - 1).then_inc(sm("hot_used"), 1)
                if k == SIM_AT - 4:
                    pe.wait_ge(sm("l0g_x12s"), 1)
                    pe.matmul(ms[:, 0:P], h[:, 0, 0:P], h[:, 0, P:2 * P], start=True, stop=True).then_inc(
                        sm("l0g_sim"), 1)
            pe.wait_ge(sm("l0g_a"), 1)
            pe.transpose(ms[:, 0:P], mat_a[:], ident[:]).then_inc(sm("l0g_aT"), 1)
            pe.wait_ge(sm("l0g_aTs"), 1)
            for i in range(5):
                for b_ in range(2):
                    cols = slice(b_ * 256, b_ * 256 + 256)
                    if i:
                        pe.wait_ge(sm("l0g_swept"), 2 * (i - 1) + b_ + 1)
                    pe.matmul(pre[b_][:, 0:256], mat_b[:], XT[:].rearrange("p c n -> p (c n)")[:, cols] if i
                              else XN[:, cols], start=True, stop=True).then_inc(sm("l0g_sweep"), 1)
            def graph_matrices(s):
                if s == 0:
                    pe.wait_ge(sm("c_sd"), 1)
                    pe.wait_ge(sm("rw_in"), 32)
                    pe.transpose(wt[1][:, 0:P], c_sd[:], ident[:])
                    for c in range(KC):
                        last = pe.transpose(wt[1][:, P + c * 15:P + (c + 1) * 15], rw_n[:, c * P:(c + 1) * P],
                                            ident[0:15, 0:15])
                    last.then_inc(sm("c_dsT"), 1)
                if s == 2:
                    pe.wait_ge(sm("agg2_rows"), 1)
                    pe.transpose(wt[1][:, 0:P], mat_a[:], ident[:]).then_inc(sm("agg2T"), 1)

            turn_x("l0f")
            pe.wait_ge(sm("wg0_in"), 16)
            pe.wait_ge(sm("b2_l0"), 16)
            pipeline(L0F, lambda: logits("l0f", wg0, E8), True, graph_matrices)
            pe.wait_ge(sm("brow_in"), 48)
            pe.matmul(pre[0][:], ones[0:1, :], brow[0:1, :], start=True, stop=False)
            pe.matmul(pre[1][:], ones[32:33, :], brow[32:33, :], start=True, stop=False)
            pe.wait_ge(sm("c_ds"), 1)
            pe.wait_ge(sm("xn"), nth("xn", "l1g"))
            for c in range(KC):
                last = pe.matmul(tp[:, c * P:(c + 1) * P], XN[:, c * P:(c + 1) * P], agg1[:], start=True, stop=True)
            last.then_inc(sm("xt"), 1)
            pe.wait_ge(sm("xhi"), nth("xhi", "l1g"))
            product(G_L1G, pre[0][:], x_hi, x_lo, False, True, low=(sm("xlo"), nth("xlo", "l1g")))
            pe.wait_ge(sm("l1g_h"), 1)
            turn(tp, h[:, 0], sm("l1g_hT"))
            pe.wait_ge(sm("l1g_hThi"), 1)
            product(G_L1G + 1, pre[1][:], hT_hi[:, 0], hT_lo[:, 0], False, True, low=(sm("l1g_hTlo"), 1))
            pe.wait_ge(sm("routers_in"), 32)
            turn_x("l1f")
            pe.matmul(pre[0][:, 0:256], ones[64:65, :], brow[64:65, 0:256], start=True, stop=False)
            logits("l1f", wr1, E8)
            pe.wait_ge(sm("l1f_w1"), 16 * KC)
            for c in range(KC):
                last = pe.matmul(pre[0][:, 0:256], XT[:, c], side[:, c], start=False, stop=c == KC - 1)
            last.then_inc(sm("l1f_pre"), 1)
            turn_gates("l1f", E8)
            pe.wait_ge(sm("b2_l1"), 16)
            seed("l1f", y[0][:])
            pe.wait_ge(sm("l1f_h"), 1)
            turn(tp, h[:, 0], sm("l1f_hT"), 2)
            pe.wait_ge(sm("l1f_hTs"), 1)
            pe.wait_ge(sm("l1f_w2"), 16)
            for c in range(2):
                last = pe.matmul(y[0][:], h[:, 1, c * P:(c + 1) * P], scratch[:, c * D:(c + 1) * D], start=False,
                                 stop=c == 1)
            last.then_inc(sm("l1f_y"), 1)
            turn_x("l2g")
            for c in range(KC):
                last = pe.matmul(y[0][:, c * P:(c + 1) * P], XN[:, c * P:(c + 1) * P], agg2[:], start=True, stop=True)
            last.then_inc(sm("l2g_xagg"), 1)
            logits("l2g", wg2, E4)
            g = G_L2G
            pe.wait_ge(sm("xhi"), nth("xhi", "l2g"))
            for s in range(E4 + 2):
                if s < E4:
                    pe.matmul(pre[s % 2][:], sel_all[:, 2 * s], bias_hl[:, BL_COL:BL_COL + D], start=True, stop=False)
                    product(g, pre[s % 2][:], x_hi, x_lo, False, False, low=(sm("xlo"), nth("xlo", "l2g")))
                    if s == 0:
                        pe.wait_ge(sm("l2g_xagghi"), 1)
                    product(g + 1, pre[s % 2][:], aggT_hi[:, 0], aggT_lo[:, 0], False, True, low=(sm("l2g_xagglo"), 1))
                    g += 2
                if s >= 2:
                    pe.wait_ge(sm("l2g_lo"), 2 * (s - 1))
                    if s >= 4:
                        pe.wait_ge(sm("l2g_out"), s - 3)
                    pe.matmul(y[s % 2][:], sel_all[:, 2 * (s - 2) + 1], bias_hl[:, BL_COL:BL_COL + D], start=True,
                              stop=False)
                    product(g, y[s % 2][:], hT_hi[:, 0], hT_lo[:, 0], False, False)
                    product(g + 1, y[s % 2][:], aggT_hi[:, 1], aggT_lo[:, 1], False, True)
                    g += 2
                if 1 <= s <= E4:
                    pe.wait_ge(sm("l2g_h"), s)
                    hs = h[:, (s - 1) % 2]
                    for c in range(KC):
                        pe.transpose(tp[:, c * P:(c + 1) * P], hs[:, c * P:(c + 1) * P], ident[:])
                    for c in range(KC):
                        last = pe.matmul(wt[0][:, c * P:(c + 1) * P], hs[:, c * P:(c + 1) * P], agg2[:], start=True,
                                         stop=True)
                    last.then_inc(sm("l2g_turned"), 1)
            turn_x("l2f")
            pe.wait_ge(sm("b2_l2"), 16)
            pipeline(L2F, lambda: logits("l2f", rwT[:, 0], 7), True)
            turn_x("l3g")
            pe.wait_ge(sm("xhi"), nth("xhi", "l3g"))
            product(G_L3G, pre[0][:], x_hi, x_lo, True, True, low=(sm("xlo"), nth("xlo", "l3g")))
            product(G_L3G + 1, pre[1][:], x_hi, x_lo, True, True)
            pe.wait_ge(sm("l3g_q"), 1)
            turn(tp, h[:, 0], sm("l3g_qT"))
            pe.wait_ge(sm("l3g_k"), 1)
            turn(y[1], h[:, 1], sm("l3g_kT"))
            product(G_L3G + 2, y[0][:], x_hi, x_lo, True, True)
            pe.wait_ge(sm("l3g_qTs"), 1)
            pe.wait_ge(sm("l3g_kTs"), 1)
            for j in range(HEADS // 2):
                for p in range(2):
                    rows = slice(p * DK, (p + 1) * DK)
                    last = pe.matmul(pre[p][:, j * P:(j + 1) * P], scratch[rows, 2 * D + j * P:2 * D + (j + 1) * P],
                                     scratch[rows, 3 * D + j * P:3 * D + (j + 1) * P], start=True, stop=True)
            last.then_inc(sm("l3g_scores"), 1)
            pe.wait_ge(sm("l3g_p"), 1)
            for p in range(2):
                for j in range(HEADS // 2):
                    i = 4 * p + j
                    last = pe.transpose((tp, y[1])[p][:, j * P:(j + 1) * P], scratch[:, i * P:(i + 1) * P], ident[:])
            last.then_inc(sm("l3g_pT"), 1)
            pe.wait_ge(sm("l3g_v"), 1)
            pe.wait_ge(sm("l3g_pTs0"), 1)
            pe.wait_ge(sm("l3g_pTs1"), 1)
            probs_T = side[:].rearrange("p c n -> p (c n)")
            for p in range(2):
                for j in range(HEADS // 2):
                    i, hd = 4 * p + j, 2 * j + p
                    last = pe.matmul(pre[0][:, hd * DK:(hd + 1) * DK], probs_T[:, i * P:(i + 1) * P],
                                     XT[:].rearrange("p c n -> p (c n)")[:, hd * DK:(hd + 1) * DK], start=True, stop=True)
            last.then_inc(sm("l3g_av"), 1)
            pe.wait_ge(sm("l3g_a"), 1)
            turn(tp, h[:, 0], sm("l3g_aT"))
            pe.wait_ge(sm("l3g_aThi"), 1)
            product(G_L3G + 3, pre[1][:], hT_hi[:, 0], hT_lo[:, 0], True, True, low=(sm("l3g_aTlo"), 1))
            pe.wait_ge(sm("l3g_mid"), 1)
            turn(tp, h[:, 1], sm("l3g_midT"))
            pe.wait_ge(sm("l3g_midTs"), 1)
            pe.wait_ge(sm("l3_small_in"), 64)
            for c in range(KC):
                last = pe.matmul(ms[0:32, 0:P], l3w1[:, c], XT[:, c], start=c == 0, stop=c == KC - 1)
            last.then_inc(sm("l3g_f1"), 1)
            pe.wait_ge(sm("l3g_f1s"), 1)
            pe.matmul(y[0][:], fT[:], b2[:], start=True, stop=True).then_inc(sm("l3g_f2"), 1)
            turn_x("l3f")
            pipeline(L3F, lambda: logits("l3f", rwT[:, 1], E8), False)

        @block.vector
        def _(dve):
            n = [0]

            def link(ins):
                n[0] += 1
                ins.then_inc(dve_link, 1)
                dve.wait_ge(dve_link, n[0])

            def chunks4(ap):
                return ap[:].rearrange("p (c n) -> p c n", n=P)

            def statistics(tag, src):
                link(dve.bn_stats(st[:], src))
                dve.bn_aggr(mv[:], st[:]).then_inc(sm("var"), 1)

            def normalise(tag, dst, src):
                dve.wait_ge(sm("rstd"), nth("rstd", tag))
                return dve.tensor_scalar(dst, src, mv[:, 0:1], rstd[:, 1:2], ALU.subtract, ALU.mult)

            def layer_norm(tag):
                statistics(tag, X[:])
                normalise(tag, XN[:], X[:]).then_inc(sm("xn"), 1)

            def low_x(tag):
                dve.wait_ge(sm("xhi"), nth("xhi", tag))
                dve.tensor_tensor(x_lo[:], chunks4(tp), x_hi[:].bitcast(F32), ALU.subtract).then_inc(
                    sm("xlo"), 1)

            def low_turned(ready, bank_ap, hi, dst, done):
                dve.wait_ge(sm(ready), 1)
                dve.tensor_tensor(dst, chunks4(bank_ap), hi.bitcast(F32), ALU.subtract).then_inc(sm(done), 1)

            def split_quarter(g, q):
                dve.wait_ge(w_hi_ready, 4 * (g + 1))
                dve.tensor_tensor(w_lo[:, g, q], raw[:, g, q], w_hi[:, g, q].bitcast(F32),
                                  ALU.subtract).then_inc(w_lo_ready, 1)

            def split_chunk(g, it=None):
                if g >= CHUNKS:
                    return
                i = g % SPLIT_SLOTS
                if transposed(g):
                    for q in range(4):
                        dve.wait_ge(w_hi_ready, at(4 * g + q + 1, 32, it))
                        dve.tensor_tensor(w_lo[:, i, q], wt[q % 2][:], w_hi[:, i, q].bitcast(F32),
                                          ALU.subtract).then_inc(w_lo_ready, 1)
                else:
                    dve.wait_ge(w_hi_ready, at(4 * (g + 1), 32, it))
                    dve.tensor_tensor(w_lo[:, i], raw[:, g % RAW_SLOTS], w_hi[:, i].bitcast(F32),
                                      ALU.subtract).then_inc(w_lo_ready, 4)

            def top(values, E, k, src, dst):
                one, other = values.unsqueeze(1).broadcast_to([P, E, E]), values.unsqueeze(2).broadcast_to([P, E, E])
                above = cmp[:, 0, 0:E * E].rearrange("p (a b) -> p a b", b=E)
                equal = cmp[:, 1, 0:E * E].rearrange("p (a b) -> p a b", b=E)
                link(dve.tensor_tensor(above, one, other, ALU.is_gt))
                link(dve.tensor_tensor(equal, one, other, ALU.is_equal))
                link(dve.tensor_tensor(equal, equal, tri[:, 0:E, 0:E], ALU.mult))
                link(dve.tensor_tensor(above, above, equal, ALU.add))
                link(dve.reduce_sum(row[:, 6, 0:E], above, AX_X))
                return dve.scalar_tensor_tensor(out=dst, in0=row[:, 6, 0:E], scalar=float(k), in1=src,
                                                op0=ALU.is_lt, op1=ALU.mult)

            def logits_in(tag, E, bias=None):
                dve.wait_ge(sm("logits"), nth("logits", tag))
                if bias is None:
                    link(dve.tensor_copy(row[:, 0, 0:E], ms[:, 0:E]))
                else:
                    return dve.tensor_tensor(row[:, 0, 0:E], ms[:, 0:E], rbias[:, bias, 0:E], ALU.add)

            def negative_max(tag, E):
                link(dve.reduce_max(row[:, 7, 2:3], row[:, 0, 0:E], AX_X))
                dve.tensor_scalar(row[:, 7, 0:1], row[:, 7, 2:3], -1.0, None, ALU.mult).then_inc(sm("max"), 1)

            def softmax_top(tag, E, k):
                dve.wait_ge(sm("exp"), nth("exp", tag))
                link(dve.reciprocal(row[:, 7, 3:4], row[:, 7, 1:2]))
                link(dve.tensor_scalar(row[:, 2, 0:E], row[:, 1, 0:E], row[:, 7, 3:4], None, ALU.mult))
                top(row[:, 2, 0:E], E, k, row[:, 2, 0:E], gates[:, 0:E]).then_inc(sm("gates"), 1)

            def copy_gates(tag):
                dve.wait_ge(sm("gT"), nth("gT", tag))
                dve.tensor_copy(gT[:], ms[0:E8, 0:P]).then_inc(sm("gTs"), 1)

            def pipeline(pipe, router, per_gate, seeded, between=None):
                def select(q, it=None):
                    e = q // (pipe.U // 2)
                    src = sel_all[:, e] if it is None else sel_all[:].rearrange("p e n -> p (e n)")[
                        :, bass.ds((e + (4 // pipe.U) * it) * P, P)]
                    dve.tensor_scalar(sel[:, q % 2], src.bitcast(F32), 1.0, None, ALU.mult).then_inc(sel_ready, 1)

                def step(s, it=None):
                    g = pipe.chunk(s)
                    if pipe.selected is not None and s % 2 == 0 and 4 <= s < pipe.n:
                        select(s // 2, it)
                    if s < pipe.n:
                        split_chunk(g + AHEAD, it)
                        if s < pipe.lead:
                            split_chunk(g + 1 + AHEAD, it)
                        g += 1
                    if s == 0:
                        router()
                    if s == 1 and seeded:
                        copy_gates(pipe.tag)
                    if 1 <= s <= pipe.n:
                        dve.wait_ge(hT_hi_ready, at(pipe.turned + s, 4, it))
                        dve.tensor_tensor(hT_lo[:, (s - 1) % 2], chunks4(tp), hT_hi[:, (s - 1) % 2].bitcast(F32),
                                          ALU.subtract).then_inc(hT_lo_ready, 1)
                    if s < pipe.lead:
                        dve.wait_ge(sm("gate_ready"), s + 1)
                        dve.tensor_tensor(h[:, s % 2], h[:, s % 2], y[s % 2][:], ALU.mult).then_inc(sm("shared_ready"), 1)
                    if s == 1 and seeded:
                        dve.wait_ge(sm("seed"), nth("seed", pipe.tag))
                        dve.tensor_tensor(X[:], X[:], wt[0][:], ALU.add).then_inc(y_summed, 1)
                    if s % 2 == 0 and s >= 4:
                        add_pair((s - 4) // 2, it)
                    if s >= 2:
                        split_chunk(g + AHEAD, it)
                    if between is not None and it is None:
                        between(s)

                def add_pair(q, it=None):
                    last = pipe.chunk(2 * q + 3) + (1 if 2 * q + 3 < pipe.n else 0)
                    dve.wait_ge(chunk_done, at(last + 1, 8, it))
                    dve.wait_ge(y_summed, at(pipe.summed + q, 2, it)) if pipe.summed + q > 0 else None
                    col = q // per_gate
                    gate = gates[:, col:col + 1] if it is None else gates[:, bass.ds(col + (2 // per_gate) * it, 1)]
                    dve.scalar_tensor_tensor(out=X[:], in0=y[q % 2][:], scalar=gate, in1=X[:], op0=ALU.mult,
                                             op1=ALU.add).then_inc(y_summed, 1)

                if pipe.selected is not None:
                    select(0)
                    select(1)
                for s in range(4):
                    step(s)
                with dve.Fori(0, pipe.loops()) as it:
                    for s in range(4, 8):
                        step(s, it)
                for s in range(4 + 4 * pipe.loops(), pipe.n + 2):
                    step(s)
                add_pair((pipe.n - 2) // 2)
                dve.wait_ge(y_summed, pipe.summed + pipe.n // 2)

            dve.wait_ge(sm("x_in"), 16)
            layer_norm("l0g")
            dve.wait_ge(sm("edges_in"), 48)
            link(dve.tensor_copy(ends[:, 0:2], ends_i[:]))
            dve.wait_ge(sm("consts"), 1)
            for k in range(EC):
                o = (k % HOTS) * 3 * P
                if k >= HOTS:
                    dve.wait_ge(sm("hot_used"), k - HOTS + 1)
                dve.tensor_scalar(hot[:, o:o + P], iota_t[:], ends[:, 0, k:k + 1], None, ALU.is_equal)
                dve.tensor_scalar(hot[:, o + P:o + 2 * P], iota_t[:], ends[:, 1, k:k + 1], ends[:, 2, k:k + 1],
                                  ALU.is_equal, ALU.mult)
                dve.tensor_scalar(hot[:, o + 2 * P:o + 3 * P], iota_t[:], ends[:, 1, k:k + 1], None,
                                  ALU.is_equal).then_inc(sm("hot_ready"), 1)
                if k == SIM_AT:
                    dve.wait_ge(sm("l0g_sim"), 1)
                    link(dve.tensor_scalar(mat_b[:], ms[:, 0:P], 0.2, None, ALU.mult))
                    link(dve.tensor_tensor(mat_a[:], ms[:, 0:P], mat_b[:], ALU.max))
                    link(dve.reduce_max(row[:, 0, 2:3], mat_a[:], AX_X))
                    dve.tensor_scalar(row[:, 0, 0:1], row[:, 0, 2:3], -1.0, None, ALU.mult).then_inc(sm("max"), 1)
            dve.wait_ge(sm("exp"), nth("exp", "l0g"))
            link(dve.reciprocal(row[:, 0, 3:4], row[:, 0, 1:2]))
            dve.wait_ge(sm("hot_used"), EC)
            link(dve.scalar_tensor_tensor(out=mat_a[:], in0=mat_b[:], scalar=row[:, 0, 3:4], in1=y[0][:, 0:P],
                                          op0=ALU.mult, op1=ALU.mult, accum_out=row[:, 0, 4:5]))
            dve.wait_ge(sm("ab"), 1)
            link(dve.tensor_scalar(row[:, 0, 5:6], row[:, 0, 4:5], 1.0, None, ALU.add))
            link(dve.scalar_tensor_tensor(out=row[:, 0, 6:7], in0=row[:, 0, 5:6], scalar=ab[:, 0:1], in1=ab[:, 1:2],
                                          op0=ALU.mult, op1=ALU.add))
            link(dve.reciprocal(row[:, 0, 7:8], row[:, 0, 6:7]))
            link(dve.tensor_tensor(row[:, 1, 0:2], ab[:], row[:, 0, 7:8].broadcast_to([P, 2]), ALU.mult))
            link(dve.tensor_scalar(mat_b[:], ident[:], row[:, 1, 0:1], None, ALU.mult))
            dve.scalar_tensor_tensor(out=mat_a[:], in0=mat_a[:], scalar=row[:, 1, 0:1], in1=mat_b[:],
                                     op0=ALU.mult, op1=ALU.add).then_inc(sm("l0g_a"), 1)
            dve.wait_ge(sm("l0g_aT"), 1)
            dve.tensor_copy(mat_b[:], ms[:, 0:P]).then_inc(sm("l0g_aTs"), 1)
            link(dve.tensor_scalar(h[:, 1], XN[:], row[:, 1, 1:2], None, ALU.mult))
            for i in range(5):
                for b_ in range(2):
                    cols = slice(b_ * 256, b_ * 256 + 256)
                    dve.wait_ge(sm("l0g_sweep"), 2 * i + b_ + 1)
                    dst = X[:, cols] if i == 4 else XT[:].rearrange("p c n -> p (c n)")[:, cols]
                    dve.tensor_tensor(dst, pre[b_][:, 0:256], h[:, int(i < 4), cols], ALU.add).then_inc(
                        sm("l0g_swept"), 1)
                    if i == 0:
                        dve.tensor_tensor(h[:, 0, cols], X[:, cols], h[:, 1, cols], ALU.add)
                    elif i < 4:
                        split_quarter(((i - 1) * 2 + b_) // 4, ((i - 1) * 2 + b_) % 4)
            dve.wait_ge(sm("l0g_swept"), 10)
            layer_norm("l0f")
            dve.tensor_copy(c_sd[:], y[0][:, P:2 * P]).then_inc(sm("c_sd"), 1)
            split_quarter(1, 2)
            split_quarter(1, 3)

            def halve_bias(cols, raw_cols):
                hl = bias_hl[:, cols]
                return dve.scalar_tensor_tensor(out=hl, in0=hl.bitcast(F32), scalar=half[:, 1:2],
                                                in1=scratch[0:16, raw_cols], op0=ALU.mult, op1=ALU.add)

            def graph_matrices(s):
                if s == 0:
                    dve.wait_ge(sm("c_dsT"), 1)
                    link(dve.tensor_copy(c_ds[:], wt[1][:, 0:P]))
                    both = wt[1][:, P:P + KC * 15].rearrange("p (c e) -> p c e", e=15)
                    link(dve.tensor_copy(rwT[:, 0, :, 0:7], both[:, :, 0:7]))
                    link(dve.tensor_copy(rwT[:, 1], both[:, :, 7:15]))
                    link(dve.reduce_sum(row[:, 3, 0:1], c_ds[:], AX_X))
                    link(dve.tensor_scalar(row[:, 3, 1:2], row[:, 3, 0:1], 1.0, None, ALU.max))
                    link(dve.reciprocal(row[:, 3, 2:3], row[:, 3, 1:2]))
                    dve.tensor_scalar(mat_a[:], c_ds[:], row[:, 3, 2:3], None, ALU.mult).then_inc(sm("agg2_rows"), 1)
                if s == 2:
                    dve.memset(row[:, 5, :], 1.0)
                    link(dve.tensor_scalar(pen[:], c_ds[:], 1.0, None, ALU.min))
                    link(dve.tensor_scalar(pen[:], pen[:], -MASKED, MASKED, ALU.mult, ALU.add))
                    link(dve.tensor_scalar(row[:, 3, 3:4], scal[:, 2:3], 1.0, None, ALU.add))
                    dve.scalar_tensor_tensor(out=agg1[:], in0=ident[:], scalar=row[:, 3, 3:4], in1=c_ds[:],
                                             op0=ALU.mult, op1=ALU.add).then_inc(sm("c_ds"), 1)
                if s == 3:
                    dve.wait_ge(sm("agg2T"), 1)
                    link(dve.tensor_copy(agg2[:], wt[1][:, 0:P]))

            low_x("l0f")
            dve.wait_ge(sm("bias_hi"), 4)
            link(halve_bias(slice(0, 2 * D), slice(0, 2 * D)))
            halve_bias(slice(BL_COL, BL_COL + D), slice(2 * D, 3 * D)).then_inc(sm("l0_bias"), 1)

            def route_l0():
                logits_in("l0f", E8)
                negative_max("l0f", E8)
                softmax_top("l0f", E8, 2)
            pipeline(L0F, route_l0, 1, True, graph_matrices)
            layer_norm("l1g")
            low_x("l1g")
            split_chunk(G_L1G + 2)
            low_turned("l1g_hThi", tp, hT_hi[:, 0], hT_lo[:, 0], "l1g_hTlo")
            dve.wait_ge(sm("affine_l1"), 32)
            link(dve.tensor_tensor(X[:], X[:], affine[:, 1], ALU.add))
            dve.wait_ge(sm("bias_hi"), 6)
            halve_bias(slice(0, BL_COL), slice(0, BL_COL)).then_inc(sm("l2_bias"), 1)
            split_chunk(G_L1G + 3)
            dve.wait_ge(chunk_done, G_L1G + 2)
            statistics("l1g_out", pre[1][:])
            link(normalise("l1g_out", XN[:], pre[1][:]))
            link(dve.tensor_tensor(XN[:], XN[:], affine[:, 0], ALU.mult))
            link(dve.tensor_tensor(X[:], X[:], XN[:], ALU.add))
            layer_norm("l1f")
            low_x("l1f")
            dve.wait_ge(sm("rbias_in"), 48)
            link(logits_in("l1f", E8, 0))
            top(row[:, 0, 0:E8], E8, 1, row[:, 5, 0:E8], gates[:, 0:E8]).then_inc(sm("gates"), 1)
            dve.wait_ge(sm("gates"), nth("gates", "l1f"))
            dve.wait_ge(sm("l1f_pre"), 1)
            dve.scalar_tensor_tensor(out=h[:, 0, 0:256].rearrange("p (e n) -> p e n", n=H1),
                                     in0=pre[0][:, 0:256].rearrange("p (e n) -> p e n", n=H1), scalar=0.0,
                                     in1=gates[:, 0:E8].unsqueeze(2).broadcast_to([P, E8, H1]), op0=ALU.max,
                                     op1=ALU.mult).then_inc(sm("l1f_h"), 1)
            copy_gates("l1f")
            dve.wait_ge(sm("l1f_y"), 1)
            dve.tensor_tensor(X[:], X[:], y[0][:], ALU.add).then_inc(sm("l1f_done"), 1)
            dve.wait_ge(sm("l1f_done"), 1)
            layer_norm("l2g")
            low_x("l2g")
            low_turned("l2g_xagghi", y[0], aggT_hi[:, 0], aggT_lo[:, 0], "l2g_xagglo")
            link(logits_in("l2g", E4, 1))
            negative_max("l2g", E4)
            softmax_top("l2g", E4, 2)
            g = G_L2G
            for s in range(E4 + 2):
                if s < E4:
                    split_chunk(g + AHEAD)
                    split_chunk(g + 1 + AHEAD)
                    g += 2
                if s >= 2:
                    split_chunk(g + AHEAD)
                    split_chunk(g + 1 + AHEAD)
                    dve.wait_ge(sm("l2g_out"), s - 1)
                    if s >= 3:
                        dve.wait_ge(sm("l2g_summed"), s - 2)
                    dve.tensor_tensor(X[:], X[:], scratch[:, (s % 2) * D:(s % 2 + 1) * D], ALU.add).then_inc(
                        sm("l2g_summed"), 1)
                    g += 2
                if 1 <= s <= E4:
                    dve.wait_ge(sm("l2g_hi"), 2 * s)
                    dve.tensor_tensor(hT_lo[:, 0], chunks4(tp), hT_hi[:, 0].bitcast(F32), ALU.subtract).then_inc(
                        sm("l2g_lo"), 1)
                    dve.tensor_tensor(aggT_lo[:, 1], chunks4(wt[0]), aggT_hi[:, 1].bitcast(F32),
                                      ALU.subtract).then_inc(sm("l2g_lo"), 1)
            dve.wait_ge(sm("l2g_summed"), E4)
            layer_norm("l2f")
            low_x("l2f")

            def route_tree():
                logits_in("l2f", 7, 2).then_inc(sm("l2f_tree"), 1)
                dve.wait_ge(sm("l2f_p"), 1)
                p, q = row[:, 1, 0:7], row[:, 2, 0:7]
                link(dve.tensor_scalar(q, p, -1.0, 1.0, ALU.mult, ALU.add))
                link(dve.tensor_copy(row[:, 3, 0:1], q[:, 0:1]))
                link(dve.tensor_copy(row[:, 3, 1:2], p[:, 0:1]))
                for n_, (a, b) in ((2, (3, 4)), (4, (4, None))):
                    leaf = row[:, a, 0:n_]
                    nxt = (gates[:, 0:2 * n_] if b is None else row[:, b, 0:2 * n_]).rearrange("p (n b) -> p n b", b=2)
                    link(dve.tensor_tensor(nxt[:, :, 0], leaf, q[:, n_ - 1:2 * n_ - 1], ALU.mult))
                    last = dve.tensor_tensor(nxt[:, :, 1], leaf, p[:, n_ - 1:2 * n_ - 1], ALU.mult)
                    if b is None:
                        last.then_inc(sm("gates"), 1)
                    else:
                        link(last)
            pipeline(L2F, route_tree, 2, True)
            layer_norm("l3g")
            low_x("l3g")
            split_chunk(G_L3G + 2)
            dve.wait_ge(chunk_done, G_L3G + 2)
            dve.tensor_copy(h[:, 1], pre[1][:]).then_inc(sm("l3g_k"), 1)
            split_chunk(G_L3G + 3)
            dve.wait_ge(sm("l3g_kT"), 1)
            dve.tensor_copy(scratch[:, 3 * D:4 * D], y[1][:]).then_inc(sm("l3g_kTs"), 1)
            split_chunk(G_L3G + 4)
            dve.wait_ge(sm("l3g_scores"), 1)
            S = scratch[:, 0:2 * D].rearrange("p (i n) -> p i n", n=P)
            for p in range(2):
                link(dve.scalar_tensor_tensor(out=S[:, 4 * p:4 * p + 4], in0=chunks4(pre[p]), scalar=DK ** -0.5,
                                              in1=pen[:].unsqueeze(1).broadcast_to([P, 4, P]), op0=ALU.mult,
                                              op1=ALU.add))
            link(dve.reduce_max(row[:, 0, :], S, AX_X))
            dve.tensor_tensor(S, S, row[:, 0, :].unsqueeze(2).broadcast_to([P, HEADS, P]), ALU.subtract).then_inc(
                sm("l3g_centred"), 1)
            dve.wait_ge(sm("exp"), nth("exp", "l3g"))
            dve.tensor_tensor(S, S, c_ds[:].unsqueeze(1).broadcast_to([P, HEADS, P]), ALU.mult).then_inc(sm("l3g_p"), 1)
            dve.wait_ge(sm("l3g_p"), 1)
            link(dve.reduce_sum(row[:, 1, :], S, AX_X))
            dve.wait_ge(sm("l3g_pT"), 1)
            dve.tensor_copy(side[:, 2:4].rearrange("p c n -> p (c n)"), y[1][:]).then_inc(sm("l3g_pTs1"), 1)
            link(dve.tensor_scalar(row[:, 2, :], row[:, 1, :], 1e-30, None, ALU.max))
            link(dve.reciprocal(row[:, 3, :], row[:, 2, :]))
            dve.wait_ge(sm("l3g_av"), 1)
            dve.tensor_tensor(h[:, 0].rearrange("t (j p d) -> t p j d", p=2, d=DK),
                              pre[0][:].rearrange("t (j p d) -> t p j d", p=2, d=DK),
                              row[:, 3, :].rearrange("t (p j) -> t p j", p=2).unsqueeze(3).broadcast_to(
                                  [P, 2, 4, DK]), ALU.mult).then_inc(sm("l3g_a"), 1)
            low_turned("l3g_aThi", tp, hT_hi[:, 0], hT_lo[:, 0], "l3g_aTlo")
            split_chunk(G_L3G + 5)
            dve.wait_ge(chunk_done, G_L3G + 4)
            link(dve.tensor_tensor(h[:, 1], XN[:], pre[1][:], ALU.add))
            statistics("l3g_mid", h[:, 1])
            link(normalise("l3g_mid", h[:, 1], h[:, 1]))
            dve.wait_ge(sm("affine_l3"), 64)
            link(dve.tensor_tensor(h[:, 1], h[:, 1], affine[:, 0], ALU.mult))
            dve.tensor_tensor(h[:, 1], h[:, 1], affine[:, 1], ALU.add).then_inc(sm("l3g_mid"), 1)
            link(dve.tensor_tensor(X[:], X[:], affine[:, 3], ALU.add))
            dve.wait_ge(sm("l3g_mid"), 1)
            dve.wait_ge(sm("l3g_f2"), 1)
            link(dve.tensor_tensor(h[:, 1], h[:, 1], y[0][:], ALU.add))
            statistics("l3g_out", h[:, 1])
            link(normalise("l3g_out", h[:, 1], h[:, 1]))
            link(dve.tensor_tensor(h[:, 1], h[:, 1], affine[:, 2], ALU.mult))
            link(dve.tensor_tensor(X[:], X[:], h[:, 1], ALU.add))
            layer_norm("l3f")
            low_x("l3f")

            def route_l3():
                logits_in("l3f", E8)
                negative_max("l3f", E8)
                dve.wait_ge(sm("exp"), nth("exp", "l3f"))
                link(top(row[:, 0, 0:E8], E8, 2, row[:, 1, 0:E8], row[:, 2, 0:E8]))
                link(dve.reduce_sum(row[:, 7, 3:4], row[:, 2, 0:E8], AX_X))
                link(dve.reciprocal(row[:, 7, 4:5], row[:, 7, 3:4]))
                link(dve.memset(gates[:, 0:1], 1.0))
                link(dve.tensor_scalar(gates[:, 1:1 + E8], row[:, 2, 0:E8], row[:, 7, 4:5], None, ALU.mult))
            pipeline(L3F, route_l3, 1, False)


_INS = ["x", "src", "dst", "edge_weight", "L0_gnn_emb_1", "L0_gnn_emb_2", "L0_gnn_alpha_p", "L0_gnn_beta_p",
        "L0_ffn_Wg", "L0_ffn_W1", "L0_ffn_b1", "L0_ffn_W2", "L0_ffn_b2", "L1_gnn_eps", "L1_gnn_W1", "L1_gnn_b1",
        "L1_gnn_W2", "L1_gnn_b2", "L1_gnn_gamma", "L1_gnn_beta", "L1_ffn_Wr", "L1_ffn_br", "L1_ffn_W1", "L1_ffn_b1",
        "L1_ffn_W2", "L1_ffn_b2", "L2_gnn_gate_W", "L2_gnn_gate_b", "L2_gnn_Wl", "L2_gnn_bl", "L2_gnn_Wr",
        "L2_ffn_rw", "L2_ffn_rb", "L2_ffn_w1", "L2_ffn_b1", "L2_ffn_w2", "L2_ffn_b2", "L3_gnn_Wq", "L3_gnn_Wk",
        "L3_gnn_Wv", "L3_gnn_Wo", "L3_gnn_ln1_g", "L3_gnn_ln1_b", "L3_gnn_ln2_g", "L3_gnn_ln2_b", "L3_gnn_W1",
        "L3_gnn_b1", "L3_gnn_W2", "L3_gnn_b2", "L3_ffn_gate_w", "L3_ffn_w1", "L3_ffn_w2", "L3_ffn_sg_gate",
        "L3_ffn_sg_up", "L3_ffn_sg_down"]


def kernel(**inputs):
    import numpy as np
    import concourse.bacc as bacc
    from concourse.bass_utils import run_bass_kernel_spmd

    nc = bacc.Bacc("TRN2", target_bir_lowering=False, num_devices=1)
    arrays, handles = {}, {}
    for name in _INS:
        a = np.ascontiguousarray(inputs[name])
        arrays["in_" + name] = a
        handles[name] = nc.dram_tensor("in_" + name, a.shape, mybir.dt.from_np(a.dtype), kind="ExternalInput").ap()
    out = nc.dram_tensor("out_x", (P, D), F32, kind="ExternalOutput").ap()
    gnn_ffn_kernel(nc, handles, out)
    result = run_bass_kernel_spmd(nc, [arrays], core_ids=[0])
    return result.results[0]["out_x"]
```

```python
from contextlib import ExitStack

import concourse.bass as bass
from concourse import mybir

P = 128
D = 512
KC = D // P
NE = 2048
EC = NE // P
RAW_SLOTS = 8
SPLIT_SLOTS = 4
BRIDGE = {"l0g": 0, "l0f": 20, "l1f": 37, "l2g": 23, "l2f": 30, "l3g": 28, "l3f": 40}
HOTS = 10
SIM_AT = 10
AHEAD = 2
E8 = 8
E4 = 4
HEADS = 8
DK = D // HEADS
H1 = 32
LN_EPS = 1e-5
MASKED = -1e30

F32 = mybir.dt.float32
F32R = mybir.dt.float32r
I32 = mybir.dt.int32
ALU = mybir.AluOpType
ACT = mybir.ActivationFunctionType
AX_X = mybir.AxisListType.X

G_L0F = 0
G_L1G = G_L0F + 32
G_L2G = G_L1G + 2
G_L2F = G_L2G + 16
G_L3G = G_L2F + 64
G_L3F = G_L3G + 4
CHUNKS = G_L3F + 38


class Pipe:

    def __init__(self, tag, g0, n, per_expert, turned, summed, act, lead=0, selected=None):
        self.tag, self.g0, self.n, self.U = tag, g0, n, per_expert
        self.turned = turned
        self.summed = summed
        self.act, self.lead = act, lead
        self.route = lead or 1
        self.selected = selected

    def chunk(self, s):
        if self.lead:
            return self.g0 + 2 * s if s <= self.n else self.g0 + 2 * self.n + (s - self.n)
        if s < 2:
            return self.g0 + s
        return self.g0 + 2 * (s - 1) if s <= self.n else self.g0 + 2 * self.n - 1

    def loops(self):
        return (self.n - 4) // 4


L0F = Pipe("l0f", G_L0F, 16, 2, 0, 1, ACT.Gelu_apprx_tanh, selected=0)
L2F = Pipe("l2f", G_L2F, 32, 4, 16, 1 + 8 + 1, ACT.Gelu, selected=8)
L3F = Pipe("l3f", G_L3F, 18, 2, 16 + 32, 1 + 8 + 1 + 16, ACT.Silu, lead=2)
BL_COL = 2048


def multiplies_x(g):
    o = g - G_L3F
    return o < 2 * L3F.lead or (o < 2 * L3F.n and o % 2 == 0)


def blocked(g):
    return G_L3F <= g < G_L3F + 2 * L3F.n and (g - G_L3F) % 2 == 0


def turned(g):
    return G_L1G <= g < G_L2G or (G_L3F <= g < CHUNKS and not blocked(g))


TURNED = [g for g in range(CHUNKS) if turned(g)]
BLOCKED = [g for g in range(CHUNKS) if blocked(g)]
LOOP_TURNED, LOOP_BLOCKED = 4, 4


def turned_within(g):
    if g == G_L1G - 1:
        return G_L1G
    return g + AHEAD if g + AHEAD > G_L3F + 1 and turned(g + AHEAD) else None


def rounded(g):
    if blocked(g):
        return BLOCKED.index(g), LOOP_BLOCKED
    return g - sum(b < g for b in BLOCKED), LOOP_TURNED if g >= G_L3F else 8


def arrived(g):
    return sum(64 if blocked(c) else 16 for c in range(g % RAW_SLOTS, g + 1, RAW_SLOTS))


NORMED = ["l0g", "l0f", "l1g", "l1g_out", "l1f", "l2g", "l2f", "l3g", "l3g_mid", "l3g_out", "l3f"]
LAYERS = [t for t in NORMED if "_" not in t]
PRODUCTS = [t for t in LAYERS if t not in ("l0g", "l1f")]
STAGES = {
    "var": NORMED, "rstd": NORMED,
    "xn": LAYERS, "xt": LAYERS,
    "xhi": PRODUCTS, "xlo": PRODUCTS,
    "xt32": [t for t in LAYERS if t not in ("l1g", "l3g")],
    "logits": ["l0f", "l1f", "l2g", "l2f", "l3f"],
    "max": ["l0g", "l0f", "l2g", "l3f"], "exp": ["l0g", "l0f", "l2g", "l3f"],
    "gates": ["l0f", "l1f", "l2g", "l2f"],
    "gT": ["l0f", "l1f", "l2f"], "gTs": ["l0f", "l1f", "l2f"],
    "seed": ["l0f", "l2f"],
}


def nth(stage, tag):
    return STAGES[stage].index(tag) + 1


def at(count, per, it):
    return count if it is None else count + per * it


def gnn_ffn_kernel(nc, A, out):
    with ExitStack() as ctx:
        def sb(name, shape, dt=F32):
            return ctx.enter_context(nc.sbuf_tensor(name, shape, dt))

        def bank(name):
            return ctx.enter_context(nc.psum_tensor(name, [P, D], F32))

        named = {}

        def sm(name):
            if name not in named:
                named[name] = ctx.enter_context(nc.semaphore("s_" + name))
            return named[name]

        raw = sb("raw", [P, RAW_SLOTS, KC, D])
        w_hi = sb("w_hi", [P, SPLIT_SLOTS, KC, D], F32R)
        w_lo = sb("w_lo", [P, SPLIT_SLOTS, KC, D], F32R)
        X = sb("X", [P, D])
        XN = sb("XN", [P, D])
        XT = sb("XT", [P, KC, P])
        x_hi = sb("x_hi", [P, KC, P], F32R)
        x_lo = sb("x_lo", [P, KC, P], F32R)
        h = sb("h", [P, 2, D])
        hT_hi = sb("hT_hi", [P, 2, KC, P], F32R)
        hT_lo = sb("hT_lo", [P, 2, KC, P], F32R)
        aggT_hi = sb("aggT_hi", [P, 2, KC, P], F32R)
        aggT_lo = sb("aggT_lo", [P, 2, KC, P], F32R)
        bias_hl = sb("bias_hl", [16, BL_COL + D], F32R)
        scratch = sb("scratch", [P, 4 * D])
        affine = sb("affine", [P, 4, D])
        side = sb("side", [P, KC, 256])
        b2 = sb("b2", [33, D])
        brow = sb("brow", [65, D])
        ones = sb("ones", [65, P])
        sel_all = sb("sel_all", [16, E8, P], F32R)
        sel = sb("sel", [16, 2, P], F32R)
        iota_t = sb("iota_t", [P, P])
        ident = sb("ident", [P, P])
        c_sd = sb("c_sd", [P, P])
        c_ds = sb("c_ds", [P, P])
        agg1 = sb("agg1", [P, P])
        agg2 = sb("agg2", [P, P])
        pen = sb("pen", [P, P])
        mat_a = sb("mat_a", [P, P])
        mat_b = sb("mat_b", [P, P])
        tri = sb("tri", [P, E8, E8])
        ends_i = sb("ends_i", [P, 2, EC], I32)
        ends = sb("ends", [P, 3, EC])
        wg0 = sb("wg0", [P, KC, E8])
        wr1 = sb("wr1", [P, KC, E8])
        wg2 = sb("wg2", [P, KC, E4])
        rw_n = sb("rw_n", [15, D])
        rwT = sb("rwT", [P, 2, KC, E8])
        rbias = sb("rbias", [P, 3, E8])
        l3w1 = sb("l3w1", [P, KC, 32])
        l3b1 = sb("l3b1", [32, 1])
        fT = sb("fT", [33, P])
        scal = sb("scal", [P, 3])
        ab = sb("ab", [P, 2])
        gates = sb("gates", [P, 16])
        gT = sb("gT", [E8, P])
        row = sb("row", [P, 8, E8])
        st = sb("st", [P, 6])
        mv = sb("mv", [P, 2])
        rstd = sb("rstd", [P, 2])
        mhalf = sb("mhalf", [P, 1])
        half = sb("half", [16, 2])
        hot = raw[:, RAW_SLOTS - 2:].rearrange("p s c n -> p (s c n)")
        sel_raw = h[0:16, :, :].rearrange("p b n -> p (b n)")

        cmp = mat_b[:].rearrange("p (a n) -> p a n", a=2)

        weighted = side[:].rearrange("p c n -> p (c n)")
        w_blocks = scratch[:].rearrange("p (c n) -> p c n", c=KC)

        pre = [bank("pre0"), bank("pre1")]
        tp = bank("tp")
        y = [bank("y0"), bank("y1")]
        wt = [bank("wt0"), bank("wt1")]
        ms = bank("ms")

        landed = [sm(f"landed{i}") for i in range(RAW_SLOTS)]
        w_hi_ready = sm("w_hi_ready")
        blocked_hi = sm("blocked_hi")
        w_lo_ready = sm("w_lo_ready")
        w_blocked = sm("w_blocked")
        w_turned = sm("w_turned")
        chunk_done = sm("chunk_done")
        h_ready = sm("h_ready")
        h_turned = sm("h_turned")
        hT_hi_ready = sm("hT_hi_ready")
        hT_lo_ready = sm("hT_lo_ready")
        y_summed = sm("y_summed")
        sel_ready = sm("sel_ready")
        dve_link = sm("dve_link")

        def wait_rounded(engine, g, quarters=4, it=None):
            before, per_loop = rounded(g)
            engine.wait_ge(blocked_hi if blocked(g) else w_hi_ready, at(4 * before + quarters, 4 * per_loop, it))

        block = ctx.enter_context(nc.Block())

        def w1_unit(w, U, u, it):
            wv = w.rearrange("e (c p) n -> e p c n", p=P)
            return wv[at(u // U, 4 // U, it)][:, :, (u % U) * D:(u % U + 1) * D]

        def w2_unit(w, U, u, it):
            wv = w.rearrange("e (k c p) n -> e p k c n", c=KC, p=P)
            return wv[at(u // U, 4 // U, it)][:, u % U]

        def blocks_of(w):
            return w.rearrange("(b j) (q m) -> q j b m", j=32, m=P)

        def w1_blocks(w, u, it):
            wv = w.rearrange("e (k b j) (q m) -> e k q j b m", k=2, j=32, m=P)
            return wv[at(u // 2, 2, it)][u % 2]

        @block.sync
        def _(sp):
            sp.dma_start(X[:], A["x"]).then_inc(sm("x_in"), 16)
            for n, name in ((0, "src"), (1, "dst")):
                sp.dma_start(ends_i[:, n], A[name].rearrange("(p k) -> p k", p=P)).then_inc(sm("edges_in"), 16)
            sp.dma_start(ends[:, 2], A["edge_weight"].rearrange("(p k) -> p k", p=P)).then_inc(sm("edges_in"), 16)

            def small(dst, src, sem):
                sp.dma_start(dst, src).then_inc(sm(sem), 16)

            def early_loads(g):
                if g == 3:
                    for top in (0, E8):
                        small(scratch[top:top + E8, 0:2 * D], A["L0_ffn_b1"], "bias_in")
                        small(scratch[top:top + E8, 2 * D:3 * D], A["L2_gnn_bl"].rearrange("e l n -> (e l) n"),
                              "bias_in")
                    small(wg0[:], A["L0_ffn_Wg"].rearrange("(c p) n -> p c n", p=P), "wg0_in")
                if g == 5:
                    small(b2[0:E8, :], A["L0_ffn_b2"], "b2_l0")
                    small(rw_n[0:7, :], A["L2_ffn_rw"], "rw_in")
                    small(rw_n[7:15, :], A["L3_ffn_gate_w"], "rw_in")
                if g == RAW_SLOTS - 2:
                    sp.wait_ge(sm("hot_used"), EC)
                if g == RAW_SLOTS:
                    small(wr1[:], A["L1_ffn_Wr"].rearrange("(c p) n -> p c n", p=P), "routers_in")
                    small(wg2[:], A["L2_gnn_gate_W"].rearrange("(c p) n -> p c n", p=P), "routers_in")
                    small(rbias[:, 0, :], A["L1_ffn_br"].partition_broadcast(P), "rbias_in")
                    small(rbias[:, 1, 0:E4], A["L2_gnn_gate_b"].partition_broadcast(P), "rbias_in")
                    small(rbias[:, 2, 0:7], A["L2_ffn_rb"].partition_broadcast(P), "rbias_in")
                    for i, name in enumerate(("L1_gnn_b1", "L1_gnn_b2")):
                        small(brow[32 * i:32 * i + 1, :], A[name].rearrange("(a n) -> a n", a=1), "brow_in")
                    small(brow[64:65, 0:E8 * H1], A["L1_ffn_b1"].rearrange("(a e) n -> a (e n)", a=1), "brow_in")
                    small(affine[:, 0], A["L1_gnn_gamma"].partition_broadcast(P), "affine_l1")
                    small(affine[:, 1], A["L1_gnn_beta"].partition_broadcast(P), "affine_l1")
                    small(affine[:, 2:4], A["L1_ffn_W2"].rearrange("(c a) b n -> (a b) c n", a=4), "l1f_w2")
                    small(l3w1[:], A["L3_gnn_W1"].rearrange("(c p) n -> p c n", p=P), "l3_small_in")
                    small(l3b1[:], A["L3_gnn_b1"].rearrange("(n a) -> n a", a=1), "l3_small_in")

            def load(g, source, it=None):
                if it is None and g <= RAW_SLOTS:
                    early_loads(g)
                if g >= RAW_SLOTS or it is not None:
                    sp.wait_ge(w_lo_ready, at(4 * (g - RAW_SLOTS + 1), 32, it))
                if blocked(g):
                    for q in range(4):
                        dst = raw[32 * q:32 * q + 32, g % RAW_SLOTS].rearrange("j c n -> j (c n)")
                        sp.dma_start(dst.rearrange("j (b m) -> j b m", m=P), source[q]).then_inc(
                            landed[g % RAW_SLOTS], 16)
                else:
                    sp.dma_start(raw[:, g % RAW_SLOTS], source).then_inc(landed[g % RAW_SLOTS], 16)

            def square(w):
                return w.rearrange("(c p) n -> p c n", p=P)

            def steps(pipe, w1, w2):
                def step(s, it=None):
                    g = pipe.chunk(s)
                    if s < pipe.n:
                        if s < pipe.lead:
                            for i, w in enumerate(("L3_ffn_sg_gate", "L3_ffn_sg_up")):
                                rows = A[w][s * D:(s + 1) * D, :]
                                load(g + i, blocks_of(rows) if blocked(g + i) else square(rows))
                            return
                        load(g, w1(s - pipe.lead, it), it)
                        g += 1
                    if s >= 2:
                        if s - 2 < pipe.lead:
                            load(g, square(A["L3_ffn_sg_down"][:, (s - 2) * D:(s - 1) * D]))
                        else:
                            load(g, w2(s - 2 - pipe.lead, it), it)
                peeled = 8 if pipe.g0 == 0 else 4
                for s in range(peeled):
                    step(s)
                with sp.Fori(0, pipe.loops() - (peeled - 4) // 4) as it:
                    for s in range(peeled, peeled + 4):
                        step(s, it)
                for s in range(4 + 4 * pipe.loops(), pipe.n + 2):
                    step(s)

            steps(L0F, lambda u, it: w1_unit(A["L0_ffn_W1"], 2, u, it),
                  lambda u, it: w2_unit(A["L0_ffn_W2"], 2, u, it))
            load(G_L1G, square(A["L1_gnn_W1"]))
            load(G_L1G + 1, square(A["L1_gnn_W2"]))
            g = G_L2G
            for s in range(E4 + 2):
                for e, layer in ((s, 0), (s - 2, 1)):
                    if 0 <= e < E4:
                        load(g, square(A["L2_gnn_Wr"][e, layer]))
                        load(g + 1, square(A["L2_gnn_Wl"][e, layer]))
                        g += 2
            steps(L2F, lambda u, it: w1_unit(A["L2_ffn_w1"], 4, u, it),
                  lambda u, it: w2_unit(A["L2_ffn_w2"], 4, u, it))
            for i, name in enumerate(("L3_gnn_Wq", "L3_gnn_Wk", "L3_gnn_Wv", "L3_gnn_Wo")):
                load(G_L3G + i, square(A[name]))
            steps(L3F, lambda u, it: w1_blocks(A["L3_ffn_w1"], u, it),
                  lambda u, it: w1_unit(A["L3_ffn_w2"], 2, u, it))
            sp.wait_ge(y_summed, L3F.summed + L3F.n // 2)
            sp.dma_start(out, X[:]).then_inc(sm("out_written"), 16)
            sp.wait_ge(sm("out_written"), 16)

        @block.gpsimd
        def _(pool):
            n = [0]

            def link(ins):
                n[0] += 1
                ins.then_inc(sm("pool_link"), 1)
                pool.wait_ge(sm("pool_link"), n[0])

            link(pool.memset(ident[:], 0.0))
            link(pool.affine_select(out=ident[:], in_=ident[:], compare_op=ALU.not_equal, fill=1.0, base=0,
                                    pattern=[[-1, P]], channel_multiplier=1))
            link(pool.memset(mhalf[:], -0.5))
            pool.iota(iota_t[:], pattern=[[1, P]], base=0, channel_multiplier=0,
                      allow_small_or_imprecise_dtypes=True).then_inc(sm("consts"), 1)

            def inv_std(tag):
                pool.wait_ge(sm("var"), nth("var", tag))
                link(pool.tensor_scalar(rstd[:, 0:1], mv[:, 1:2], LN_EPS, None, ALU.add))
                pool.tensor_tensor(rstd[:, 1:2], rstd[:, 0:1], mhalf[:], ALU.pow).then_inc(sm("rstd"), 1)

            inv_std("l0g")
            link(pool.memset(tri[:], 1.0))
            link(pool.affine_select(out=tri[:], in_=tri[:], compare_op=ALU.is_gt, fill=0.0, base=0,
                                    pattern=[[1, E8], [-1, E8]], channel_multiplier=0))
            link(pool.memset(ones[:], 1.0))
            link(pool.memset(fT[:], 1.0))
            link(pool.memset(half[:], 1.0))
            link(pool.affine_select(out=half[:, 0:1], in_=half[:, 0:1], compare_op=ALU.is_gt, fill=0.0, base=-7,
                                    pattern=[[0, 1]], channel_multiplier=1))
            link(pool.affine_select(out=half[:, 1:2], in_=half[:, 1:2], compare_op=ALU.is_gt, fill=-1.0, base=8,
                                    pattern=[[0, 1]], channel_multiplier=-1))
            link(pool.memset(sel_raw, 0.0))
            link(pool.affine_select(out=sel_raw, in_=sel_raw, compare_op=ALU.not_equal, fill=1.0, base=0,
                                    pattern=[[-1, E8], [0, P]], channel_multiplier=1))
            pool.affine_select(out=sel_raw, in_=sel_raw, compare_op=ALU.not_equal, fill=1.0, base=-E8,
                               pattern=[[-1, E8], [0, P]], channel_multiplier=1).then_inc(sm("sel_raw"), 1)

            for tag in NORMED[1:]:
                inv_std(tag)

        @block.scalar
        def _(act):
            def small(dst, src, sem):
                act.dma_start(dst, src).then_inc(sm(sem), 16)

            emb = [A[n].rearrange("(c p) n -> p c n", p=P) for n in ("L0_gnn_emb_1", "L0_gnn_emb_2")]
            small(side[:, :, 0:P], emb[0], "emb_in")
            small(side[:, :, P:2 * P], emb[1], "emb_in")
            for i, name in enumerate(("L0_gnn_alpha_p", "L0_gnn_beta_p", "L1_gnn_eps")):
                small(scal[:, i:i + 1], A[name].partition_broadcast(P), "scal_in")

            def round_block(g, q, it=None):
                if q == 0:
                    act.wait_ge(chunk_done, at(g - SPLIT_SLOTS + 1, 8, it))
                act.wait_ge(w_blocked, at(4 * BLOCKED.index(g) + q + 1, 4 * LOOP_BLOCKED, it))
                act.activation(w_hi[:, g % SPLIT_SLOTS, q], w_blocks[:, q], ACT.Copy).then_inc(blocked_hi, 1)

            def round_turned_quarter(g, q, it=None):
                act.wait_ge(w_turned, at(4 * TURNED.index(g) + q + 1, 4 * LOOP_TURNED, it))
                act.activation(w_hi[:, g % SPLIT_SLOTS, q], wt[q % 2][:], ACT.Copy).then_inc(w_hi_ready, 1)

            def round_chunk(g, it=None, also=None):
                if g >= CHUNKS or blocked(g):
                    return
                if g >= SPLIT_SLOTS or it is not None:
                    act.wait_ge(chunk_done, at(g - SPLIT_SLOTS + 1, 8, it))
                if turned(g):
                    for q in range(4):
                        round_turned_quarter(g, q, it)
                        if also is not None:
                            round_block(also, q, it)
                else:
                    act.wait_ge(landed[g % RAW_SLOTS], at(arrived(g), 16, it))
                    act.activation(w_hi[:, g % SPLIT_SLOTS], raw[:, g % RAW_SLOTS], ACT.Copy).then_inc(w_hi_ready, 4)

            def round_x(tag, plain):
                act.wait_ge(sm("xt"), nth("xt", tag))
                act.activation(x_hi[:], tp[:].rearrange("p (c n) -> p c n", n=P), ACT.Copy).then_inc(sm("xhi"), 1)
                if plain:
                    act.wait_ge(sm("xlo"), nth("xlo", tag))
                    act.activation(XT[:], tp[:].rearrange("p (c n) -> p c n", n=P), ACT.Copy).then_inc(
                        sm("xt32"), 1)

            def round_turned(ready, bank_ap, dst, done):
                act.wait_ge(sm(ready), 1)
                act.activation(dst, bank_ap[:].rearrange("p (c n) -> p c n", n=P), ACT.Copy).then_inc(sm(done), 1)

            def pipeline(pipe, after0):
                def select(q, it=None):
                    e = q // (pipe.U // 2)
                    src = sel_all[:, e] if it is None else sel_all[:].rearrange("p e n -> p (e n)")[
                        :, bass.ds((e + (4 // pipe.U) * it) * P, P)]
                    act.activation(sel[:, q % 2], src.bitcast(F32), ACT.Copy).then_inc(sel_ready, 1)

                def step(s, it=None):
                    g = pipe.chunk(s)
                    if pipe.selected is not None and s % 2 == 0 and s < pipe.n and (s >= 4 or s == 0):
                        select(s // 2, it)
                        if s == 0:
                            select(1)
                    also = g + 4 if blocked(g + 4) else None
                    if s < pipe.lead:
                        lead_step(s, g, also)
                    else:
                        if s < pipe.n:
                            round_chunk(g + AHEAD, it)
                            g += 1
                        if 1 <= s <= pipe.n:
                            high_turned(s, it)
                        if s < pipe.n:
                            act.wait_ge(chunk_done, at(pipe.chunk(s) + 1, 8, it))
                            act.activation(h[:, s % 2], pre[s % 2][:], pipe.act).then_inc(h_ready, 1)
                        if s >= 2:
                            if s == pipe.route:
                                after0()
                            round_chunk(g + AHEAD, it, also)
                        if s == pipe.route == 1:
                            after0()

                def high_turned(s, it=None):
                    act.wait_ge(h_turned, at(pipe.turned + s, 4, it))
                    act.activation(hT_hi[:, (s - 1) % 2], tp[:].rearrange("p (c n) -> p c n", n=P),
                                   ACT.Copy).then_inc(hT_hi_ready, 1)

                def lead_step(s, g, also):
                    act.wait_ge(chunk_done, g + 1)
                    act.activation(h[:, s % 2], pre[s % 2][:], pipe.act).then_inc(sm("gate_ready"), 1)
                    round_chunk(g + 1 + AHEAD, None, also)
                    if s > 0:
                        high_turned(s)
                for s in range(4):
                    step(s)
                with act.Fori(0, pipe.loops()) as it:
                    for s in range(4, 8):
                        step(s, it)
                for s in range(4 + 4 * pipe.loops(), pipe.n + 2):
                    step(s)

            def exp_logits(tag, E):
                act.wait_ge(sm("max"), nth("max", tag))
                act.activation(row[:, 1, 0:E], row[:, 0, 0:E], ACT.Exp, bias=row[:, 7, 0:1],
                               accum_out=row[:, 7, 1:2]).then_inc(sm("exp"), 1)

            def halve_bias(cols, raw_cols):
                act.activation(bias_hl[:, cols], scratch[0:16, raw_cols], ACT.Copy).then_inc(sm("bias_hi"), 1)
                act.activation(scratch[0:16, raw_cols], scratch[0:16, raw_cols], ACT.Copy,
                               scale=half[:, 0:1]).then_inc(sm("bias_hi"), 1)

            act.wait_ge(sm("xt"), nth("xt", "l0g"))
            act.activation(XT[:], tp[:].rearrange("p (c n) -> p c n", n=P), ACT.Copy).then_inc(sm("xt32"), 1)
            act.wait_ge(sm("scal_in"), 48)
            act.activation(ab[:], scal[:, 0:2], ACT.Exp).then_inc(sm("ab"), 1)
            act.wait_ge(sm("sel_raw"), 1)
            act.activation(sel_all[:].rearrange("p e n -> p (e n)"), sel_raw, ACT.Copy).then_inc(sm("sel_all"), 1)
            act.wait_ge(sm("sel_all"), 1)
            act.wait_ge(sm("l0g_x12"), 1)
            act.activation(h[:, 0, 0:2 * P], pre[0][:, 0:2 * P], ACT.Copy).then_inc(sm("l0g_x12s"), 1)
            act.wait_ge(sm("max"), nth("max", "l0g"))
            act.activation(mat_b[:], mat_a[:], ACT.Exp, bias=row[:, 0, 0:1],
                           accum_out=row[:, 0, 1:2]).then_inc(sm("exp"), 1)
            for c in range(KC):
                small(side[:, c].rearrange("p (e n) -> p e n", n=H1),
                      A["L1_ffn_W1"][:, c * P:(c + 1) * P, :].rearrange("e p n -> p e n"), "l1f_w1")
            round_chunk(0)
            round_chunk(1)
            act.wait_ge(sm("bias_in"), 64)
            halve_bias(slice(0, 2 * D), slice(0, 2 * D))
            halve_bias(slice(BL_COL, BL_COL + D), slice(2 * D, 3 * D))
            round_x("l0f", True)
            pipeline(L0F, lambda: exp_logits("l0f", E8))
            act.wait_ge(sm("l0_bias"), 1)
            for top in (0, E8):
                small(scratch[top:top + E8, :], A["L2_ffn_b1"], "bias_in")
            small(b2[0:E8, :], A["L1_ffn_b2"], "b2_l1")
            round_x("l1g", False)
            act.wait_ge(chunk_done, G_L1G + 1)
            act.activation(h[:, 0], pre[0][:], ACT.Relu).then_inc(sm("l1g_h"), 1)
            round_turned("l1g_hT", tp, hT_hi[:, 0], "l1g_hThi")
            round_chunk(G_L1G + 2)
            round_chunk(G_L1G + 3)
            act.wait_ge(sm("xt"), nth("xt", "l1f"))
            act.activation(XT[:], tp[:].rearrange("p (c n) -> p c n", n=P), ACT.Copy).then_inc(sm("xt32"), 1)
            act.wait_ge(sm("l1f_hT"), 1)
            act.activation(h[:, 1, 0:2 * P], tp[:, 0:2 * P], ACT.Copy).then_inc(sm("l1f_hTs"), 1)
            small_done = sm("l1f_done")
            act.wait_ge(small_done, 1)
            small(b2[0:E8, :], A["L2_ffn_b2"], "b2_l2")
            for i, name in enumerate(("L3_gnn_ln1_g", "L3_gnn_ln1_b", "L3_gnn_ln2_g", "L3_gnn_ln2_b")):
                small(affine[:, i], A[name].partition_broadcast(P), "affine_l3")
            round_x("l2g", True)
            round_turned("l2g_xagg", y[0], aggT_hi[:, 0], "l2g_xagghi")
            g = G_L2G
            for s in range(E4 + 2):
                if s < E4:
                    round_chunk(g + AHEAD)
                    round_chunk(g + 1 + AHEAD)
                    act.wait_ge(chunk_done, g + 2)
                    act.activation(h[:, s % 2], pre[s % 2][:], ACT.Relu).then_inc(sm("l2g_h"), 1)
                    if s == 0:
                        exp_logits("l2g", E4)
                    if s == 0:
                        act.wait_ge(sm("bias_in"), 96)
                    halve_bias(slice(s * D, s * D + D), slice(s * D, s * D + D))
                    g += 2
                if 1 <= s <= E4:
                    act.wait_ge(sm("l2g_turned"), s)
                    act.activation(hT_hi[:, (s - 1) % 2], tp[:].rearrange("p (c n) -> p c n", n=P), ACT.Copy).then_inc(
                        sm("l2g_h_hi"), 1)
                if s >= 2:
                    round_chunk(g + AHEAD)
                    round_chunk(g + 1 + AHEAD)
                    act.wait_ge(sm("gates"), nth("gates", "l2g"))
                    act.wait_ge(chunk_done, g + 2)
                    if s >= 4:
                        act.wait_ge(sm("l2g_summed"), s - 3)
                    act.activation(weighted[:, (s % 2) * D:(s % 2 + 1) * D], y[s % 2][:], ACT.Relu,
                                   scale=gates[:, s - 2:s - 1]).then_inc(sm("l2g_out"), 1)
                    g += 2
                if 1 <= s <= E4:
                    act.wait_ge(sm("l2g_agg"), s)
                    act.activation(aggT_hi[:, 1], wt[0][:].rearrange("p (c n) -> p c n", n=P), ACT.Copy).then_inc(
                        sm("l2g_agg_hi"), 1)
            def leaf_sigmoid():
                act.wait_ge(sm("l2f_tree"), 1)
                act.activation(row[:, 1, 0:7], row[:, 0, 0:7], ACT.Sigmoid).then_inc(sm("l2f_p"), 1)
            round_x("l2f", True)
            pipeline(L2F, leaf_sigmoid)
            small(b2[0:32, :], A["L3_gnn_W2"], "l3_small_in")
            small(b2[32:33, :], A["L3_gnn_b2"].rearrange("(a n) -> a n", a=1), "l3_small_in")
            round_x("l3g", False)
            round_chunk(G_L3G + 2)
            round_chunk(G_L3G + 3)
            act.wait_ge(chunk_done, G_L3G + 1)
            act.activation(h[:, 0], pre[0][:], ACT.Copy).then_inc(sm("l3g_q"), 1)
            act.wait_ge(sm("l3g_qT"), 1)
            act.activation(scratch[:, 2 * D:3 * D], tp[:], ACT.Copy).then_inc(sm("l3g_qTs"), 1)
            for p in range(2):
                act.wait_ge(sm("l3g_centred"), p + 1)
                act.activation(scratch[:, p * D:p * D + D], scratch[:, p * D:p * D + D], ACT.Exp).then_inc(
                    sm("l3g_exp"), 1)
            act.wait_ge(chunk_done, G_L3G + 3)
            act.activation(XT[:].rearrange("p c n -> p (c n)"), y[0][:], ACT.Copy).then_inc(sm("l3g_v"), 1)
            act.wait_ge(sm("l3g_pT"), 1)
            act.activation(side[:, 0:2].rearrange("p c n -> p (c n)"), tp[:], ACT.Copy).then_inc(sm("l3g_pTs0"), 1)
            round_turned("l3g_aT", tp, hT_hi[:, 0], "l3g_aThi")
            for q in range(4):
                round_block(G_L3F, q)
            act.wait_ge(chunk_done, G_L3F + 1 - SPLIT_SLOTS + 1)
            round_turned_quarter(G_L3F + 1, 0)
            round_turned_quarter(G_L3F + 1, 1)
            act.wait_ge(sm("l3g_midT"), 1)
            act.activation(XT[:], tp[:].rearrange("p (c n) -> p c n", n=P), ACT.Copy).then_inc(sm("l3g_midTs"), 1)
            act.wait_ge(sm("l3g_f1"), 1)
            act.activation(fT[0:32, :], ms[0:32, 0:P], ACT.Relu, bias=l3b1[:, 0:1]).then_inc(sm("l3g_f1s"), 1)
            round_turned_quarter(G_L3F + 1, 2)
            round_turned_quarter(G_L3F + 1, 3)
            round_x("l3f", True)
            for q in range(4):
                round_block(G_L3F + 2, q)
            pipeline(L3F, lambda: exp_logits("l3f", E8))

        @block.tensor
        def _(pe):
            def blocked_columns(ap, c):
                return ap.rearrange("p (n c) -> p c n", c=KC)[:, c]

            def turn_weights(g, q, it=None):
                if q == 0:
                    pe.wait_ge(landed[g % RAW_SLOTS], at(arrived(g), 16, it))
                if q >= 2:
                    pe.wait_ge(w_lo_ready, at(4 * g + q - 1, 32, it))
                elif TURNED.index(g) > 0:
                    before = TURNED[TURNED.index(g) - 1]
                    pe.wait_ge(w_lo_ready, at(4 * before + q + 3, 32, it))
                for c in range(KC):
                    rows = raw[:, g % RAW_SLOTS, c]
                    if g >= G_L3F and multiplies_x(g):
                        cols = blocked_columns(rows, q)
                    else:
                        cols = rows[:, q * P:(q + 1) * P]
                    last = pe.transpose(wt[q % 2][:, c * P:(c + 1) * P], cols, ident[:])
                last.then_inc(w_turned, 1)

            def product(g, dst, xs_hi, xs_lo, start, stop, it=None, bias=None, low=None):
                hi, lo = w_hi[:, g % SPLIT_SLOTS], w_lo[:, g % SPLIT_SLOTS]
                passes = [(xs_hi, hi, k) for k in range(KC)] + [(xs_hi, lo, k) for k in range(KC)] + [
                    (xs_lo, hi, k) for k in range(KC)]
                wait_rounded(pe, g, 4, it)
                for i, (xs, ws, k) in enumerate(passes):
                    if i % 3 == 0 and turned_within(g) is not None:
                        turn_weights(turned_within(g), i // 3, it)
                    if i == KC:
                        pe.wait_ge(w_lo_ready, at(4 * (g + 1), 32, it))
                    if i == 2 * KC and low is not None:
                        pe.wait_ge(low[0], low[1])
                    last = pe.matmul(dst, xs[:, k], ws[:, k], start=start and i == 0,
                                     stop=stop and i == len(passes) - 1 and bias is None)
                if bias is not None:
                    pair, rows, halves = bias
                    if g in (G_L0F, G_L2F):
                        pe.wait_ge(*((sm("l0_bias"), 1) if g == G_L0F else (sm("l2_bias"), 4)))
                    pe.wait_ge(sel_ready, pair)
                    last = pe.matmul(dst, rows, halves, start=False, stop=True)
                last.then_inc(chunk_done, 1)

            def turn(dst, src, done, n=KC):
                for c in range(n):
                    last = pe.transpose(dst[:, c * P:(c + 1) * P], src[:, c * P:(c + 1) * P], ident[:])
                last.then_inc(done, 1)

            def keep_clock(n):
                for _ in range(n):
                    pe.transpose(ms[:, 0:P], ident[:], ident[:])

            def turn_x(tag):
                keep_clock(BRIDGE[tag])
                pe.wait_ge(sm("xn"), nth("xn", tag))
                if tag == "l3f":
                    for c in range(KC):
                        last = pe.transpose(tp[:, c * P:(c + 1) * P], blocked_columns(XN[:], c), ident[:])
                    last.then_inc(sm("xt"), 1)
                else:
                    turn(tp, XN, sm("xt"))

            def logits(tag, w, E):
                pe.wait_ge(sm("xt32"), nth("xt32", tag))
                for c in range(KC):
                    last = pe.matmul(ms[:, 0:E], XT[:, c], w[:, c, 0:E], start=c == 0, stop=c == KC - 1)
                last.then_inc(sm("logits"), 1)

            def turn_gates(tag, n):
                pe.wait_ge(sm("gates"), nth("gates", tag))
                pe.transpose(ms[0:n, 0:P], gates[:, 0:n], ident[:]).then_inc(sm("gT"), 1)

            def seed(tag, dst):
                pe.wait_ge(sm("gTs"), nth("gTs", tag))
                return pe.matmul(dst, gT[:], b2[0:E8, :], start=True, stop=tag != "l1f")

            def pipeline(pipe, router, seeded, between=None):
                def step(s, it=None):
                    g = pipe.chunk(s)
                    low = None
                    if s == 0:
                        pe.wait_ge(sm("xhi"), nth("xhi", pipe.tag))
                        low = (sm("xlo"), nth("xlo", pipe.tag))
                    if s < pipe.lead:
                        product(g, pre[s % 2][:], x_hi, x_lo, True, True, low=low)
                        product(g + 1, y[s % 2][:], x_hi, x_lo, True, True)
                    elif s < pipe.n:
                        bias = None
                        if pipe.selected is not None:
                            col = (s % pipe.U) * D
                            bias = (at(pipe.selected + s // 2 + 1, 2, it), sel[:, (s // 2) % 2],
                                    bias_hl[:, col:col + D])
                        product(g, pre[s % 2][:], x_hi, x_lo, True, True, it, bias, low)
                        g += 1
                    if s == 0:
                        router()
                    if s == 3 and seeded:
                        turn_gates(pipe.tag, E8)
                    if 1 <= s <= pipe.n:
                        if s - 1 < pipe.lead:
                            pe.wait_ge(sm("shared_ready"), s)
                        else:
                            pe.wait_ge(h_ready, at(pipe.turned + s - pipe.lead, 4, it))
                        if pipe.turned + s - 1 > 0:
                            pe.wait_ge(hT_lo_ready, at(pipe.turned + s - 1, 4, it))
                        turn(tp, h[:, (s - 1) % 2], h_turned)
                    if s >= 2:
                        pe.wait_ge(hT_hi_ready, at(pipe.turned + s - 1, 4, it))
                        if s % 2 == 0 and s >= 4:
                            pe.wait_ge(y_summed, at(pipe.summed + (s - 4) // 2, 2, it))
                        product(g, y[((s - 2) // 2) % 2][:], hT_hi[:, s % 2], hT_lo[:, s % 2],
                                s % 2 == 0, s % 2 == 1, it, low=(hT_lo_ready, at(pipe.turned + s - 1, 4, it)))
                    if s == 3 and seeded:
                        seed(pipe.tag, wt[0][:]).then_inc(sm("seed"), 1)
                    if between is not None and it is None:
                        between(s)
                for s in range(4):
                    step(s)
                with pe.Fori(0, pipe.loops()) as it:
                    for s in range(4, 8):
                        step(s, it)
                for s in range(4 + 4 * pipe.loops(), pipe.n + 2):
                    step(s)

            pe.wait_ge(sm("consts"), 1)
            turn_x("l0g")
            pe.wait_ge(sm("xt32"), nth("xt32", "l0g"))
            pe.wait_ge(sm("emb_in"), 32)
            for i in range(2):
                for c in range(KC):
                    last = pe.matmul(pre[0][:, i * P:(i + 1) * P], side[:, c, i * P:(i + 1) * P], XT[:, c],
                                     start=c == 0, stop=c == KC - 1)
            last.then_inc(sm("l0g_x12"), 1)
            for k in range(EC):
                o = (k % HOTS) * 3 * P
                pe.wait_ge(sm("hot_ready"), k + 1)
                pe.matmul(y[0][:, 0:2 * P], hot[:, o:o + P], hot[:, o + P:o + 3 * P], start=k == 0,
                          stop=k == EC - 1).then_inc(sm("hot_used"), 1)
                if k == SIM_AT - 4:
                    pe.wait_ge(sm("l0g_x12s"), 1)
                    pe.matmul(ms[:, 0:P], h[:, 0, 0:P], h[:, 0, P:2 * P], start=True, stop=True).then_inc(
                        sm("l0g_sim"), 1)
            pe.wait_ge(sm("l0g_a"), 1)
            pe.transpose(ms[:, 0:P], mat_a[:], ident[:]).then_inc(sm("l0g_aT"), 1)
            pe.wait_ge(sm("l0g_aTs"), 1)
            for i in range(5):
                for part in range(2):
                    cols = slice(part * 256, part * 256 + 256)
                    if i:
                        pe.wait_ge(sm("l0g_swept"), 2 * (i - 1) + part + 1)
                    pe.matmul(pre[part][:, 0:256], mat_b[:], XT[:].rearrange("p c n -> p (c n)")[:, cols] if i
                              else XN[:, cols], start=True, stop=True).then_inc(sm("l0g_sweep"), 1)
            def graph_matrices(s):
                if s == 1:
                    pe.wait_ge(sm("c_sd"), 1)
                    pe.wait_ge(sm("rw_in"), 32)
                    pe.transpose(wt[1][:, 0:P], c_sd[:], ident[:])
                    for c in range(KC):
                        for i, cols in enumerate((rw_n[:, c * P:(c + 1) * P], blocked_columns(rw_n[:], c))):
                            o = P + (i * KC + c) * 15
                            last = pe.transpose(wt[1][:, o:o + 15], cols, ident[0:15, 0:15])
                    last.then_inc(sm("c_dsT"), 1)
                if s == 2:
                    pe.wait_ge(sm("agg2_rows"), 1)
                    pe.transpose(wt[1][:, 0:P], mat_a[:], ident[:]).then_inc(sm("agg2T"), 1)

            turn_x("l0f")
            pe.wait_ge(sm("wg0_in"), 16)
            pe.wait_ge(sm("b2_l0"), 16)
            pipeline(L0F, lambda: logits("l0f", wg0, E8), True, graph_matrices)
            pe.wait_ge(sm("brow_in"), 48)
            pe.matmul(pre[0][:], ones[0:1, :], brow[0:1, :], start=True, stop=False)
            pe.matmul(pre[1][:], ones[32:33, :], brow[32:33, :], start=True, stop=False)
            pe.wait_ge(sm("c_ds"), 1)
            for q in range(4):
                turn_weights(G_L1G + 1, q)
            pe.wait_ge(sm("xn"), nth("xn", "l1g"))
            for c in range(KC):
                last = pe.matmul(tp[:, c * P:(c + 1) * P], XN[:, c * P:(c + 1) * P], agg1[:], start=True, stop=True)
            last.then_inc(sm("xt"), 1)
            pe.wait_ge(sm("xhi"), nth("xhi", "l1g"))
            product(G_L1G, pre[0][:], x_hi, x_lo, False, True, low=(sm("xlo"), nth("xlo", "l1g")))
            pe.wait_ge(sm("l1g_h"), 1)
            turn(tp, h[:, 0], sm("l1g_hT"))
            pe.wait_ge(sm("l1g_hThi"), 1)
            product(G_L1G + 1, pre[1][:], hT_hi[:, 0], hT_lo[:, 0], False, True, low=(sm("l1g_hTlo"), 1))
            pe.matmul(pre[0][:, 0:256], ones[64:65, :], brow[64:65, 0:256], start=True, stop=False)
            pe.wait_ge(sm("routers_in"), 32)
            turn_x("l1f")
            logits("l1f", wr1, E8)
            pe.wait_ge(sm("l1f_w1"), 16 * KC)
            for c in range(KC):
                last = pe.matmul(pre[0][:, 0:256], XT[:, c], side[:, c], start=False, stop=c == KC - 1)
            last.then_inc(sm("l1f_pre"), 1)
            turn_gates("l1f", E8)
            pe.wait_ge(sm("b2_l1"), 16)
            pe.wait_ge(sm("l1f_h"), 1)
            turn(tp, h[:, 0], sm("l1f_hT"), 2)
            seed("l1f", y[0][:])
            pe.wait_ge(sm("l1f_hTs"), 1)
            pe.wait_ge(sm("l1f_w2"), 16)
            for c in range(2):
                last = pe.matmul(y[0][:], h[:, 1, c * P:(c + 1) * P], affine[:, 2 + c], start=False,
                                 stop=c == 1)
            last.then_inc(sm("l1f_y"), 1)
            turn_x("l2g")
            for c in range(KC):
                last = pe.matmul(y[0][:, c * P:(c + 1) * P], XN[:, c * P:(c + 1) * P], agg2[:], start=True, stop=True)
            last.then_inc(sm("l2g_xagg"), 1)
            g = G_L2G
            pe.wait_ge(sm("xhi"), nth("xhi", "l2g"))
            for s in range(E4 + 2):
                if s < E4:
                    pe.matmul(pre[s % 2][:], sel_all[:, 2 * s], bias_hl[:, BL_COL:BL_COL + D], start=True, stop=False)
                    product(g, pre[s % 2][:], x_hi, x_lo, False, False, low=(sm("xlo"), nth("xlo", "l2g")))
                    if s == 0:
                        pe.wait_ge(sm("l2g_xagghi"), 1)
                    product(g + 1, pre[s % 2][:], aggT_hi[:, 0], aggT_lo[:, 0], False, True, low=(sm("l2g_xagglo"), 1))
                    if s == 0:
                        logits("l2g", wg2, E4)
                    g += 2
                if 1 <= s <= E4:
                    if s == E4:
                        keep_clock(23)
                    pe.wait_ge(sm("l2g_h"), s)
                    if s >= 2:
                        pe.wait_ge(sm("l2g_h_lo"), s - 1)
                        pe.wait_ge(sm("l2g_agg_lo"), s - 1)
                    hs = h[:, (s - 1) % 2]
                    turn(tp, hs, sm("l2g_turned"))
                    for c in range(KC):
                        last = pe.matmul(wt[0][:, c * P:(c + 1) * P], hs[:, c * P:(c + 1) * P], agg2[:], start=True,
                                         stop=True)
                    last.then_inc(sm("l2g_agg"), 1)
                if s >= 2:
                    pe.wait_ge(sm("l2g_h_hi"), s - 1)
                    if s >= 4:
                        pe.wait_ge(sm("l2g_out"), s - 3)
                    pe.matmul(y[s % 2][:], sel_all[:, 2 * (s - 2) + 1], bias_hl[:, BL_COL:BL_COL + D], start=True,
                              stop=False)
                    product(g, y[s % 2][:], hT_hi[:, s % 2], hT_lo[:, s % 2], False, False,
                            low=(sm("l2g_h_lo"), s - 1))
                    pe.wait_ge(sm("l2g_agg_hi"), s - 1)
                    product(g + 1, y[s % 2][:], aggT_hi[:, 1], aggT_lo[:, 1], False, True,
                            low=(sm("l2g_agg_lo"), s - 1))
                    g += 2
            turn_x("l2f")
            pe.wait_ge(sm("b2_l2"), 16)
            pipeline(L2F, lambda: logits("l2f", rwT[:, 0], 7), True)
            turn_x("l3g")
            pe.wait_ge(sm("xhi"), nth("xhi", "l3g"))
            product(G_L3G, pre[0][:], x_hi, x_lo, True, True, low=(sm("xlo"), nth("xlo", "l3g")))
            product(G_L3G + 1, pre[1][:], x_hi, x_lo, True, True)
            pe.wait_ge(sm("l3g_q"), 1)
            turn(tp, h[:, 0], sm("l3g_qT"))
            pe.wait_ge(sm("l3g_k"), 1)
            turn(y[1], h[:, 1], sm("l3g_kT"))
            pe.wait_ge(sm("l3g_qTs"), 1)
            pe.wait_ge(sm("l3g_kTs"), 1)
            for j in range(HEADS // 2):
                for p in range(2):
                    rows = slice(p * DK, (p + 1) * DK)
                    last = pe.matmul(pre[p][:, j * P:(j + 1) * P], scratch[rows, 2 * D + j * P:2 * D + (j + 1) * P],
                                     scratch[rows, 3 * D + j * P:3 * D + (j + 1) * P], start=True, stop=True)
            last.then_inc(sm("l3g_scores"), 1)
            product(G_L3G + 2, y[0][:], x_hi, x_lo, True, True)
            for p in range(2):
                if p == 0:
                    keep_clock(14)
                pe.wait_ge(sm("l3g_p"), p + 1)
                for j in range(HEADS // 2):
                    i = 4 * p + j
                    last = pe.transpose((tp, y[1])[p][:, j * P:(j + 1) * P], scratch[:, i * P:(i + 1) * P], ident[:])
                last.then_inc(sm("l3g_pT"), 1)
            pe.wait_ge(sm("l3g_v"), 1)
            probs_T = side[:].rearrange("p c n -> p (c n)")
            for p in range(2):
                pe.wait_ge(sm("l3g_pTs0" if p == 0 else "l3g_pTs1"), 1)
                for j in range(HEADS // 2):
                    i, hd = 4 * p + j, 2 * j + p
                    last = pe.matmul(pre[0][:, hd * DK:(hd + 1) * DK], probs_T[:, i * P:(i + 1) * P],
                                     XT[:].rearrange("p c n -> p (c n)")[:, hd * DK:(hd + 1) * DK], start=True, stop=True)
            last.then_inc(sm("l3g_av"), 1)
            pe.wait_ge(sm("l3g_a"), 1)
            turn(tp, h[:, 0], sm("l3g_aT"))
            pe.wait_ge(sm("l3g_aThi"), 1)
            product(G_L3G + 3, pre[1][:], hT_hi[:, 0], hT_lo[:, 0], True, True, low=(sm("l3g_aTlo"), 1))
            turn_weights(G_L3F + 1, 0)
            turn_weights(G_L3F + 1, 1)
            keep_clock(37)
            pe.wait_ge(sm("l3g_mid"), 1)
            turn(tp, h[:, 1], sm("l3g_midT"))
            pe.wait_ge(sm("l3g_midTs"), 1)
            pe.wait_ge(sm("l3_small_in"), 64)
            for c in range(KC):
                last = pe.matmul(ms[0:32, 0:P], l3w1[:, c], XT[:, c], start=c == 0, stop=c == KC - 1)
            last.then_inc(sm("l3g_f1"), 1)
            turn_weights(G_L3F + 1, 2)
            pe.wait_ge(sm("l3g_f1s"), 1)
            pe.matmul(y[0][:], fT[:], b2[:], start=True, stop=True).then_inc(sm("l3g_f2"), 1)
            turn_weights(G_L3F + 1, 3)
            turn_x("l3f")
            pipeline(L3F, lambda: logits("l3f", rwT[:, 1], E8), False)

        @block.vector
        def _(dve):
            n = [0]

            def link(ins):
                n[0] += 1
                ins.then_inc(dve_link, 1)
                dve.wait_ge(dve_link, n[0])

            def chunks4(ap):
                return ap[:].rearrange("p (c n) -> p c n", n=P)

            def statistics(tag, src):
                link(dve.bn_stats(st[:], src))
                dve.bn_aggr(mv[:], st[:]).then_inc(sm("var"), 1)

            def centre_scale(tag, dst, src, gamma):
                dve.wait_ge(sm("var"), nth("var", tag))
                return dve.scalar_tensor_tensor(out=dst, in0=src, scalar=mv[:, 0:1], in1=gamma, op0=ALU.subtract,
                                                op1=ALU.mult)

            def times_rstd_plus(dst, src, add):
                return dve.scalar_tensor_tensor(out=dst, in0=src, scalar=rstd[:, 1:2], in1=add, op0=ALU.mult,
                                                op1=ALU.add)

            def layer_norm(tag):
                statistics(tag, X[:])
                normalise_x(tag)

            def normalise_x(tag):
                dve.wait_ge(sm("rstd"), nth("rstd", tag))
                dve.tensor_scalar(XN[:], X[:], mv[:, 0:1], rstd[:, 1:2], ALU.subtract, ALU.mult).then_inc(sm("xn"), 1)

            def low_x(tag):
                dve.wait_ge(sm("xhi"), nth("xhi", tag))
                dve.tensor_tensor(x_lo[:], chunks4(tp), x_hi[:].bitcast(F32), ALU.subtract).then_inc(
                    sm("xlo"), 1)

            def low_turned(ready, bank_ap, hi, dst, done):
                dve.wait_ge(sm(ready), 1)
                dve.tensor_tensor(dst, chunks4(bank_ap), hi.bitcast(F32), ALU.subtract).then_inc(sm(done), 1)

            def split_quarter(g, q):
                wait_rounded(dve, g)
                dve.tensor_tensor(w_lo[:, g, q], raw[:, g, q], w_hi[:, g, q].bitcast(F32),
                                  ALU.subtract).then_inc(w_lo_ready, 1)

            def transpose_block(g, q, it=None):
                if q == 0:
                    dve.wait_ge(landed[g % RAW_SLOTS], at(arrived(g), 64, it))
                    if g > BLOCKED[0]:
                        before = BLOCKED[BLOCKED.index(g) - 1]
                        dve.wait_ge(w_lo_ready, at(4 * (before + 1), 32, it))
                source = raw[:, g % RAW_SLOTS].rearrange("p c n -> p (c n)").rearrange(
                    "p (b i c) -> p c b i", c=KC, i=32)
                dve.transpose(w_blocks[:, q].rearrange("p (b j) -> p b j", j=32), source[:, q]).then_inc(w_blocked, 1)

            def transpose_blocks(g):
                for q in range(4):
                    transpose_block(g, q)

            def split_turned_quarter(g, q, it=None):
                wait_rounded(dve, g, q + 1, it)
                dve.tensor_tensor(w_lo[:, g % SPLIT_SLOTS, q], wt[q % 2][:], w_hi[:, g % SPLIT_SLOTS, q].bitcast(F32),
                                  ALU.subtract).then_inc(w_lo_ready, 1)

            def split_chunk(g, it=None, also=None):
                if g >= CHUNKS:
                    return
                i = g % SPLIT_SLOTS
                if turned(g):
                    for q in range(4):
                        split_turned_quarter(g, q, it)
                        if also is not None and q < 3:
                            transpose_block(also, q + 1, it)
                else:
                    wait_rounded(dve, g, 4, it)
                    dve.tensor_tensor(w_lo[:, i], w_blocks if blocked(g) else raw[:, g % RAW_SLOTS],
                                      w_hi[:, i].bitcast(F32), ALU.subtract).then_inc(w_lo_ready, 4)

            def top(values, E, k, src, dst):
                one, other = values.unsqueeze(1).broadcast_to([P, E, E]), values.unsqueeze(2).broadcast_to([P, E, E])
                above = cmp[:, 0, 0:E * E].rearrange("p (a b) -> p a b", b=E)
                equal = cmp[:, 1, 0:E * E].rearrange("p (a b) -> p a b", b=E)
                link(dve.tensor_tensor(above, one, other, ALU.is_gt))
                link(dve.tensor_tensor(equal, one, other, ALU.is_equal))
                link(dve.tensor_tensor(equal, equal, tri[:, 0:E, 0:E], ALU.mult))
                link(dve.tensor_tensor(above, above, equal, ALU.add))
                link(dve.reduce_sum(row[:, 6, 0:E], above, AX_X))
                return dve.scalar_tensor_tensor(out=dst, in0=row[:, 6, 0:E], scalar=float(k), in1=src,
                                                op0=ALU.is_lt, op1=ALU.mult)

            def logits_in(tag, E, bias=None):
                dve.wait_ge(sm("logits"), nth("logits", tag))
                if bias is None:
                    link(dve.tensor_copy(row[:, 0, 0:E], ms[:, 0:E]))
                else:
                    return dve.tensor_tensor(row[:, 0, 0:E], ms[:, 0:E], rbias[:, bias, 0:E], ALU.add)

            def negative_max(tag, E):
                link(dve.reduce_max(row[:, 7, 2:3], row[:, 0, 0:E], AX_X))
                dve.tensor_scalar(row[:, 7, 0:1], row[:, 7, 2:3], -1.0, None, ALU.mult).then_inc(sm("max"), 1)

            def softmax_top(tag, E, k):
                dve.wait_ge(sm("exp"), nth("exp", tag))
                link(dve.reciprocal(row[:, 7, 3:4], row[:, 7, 1:2]))
                link(dve.tensor_scalar(row[:, 2, 0:E], row[:, 1, 0:E], row[:, 7, 3:4], None, ALU.mult))
                top(row[:, 2, 0:E], E, k, row[:, 2, 0:E], gates[:, 0:E]).then_inc(sm("gates"), 1)

            def copy_gates(tag):
                dve.wait_ge(sm("gT"), nth("gT", tag))
                dve.tensor_copy(gT[:], ms[0:E8, 0:P]).then_inc(sm("gTs"), 1)

            def pipeline(pipe, router, per_gate, seeded, between=None):
                def step(s, it=None):
                    g = pipe.chunk(s)
                    also = g + 4 if blocked(g + 4) else None
                    if s < pipe.n:
                        split_chunk(g + AHEAD, it)
                        g += 1
                    if also is not None:
                        transpose_block(also, 0, it)
                    if s == pipe.route == 2:
                        router()
                    if s < pipe.lead:
                        split_chunk(g + AHEAD, None, also)
                    if s == 3 and seeded:
                        copy_gates(pipe.tag)
                    if 1 <= s <= pipe.n:
                        dve.wait_ge(hT_hi_ready, at(pipe.turned + s, 4, it))
                        dve.tensor_tensor(hT_lo[:, (s - 1) % 2], chunks4(tp), hT_hi[:, (s - 1) % 2].bitcast(F32),
                                          ALU.subtract).then_inc(hT_lo_ready, 1)
                    if s < pipe.lead:
                        dve.wait_ge(sm("gate_ready"), s + 1)
                        dve.wait_ge(chunk_done, pipe.chunk(s) + 2)
                        dve.tensor_tensor(h[:, s % 2], h[:, s % 2], y[s % 2][:], ALU.mult).then_inc(
                            sm("shared_ready"), 1)
                    if s == pipe.route == 1:
                        router()
                    if s % 2 == 0 and s >= 4 and not pipe.lead:
                        add_pair((s - 4) // 2, it)
                    if s >= 2 and g + AHEAD not in (G_L1G + 1, G_L3G + 1):
                        split_chunk(g + AHEAD, it, also)
                    if s % 2 == 0 and s >= 4 and pipe.lead:
                        add_pair((s - 4) // 2, it)
                    if s == 3 and seeded:
                        dve.wait_ge(sm("seed"), nth("seed", pipe.tag))
                        dve.tensor_tensor(X[:], X[:], wt[0][:], ALU.add).then_inc(y_summed, 1)
                    if between is not None and it is None:
                        between(s)

                def add_pair(q, it=None):
                    last = pipe.chunk(2 * q + 3) + (1 if 2 * q + 3 < pipe.n else 0)
                    dve.wait_ge(chunk_done, at(last + 1, 8, it))
                    dve.wait_ge(y_summed, at(pipe.summed + q, 2, it)) if pipe.summed + q > 0 else None
                    col = q // per_gate
                    gate = gates[:, col:col + 1] if it is None else gates[:, bass.ds(col + (2 // per_gate) * it, 1)]
                    dve.scalar_tensor_tensor(out=X[:], in0=y[q % 2][:], scalar=gate, in1=X[:], op0=ALU.mult,
                                             op1=ALU.add).then_inc(y_summed, 1)

                for s in range(4):
                    step(s)
                with dve.Fori(0, pipe.loops()) as it:
                    for s in range(4, 8):
                        step(s, it)
                for s in range(4 + 4 * pipe.loops(), pipe.n + 2):
                    step(s)
                add_pair((pipe.n - 2) // 2)
                dve.wait_ge(y_summed, pipe.summed + pipe.n // 2)

            dve.wait_ge(sm("x_in"), 16)
            layer_norm("l0g")
            dve.wait_ge(sm("edges_in"), 48)
            link(dve.tensor_copy(ends[:, 0:2], ends_i[:]))
            dve.wait_ge(sm("consts"), 1)
            for k in range(EC):
                o = (k % HOTS) * 3 * P
                if k >= HOTS:
                    dve.wait_ge(sm("hot_used"), k - HOTS + 1)
                dve.tensor_scalar(hot[:, o:o + P], iota_t[:], ends[:, 0, k:k + 1], None, ALU.is_equal)
                dve.tensor_scalar(hot[:, o + P:o + 2 * P], iota_t[:], ends[:, 1, k:k + 1], ends[:, 2, k:k + 1],
                                  ALU.is_equal, ALU.mult)
                dve.tensor_scalar(hot[:, o + 2 * P:o + 3 * P], iota_t[:], ends[:, 1, k:k + 1], None,
                                  ALU.is_equal).then_inc(sm("hot_ready"), 1)
                if k == SIM_AT:
                    dve.wait_ge(sm("l0g_sim"), 1)
                    link(dve.tensor_scalar(mat_b[:], ms[:, 0:P], 0.2, None, ALU.mult))
                    link(dve.tensor_tensor(mat_a[:], ms[:, 0:P], mat_b[:], ALU.max))
                    link(dve.reduce_max(row[:, 0, 2:3], mat_a[:], AX_X))
                    dve.tensor_scalar(row[:, 0, 0:1], row[:, 0, 2:3], -1.0, None, ALU.mult).then_inc(sm("max"), 1)
            dve.wait_ge(sm("exp"), nth("exp", "l0g"))
            link(dve.reciprocal(row[:, 0, 3:4], row[:, 0, 1:2]))
            dve.wait_ge(sm("hot_used"), EC)
            link(dve.scalar_tensor_tensor(out=mat_a[:], in0=mat_b[:], scalar=row[:, 0, 3:4], in1=y[0][:, 0:P],
                                          op0=ALU.mult, op1=ALU.mult, accum_out=row[:, 0, 4:5]))
            dve.wait_ge(sm("ab"), 1)
            link(dve.tensor_scalar(row[:, 0, 5:6], row[:, 0, 4:5], 1.0, None, ALU.add))
            link(dve.scalar_tensor_tensor(out=row[:, 0, 6:7], in0=row[:, 0, 5:6], scalar=ab[:, 0:1], in1=ab[:, 1:2],
                                          op0=ALU.mult, op1=ALU.add))
            link(dve.reciprocal(row[:, 0, 7:8], row[:, 0, 6:7]))
            link(dve.tensor_tensor(row[:, 1, 0:2], ab[:], row[:, 0, 7:8].broadcast_to([P, 2]), ALU.mult))
            link(dve.tensor_scalar(mat_b[:], ident[:], row[:, 1, 0:1], None, ALU.mult))
            dve.scalar_tensor_tensor(out=mat_a[:], in0=mat_a[:], scalar=row[:, 1, 0:1], in1=mat_b[:],
                                     op0=ALU.mult, op1=ALU.add).then_inc(sm("l0g_a"), 1)
            dve.wait_ge(sm("l0g_aT"), 1)
            dve.tensor_copy(mat_b[:], ms[:, 0:P]).then_inc(sm("l0g_aTs"), 1)
            link(dve.tensor_scalar(h[:, 1], XN[:], row[:, 1, 1:2], None, ALU.mult))
            for i in range(5):
                for part in range(2):
                    cols = slice(part * 256, part * 256 + 256)
                    dve.wait_ge(sm("l0g_sweep"), 2 * i + part + 1)
                    dst = X[:, cols] if i == 4 else XT[:].rearrange("p c n -> p (c n)")[:, cols]
                    dve.tensor_tensor(dst, pre[part][:, 0:256], h[:, int(i < 4), cols], ALU.add).then_inc(
                        sm("l0g_swept"), 1)
                    if i == 0:
                        dve.tensor_tensor(h[:, 0, cols], X[:, cols], h[:, 1, cols], ALU.add)
            dve.wait_ge(sm("l0g_swept"), 10)
            statistics("l0f", X[:])
            split_quarter(0, 0)
            normalise_x("l0f")
            split_quarter(0, 1)
            split_quarter(0, 2)

            def halve_bias(cols, raw_cols):
                hl = bias_hl[:, cols]
                return dve.scalar_tensor_tensor(out=hl, in0=hl.bitcast(F32), scalar=half[:, 1:2],
                                                in1=scratch[0:16, raw_cols], op0=ALU.mult, op1=ALU.add)

            def graph_matrices(s):
                if s == 1:
                    dve.wait_ge(sm("c_dsT"), 1)
                    link(dve.tensor_copy(c_ds[:], wt[1][:, 0:P]))
                    both = wt[1][:, P:P + 2 * KC * 15].rearrange("p (i c e) -> p i c e", i=2, e=15)
                    link(dve.tensor_copy(rwT[:, 0, :, 0:7], both[:, 0, :, 0:7]))
                    link(dve.tensor_copy(rwT[:, 1], both[:, 1, :, 7:15]))
                    link(dve.reduce_sum(row[:, 3, 0:1], c_ds[:], AX_X))
                    link(dve.tensor_scalar(row[:, 3, 1:2], row[:, 3, 0:1], 1.0, None, ALU.max))
                    link(dve.reciprocal(row[:, 3, 2:3], row[:, 3, 1:2]))
                    dve.tensor_scalar(mat_a[:], c_ds[:], row[:, 3, 2:3], None, ALU.mult).then_inc(sm("agg2_rows"), 1)
                if s == 2:
                    dve.memset(row[:, 5, :], 1.0)
                    link(dve.tensor_scalar(pen[:], c_ds[:], 1.0, None, ALU.min))
                    link(dve.tensor_scalar(pen[:], pen[:], -MASKED, MASKED, ALU.mult, ALU.add))
                    link(dve.tensor_scalar(row[:, 3, 3:4], scal[:, 2:3], 1.0, None, ALU.add))
                    dve.scalar_tensor_tensor(out=agg1[:], in0=ident[:], scalar=row[:, 3, 3:4], in1=c_ds[:],
                                             op0=ALU.mult, op1=ALU.add).then_inc(sm("c_ds"), 1)
                if s == 3:
                    dve.wait_ge(sm("agg2T"), 1)
                    link(dve.tensor_copy(agg2[:], wt[1][:, 0:P]))

            low_x("l0f")
            split_quarter(0, 3)
            dve.wait_ge(sm("bias_hi"), 4)
            link(halve_bias(slice(0, 2 * D), slice(0, 2 * D)))
            halve_bias(slice(BL_COL, BL_COL + D), slice(2 * D, 3 * D)).then_inc(sm("l0_bias"), 1)
            split_chunk(1)
            dve.tensor_copy(c_sd[:], y[0][:, P:2 * P]).then_inc(sm("c_sd"), 1)

            def route_l0():
                logits_in("l0f", E8)
                negative_max("l0f", E8)
                softmax_top("l0f", E8, 2)
            pipeline(L0F, route_l0, 1, True, graph_matrices)
            statistics("l1g", X[:])
            split_turned_quarter(G_L1G + 1, 0)
            split_turned_quarter(G_L1G + 1, 1)
            normalise_x("l1g")
            split_turned_quarter(G_L1G + 1, 2)
            split_turned_quarter(G_L1G + 1, 3)
            low_x("l1g")
            low_turned("l1g_hThi", tp, hT_hi[:, 0], hT_lo[:, 0], "l1g_hTlo")
            dve.wait_ge(sm("affine_l1"), 32)
            link(dve.tensor_tensor(X[:], X[:], affine[:, 1], ALU.add))
            dve.wait_ge(chunk_done, G_L1G + 2)
            statistics("l1g_out", pre[1][:])
            link(centre_scale("l1g_out", XN[:], pre[1][:], affine[:, 0]))
            dve.wait_ge(sm("rstd"), nth("rstd", "l1g_out"))
            link(times_rstd_plus(X[:], XN[:], X[:]))
            layer_norm("l1f")
            split_chunk(G_L1G + 2)
            dve.wait_ge(sm("rbias_in"), 48)
            link(logits_in("l1f", E8, 0))
            top(row[:, 0, 0:E8], E8, 1, row[:, 5, 0:E8], gates[:, 0:E8]).then_inc(sm("gates"), 1)
            dve.wait_ge(sm("gates"), nth("gates", "l1f"))
            dve.wait_ge(sm("l1f_pre"), 1)
            dve.scalar_tensor_tensor(out=h[:, 0, 0:256].rearrange("p (e n) -> p e n", n=H1),
                                     in0=pre[0][:, 0:256].rearrange("p (e n) -> p e n", n=H1), scalar=0.0,
                                     in1=gates[:, 0:E8].unsqueeze(2).broadcast_to([P, E8, H1]), op0=ALU.max,
                                     op1=ALU.mult).then_inc(sm("l1f_h"), 1)
            copy_gates("l1f")
            split_chunk(G_L1G + 3)
            dve.wait_ge(sm("l1f_y"), 1)
            dve.tensor_tensor(X[:], X[:], y[0][:], ALU.add).then_inc(sm("l1f_done"), 1)
            dve.wait_ge(sm("l1f_done"), 1)
            layer_norm("l2g")
            low_x("l2g")
            low_turned("l2g_xagghi", y[0], aggT_hi[:, 0], aggT_lo[:, 0], "l2g_xagglo")
            g = G_L2G
            for s in range(E4 + 2):
                if s < E4:
                    split_chunk(g + AHEAD)
                    split_chunk(g + 1 + AHEAD)
                    if s == 0:
                        link(logits_in("l2g", E4, 1))
                        negative_max("l2g", E4)
                        softmax_top("l2g", E4, 2)
                    dve.wait_ge(sm("bias_hi"), 4 + 2 * (s + 1))
                    halve_bias(slice(s * D, s * D + D), slice(s * D, s * D + D)).then_inc(sm("l2_bias"), 1)
                    g += 2
                if 1 <= s <= E4:
                    dve.wait_ge(sm("l2g_h_hi"), s)
                    dve.tensor_tensor(hT_lo[:, (s - 1) % 2], chunks4(tp), hT_hi[:, (s - 1) % 2].bitcast(F32),
                                      ALU.subtract).then_inc(sm("l2g_h_lo"), 1)
                if s >= 2:
                    split_chunk(g + AHEAD)
                    if s < E4 + 1:
                        split_chunk(g + 1 + AHEAD)
                    dve.wait_ge(sm("l2g_out"), s - 1)
                    if s >= 3:
                        dve.wait_ge(sm("l2g_summed"), s - 2)
                    dve.tensor_tensor(X[:], X[:], weighted[:, (s % 2) * D:(s % 2 + 1) * D], ALU.add).then_inc(
                        sm("l2g_summed"), 1)
                    g += 2
                if 1 <= s <= E4:
                    dve.wait_ge(sm("l2g_agg_hi"), s)
                    dve.tensor_tensor(aggT_lo[:, 1], chunks4(wt[0]), aggT_hi[:, 1].bitcast(F32),
                                      ALU.subtract).then_inc(sm("l2g_agg_lo"), 1)
            dve.wait_ge(sm("l2g_summed"), E4)
            layer_norm("l2f")
            split_chunk(G_L2F + 1)
            low_x("l2f")

            def route_tree():
                logits_in("l2f", 7, 2).then_inc(sm("l2f_tree"), 1)
                dve.wait_ge(sm("l2f_p"), 1)
                p, q = row[:, 1, 0:7], row[:, 2, 0:7]
                link(dve.tensor_scalar(q, p, -1.0, 1.0, ALU.mult, ALU.add))
                link(dve.tensor_copy(row[:, 3, 0:1], q[:, 0:1]))
                link(dve.tensor_copy(row[:, 3, 1:2], p[:, 0:1]))
                for width, (a, b) in ((2, (3, 4)), (4, (4, None))):
                    leaf = row[:, a, 0:width]
                    nxt = gates[:, 0:2 * width] if b is None else row[:, b, 0:2 * width]
                    nxt = nxt.rearrange("p (n b) -> p n b", b=2)
                    link(dve.tensor_tensor(nxt[:, :, 0], leaf, q[:, width - 1:2 * width - 1], ALU.mult))
                    last = dve.tensor_tensor(nxt[:, :, 1], leaf, p[:, width - 1:2 * width - 1], ALU.mult)
                    if b is None:
                        last.then_inc(sm("gates"), 1)
                    else:
                        link(last)
            pipeline(L2F, route_tree, 2, True)
            layer_norm("l3g")
            split_chunk(G_L3G + 1)
            low_x("l3g")
            split_chunk(G_L3G + 2)
            split_chunk(G_L3G + 3)
            dve.wait_ge(chunk_done, G_L3G + 2)
            dve.tensor_copy(h[:, 1], pre[1][:]).then_inc(sm("l3g_k"), 1)
            dve.wait_ge(sm("l3g_kT"), 1)
            dve.tensor_copy(scratch[:, 3 * D:4 * D], y[1][:]).then_inc(sm("l3g_kTs"), 1)
            dve.wait_ge(sm("l3g_scores"), 1)
            S = scratch[:, 0:2 * D].rearrange("p (i n) -> p i n", n=P)
            for p in range(2):
                hs = slice(4 * p, 4 * p + 4)
                link(dve.scalar_tensor_tensor(out=S[:, hs], in0=chunks4(pre[p]), scalar=DK ** -0.5,
                                              in1=pen[:].unsqueeze(1).broadcast_to([P, 4, P]), op0=ALU.mult,
                                              op1=ALU.add))
                link(dve.reduce_max(row[:, 0, hs], S[:, hs], AX_X))
                dve.tensor_tensor(S[:, hs], S[:, hs], row[:, 0, hs].unsqueeze(2).broadcast_to([P, 4, P]),
                                  ALU.subtract).then_inc(sm("l3g_centred"), 1)
            for p in range(2):
                hs = slice(4 * p, 4 * p + 4)
                dve.wait_ge(sm("l3g_exp"), p + 1)
                dve.tensor_tensor(S[:, hs], S[:, hs], c_ds[:].unsqueeze(1).broadcast_to([P, 4, P]), ALU.mult).then_inc(
                    sm("l3g_p"), 1)
            dve.wait_ge(sm("l3g_pT"), 2)
            dve.tensor_copy(side[:, 2:4].rearrange("p c n -> p (c n)"), y[1][:]).then_inc(sm("l3g_pTs1"), 1)
            link(dve.reduce_sum(row[:, 1, :], S, AX_X))
            link(dve.tensor_scalar(row[:, 2, :], row[:, 1, :], 1e-30, None, ALU.max))
            link(dve.reciprocal(row[:, 3, :], row[:, 2, :]))
            dve.wait_ge(sm("l3g_av"), 1)
            dve.tensor_tensor(h[:, 0].rearrange("t (j p d) -> t p j d", p=2, d=DK),
                              pre[0][:].rearrange("t (j p d) -> t p j d", p=2, d=DK),
                              row[:, 3, :].rearrange("t (p j) -> t p j", p=2).unsqueeze(3).broadcast_to(
                                  [P, 2, 4, DK]), ALU.mult).then_inc(sm("l3g_a"), 1)
            low_turned("l3g_aThi", tp, hT_hi[:, 0], hT_lo[:, 0], "l3g_aTlo")
            transpose_blocks(G_L3F)
            split_chunk(G_L3F)
            dve.wait_ge(chunk_done, G_L3G + 4)
            link(dve.tensor_tensor(h[:, 1], XN[:], pre[1][:], ALU.add))
            statistics("l3g_mid", h[:, 1])
            dve.wait_ge(sm("affine_l3"), 64)
            link(centre_scale("l3g_mid", h[:, 1], h[:, 1], affine[:, 0]))
            dve.wait_ge(sm("rstd"), nth("rstd", "l3g_mid"))
            times_rstd_plus(h[:, 1], h[:, 1], affine[:, 1]).then_inc(sm("l3g_mid"), 1)
            split_turned_quarter(G_L3F + 1, 0)
            split_turned_quarter(G_L3F + 1, 1)
            link(dve.tensor_tensor(X[:], X[:], affine[:, 3], ALU.add))
            split_turned_quarter(G_L3F + 1, 2)
            dve.wait_ge(sm("l3g_mid"), 1)
            dve.wait_ge(sm("l3g_f2"), 1)
            link(dve.tensor_tensor(h[:, 1], h[:, 1], y[0][:], ALU.add))
            statistics("l3g_out", h[:, 1])
            link(centre_scale("l3g_out", h[:, 1], h[:, 1], affine[:, 2]))
            dve.wait_ge(sm("rstd"), nth("rstd", "l3g_out"))
            link(times_rstd_plus(X[:], h[:, 1], X[:]))
            layer_norm("l3f")
            split_turned_quarter(G_L3F + 1, 3)
            transpose_block(G_L3F + 2, 0)
            low_x("l3f")
            for q in range(1, 4):
                transpose_block(G_L3F + 2, q)

            def route_l3():
                logits_in("l3f", E8)
                negative_max("l3f", E8)
                dve.wait_ge(sm("exp"), nth("exp", "l3f"))
                link(top(row[:, 0, 0:E8], E8, 2, row[:, 1, 0:E8], row[:, 2, 0:E8]))
                link(dve.reduce_sum(row[:, 7, 3:4], row[:, 2, 0:E8], AX_X))
                link(dve.reciprocal(row[:, 7, 4:5], row[:, 7, 3:4]))
                link(dve.memset(gates[:, 0:1], 1.0))
                link(dve.tensor_scalar(gates[:, 1:1 + E8], row[:, 2, 0:E8], row[:, 7, 4:5], None, ALU.mult))
            pipeline(L3F, route_l3, 1, False)


_INS = ["x", "src", "dst", "edge_weight", "L0_gnn_emb_1", "L0_gnn_emb_2", "L0_gnn_alpha_p", "L0_gnn_beta_p",
        "L0_ffn_Wg", "L0_ffn_W1", "L0_ffn_b1", "L0_ffn_W2", "L0_ffn_b2", "L1_gnn_eps", "L1_gnn_W1", "L1_gnn_b1",
        "L1_gnn_W2", "L1_gnn_b2", "L1_gnn_gamma", "L1_gnn_beta", "L1_ffn_Wr", "L1_ffn_br", "L1_ffn_W1", "L1_ffn_b1",
        "L1_ffn_W2", "L1_ffn_b2", "L2_gnn_gate_W", "L2_gnn_gate_b", "L2_gnn_Wl", "L2_gnn_bl", "L2_gnn_Wr",
        "L2_ffn_rw", "L2_ffn_rb", "L2_ffn_w1", "L2_ffn_b1", "L2_ffn_w2", "L2_ffn_b2", "L3_gnn_Wq", "L3_gnn_Wk",
        "L3_gnn_Wv", "L3_gnn_Wo", "L3_gnn_ln1_g", "L3_gnn_ln1_b", "L3_gnn_ln2_g", "L3_gnn_ln2_b", "L3_gnn_W1",
        "L3_gnn_b1", "L3_gnn_W2", "L3_gnn_b2", "L3_ffn_gate_w", "L3_ffn_w1", "L3_ffn_w2", "L3_ffn_sg_gate",
        "L3_ffn_sg_up", "L3_ffn_sg_down"]


def kernel(**inputs):
    import numpy as np
    import concourse.bacc as bacc
    from concourse.bass_utils import run_bass_kernel_spmd

    nc = bacc.Bacc("TRN2", target_bir_lowering=False, num_devices=1)
    arrays, handles = {}, {}
    for name in _INS:
        a = np.ascontiguousarray(inputs[name])
        arrays["in_" + name] = a
        handles[name] = nc.dram_tensor("in_" + name, a.shape, mybir.dt.from_np(a.dtype), kind="ExternalInput").ap()
    out = nc.dram_tensor("out_x", (P, D), F32, kind="ExternalOutput").ap()
    gnn_ffn_kernel(nc, handles, out)
    result = run_bass_kernel_spmd(nc, [arrays], core_ids=[0])
    return result.results[0]["out_x"]
```
